# Optimizing a Trainium2 kernel written in Bass

```python
import numpy as np
import jax
import jax.numpy as jnp

def _softmax(x, axis=-1):
    return jax.nn.softmax(x, axis=axis)

def _gelu(x):
    return jax.nn.gelu(x, approximate=True)

def _silu(x):
    return jax.nn.silu(x)

def _sigmoid(x):
    return jax.nn.sigmoid(x)

def _layernorm(x, axis=-1, eps=1e-05):
    m = jnp.mean(x, axis=axis, keepdims=True)
    v = jnp.var(x, axis=axis, keepdims=True)
    return (x - m) / jnp.sqrt(v + eps)

def _scatter_add(tgt, idx, src, axis=0):
    return tgt.at[idx].add(src)

def _segment_sum(src, seg, n):
    return jax.ops.segment_sum(src, seg, n)
kernel_name = 'mk_lm_tower_d2_tok_ids512_r4_11baf3'

def setup_inputs(seed: int=0):
    np.random.seed(seed)
    _w = jnp.asarray

    def _rec_inputs():
        import jax
        import jax.numpy as jnp
        _rk = jax.random.key(seed)
        x = jax.random.randint(jax.random.fold_in(_rk, 1), (8, 256), 0, 12564, jnp.int32)
        return x
    x = _rec_inputs()

    def _L0_tok_setup():
        import jax, jax.numpy as jnp
        import numpy as np
        NUM_EMBEDDINGS = 50257
        EMBED_SIZE = 128
        key = jax.random.key(seed)
        k1, k2 = jax.random.split(key)
        x = jax.random.randint(k1, (8, 512), 0, NUM_EMBEDDINGS)
        embed_matrix = jax.random.normal(k2, (NUM_EMBEDDINGS, EMBED_SIZE), dtype=jnp.float32)
        return {'x': x, 'embed_matrix': embed_matrix}
    _L0_tok_all = _L0_tok_setup()
    _L0_tok_in = {k: v for k, v in _L0_tok_all.items() if k in ('embed_matrix',)}
    del _L0_tok_all

    def _L0_attn_setup():
        import jax, jax.numpy as jnp
        import numpy as np
        N_HEADS = 8
        key = jax.random.key(seed)
        ks = jax.random.split(key, 5)
        b, s, d = (2, 1024, 128)
        return {'x': jax.random.normal(ks[0], (b, s, d), dtype=jnp.float32), 'qkv_w': jax.random.normal(ks[1], (3 * d, d), dtype=jnp.float32) * 0.02, 'qkv_b': jax.random.normal(ks[2], (3 * d,), dtype=jnp.float32) * 0.02, 'out_w': jax.random.normal(ks[3], (d, d), dtype=jnp.float32) * 0.02, 'out_b': jax.random.normal(ks[4], (d,), dtype=jnp.float32) * 0.02}
    _L0_attn_all = _L0_attn_setup()
    _L0_attn_in = {k: v for k, v in _L0_attn_all.items() if k in ('qkv_w', 'qkv_b', 'out_w', 'out_b')}
    del _L0_attn_all

    def _L0_ffn_setup():
        import jax, jax.numpy as jnp
        import numpy as np
        import math
        E, K, CAPF = (8, 2, 1.25)
        D, DFF = (128, 512)

        def _moe(x, Wr, br, W1, b1, W2, b2):
            orig = x.shape
            d = orig[-1]
            xf = x.reshape(-1, d)
            N = xf.shape[0]
            logits = xf @ Wr + br
            probs = jax.nn.softmax(logits, axis=-1)
            topk_p, topk_i = jax.lax.top_k(probs, K)
            topk_w = topk_p / (jnp.sum(topk_p, axis=-1, keepdims=True) + 1e-09)
            cap = max(1, int(math.ceil(CAPF * float(N * K) / float(E))))
            flat_e = topk_i.reshape(-1)
            flat_w = topk_w.reshape(-1)
            tok = jnp.repeat(jnp.arange(N), K)
            one_hot = jax.nn.one_hot(flat_e, E, dtype=xf.dtype)
            pos = (jnp.cumsum(one_hot, axis=0) - one_hot)[jnp.arange(N * K), flat_e]
            pos = pos.astype(jnp.int32)
            keep = pos < cap
            w_k = jnp.where(keep, flat_w, 0.0)
            sum_w = jnp.zeros((N,), xf.dtype).at[tok].add(w_k)
            w_norm = w_k / (sum_w[tok] + 1e-09)
            slot = flat_e * cap + pos
            slot_safe = jnp.where(keep, slot, E * cap)
            expert_in = jnp.zeros((E * cap, d), xf.dtype).at[slot_safe].set(xf[tok], mode='drop').reshape(E, cap, d)
            h = jax.nn.gelu(jnp.einsum('ecd,edf->ecf', expert_in, W1) + b1[:, None, :], approximate=False)
            expert_out = (jnp.einsum('ecf,efd->ecd', h, W2) + b2[:, None, :]).reshape(E * cap, d)
            contrib = expert_out[jnp.where(keep, slot, 0)]
            y = jnp.zeros((N, d), xf.dtype).at[tok].add(contrib * w_norm[:, None])
            return y.reshape(orig)
        key = jax.random.key(seed)
        ks = jax.random.split(key, 5)
        s = lambda k, sh, sc: jax.random.normal(k, sh, jnp.float32) * sc
        return {'x': jax.random.normal(ks[0], (8, 1024, D), jnp.float32), 'Wr': s(ks[1], (D, E), 1.0 / math.sqrt(D)), 'br': jnp.zeros((E,), jnp.float32), 'W1': s(ks[2], (E, D, DFF), 1.0 / math.sqrt(D)), 'b1': jnp.zeros((E, DFF), jnp.float32), 'W2': s(ks[3], (E, DFF, D), 1.0 / math.sqrt(DFF)), 'b2': jnp.zeros((E, D), jnp.float32)}
    _L0_ffn_all = _L0_ffn_setup()
    _L0_ffn_in = {k: v for k, v in _L0_ffn_all.items() if k in ('Wr', 'br', 'W1', 'b1', 'W2', 'b2')}
    del _L0_ffn_all

    def _L1_attn_setup():
        import jax, jax.numpy as jnp
        import numpy as np
        EPS = 1e-05

        def _ln(x, w, b, axes):
            mu = jnp.mean(x, axis=axes, keepdims=True)
            var = jnp.mean((x - mu) ** 2, axis=axes, keepdims=True)
            return (x - mu) / jnp.sqrt(var + EPS) * w + b
        key = jax.random.key(seed)
        ks = jax.random.split(key, 6)
        B, L, D, A, H, F = (1, 256, 128, 32, 8, 512)
        s = 0.02
        return {'x': jax.random.normal(ks[0], (B, L, D), jnp.float32), 'ln0_w': jnp.ones((D,), jnp.float32), 'ln0_b': jnp.zeros((D,), jnp.float32), 'ln1_w': jnp.ones((D, H), jnp.float32), 'ln1_b': jnp.zeros((D, H), jnp.float32), 'qw': jax.random.normal(ks[1], (D, A * H), jnp.float32) * s, 'qb': jnp.zeros((A * H,), jnp.float32), 'kw': jax.random.normal(ks[2], (D, A * H), jnp.float32) * s, 'kb': jnp.zeros((A * H,), jnp.float32), 'vw': jax.random.normal(ks[3], (D, D * H), jnp.float32) * s, 'vb': jnp.zeros((D * H,), jnp.float32), 'w1': jax.random.normal(ks[4], (D * H, F), jnp.float32) * s, 'b1': jnp.zeros((F,), jnp.float32), 'w2': jax.random.normal(ks[5], (F, D), jnp.float32) * s, 'b2': jnp.zeros((D,), jnp.float32)}
    _L1_attn_all = _L1_attn_setup()
    _L1_attn_in = {k: v for k, v in _L1_attn_all.items() if k in ('ln0_w', 'ln0_b', 'ln1_w', 'ln1_b', 'qw', 'qb', 'kw', 'kb', 'vw', 'vb', 'w1', 'b1', 'w2', 'b2')}
    del _L1_attn_all

    def _L1_ffn_setup():
        import jax, jax.numpy as jnp
        import numpy as np
        B, S, D, H, E, K = (2, 512, 128, 256, 8, 2)

        def _moe(x, router_w, w_gate, w_up, w_down):
            bsz, seq, d = x.shape
            flat = x.reshape(-1, d)
            logits = flat @ router_w.T
            topk_vals, topk_idx = jax.lax.top_k(logits, K)
            topk_w = jax.nn.softmax(topk_vals, axis=-1)
            s = flat.shape[0]
            dense_w = jnp.zeros((s, E), dtype=flat.dtype).at[jnp.arange(s)[:, None], topk_idx].add(topk_w)
            g = jnp.einsum('sd,edh->esh', flat, w_gate)
            u = jnp.einsum('sd,edh->esh', flat, w_up)
            y = jnp.einsum('esh,ehd->esd', jax.nn.silu(g) * u, w_down)
            out = jnp.einsum('esd,se->sd', y, dense_w)
            return out.reshape(bsz, seq, d)
        key = jax.random.key(seed)
        k1, k2, k3, k4, k5 = jax.random.split(key, 5)
        return {'x': jax.random.normal(k1, (B, S, D), dtype=jnp.float32), 'router_w': jax.random.normal(k2, (E, D), dtype=jnp.float32) * D ** (-0.5), 'w_gate': jax.random.normal(k3, (E, D, H), dtype=jnp.float32) * D ** (-0.5), 'w_up': jax.random.normal(k4, (E, D, H), dtype=jnp.float32) * D ** (-0.5), 'w_down': jax.random.normal(k5, (E, H, D), dtype=jnp.float32) * H ** (-0.5)}
    _L1_ffn_all = _L1_ffn_setup()
    _L1_ffn_in = {k: v for k, v in _L1_ffn_all.items() if k in ('router_w', 'w_gate', 'w_up', 'w_down')}
    del _L1_ffn_all
    return {'x': x, 'L0_tok_embed_matrix': _L0_tok_in['embed_matrix'], 'L0_attn_qkv_w': _L0_attn_in['qkv_w'], 'L0_attn_qkv_b': _L0_attn_in['qkv_b'], 'L0_attn_out_w': _L0_attn_in['out_w'], 'L0_attn_out_b': _L0_attn_in['out_b'], 'L0_ffn_Wr': _L0_ffn_in['Wr'], 'L0_ffn_br': _L0_ffn_in['br'], 'L0_ffn_W1': _L0_ffn_in['W1'], 'L0_ffn_b1': _L0_ffn_in['b1'], 'L0_ffn_W2': _L0_ffn_in['W2'], 'L0_ffn_b2': _L0_ffn_in['b2'], 'L1_attn_ln0_w': _L1_attn_in['ln0_w'], 'L1_attn_ln0_b': _L1_attn_in['ln0_b'], 'L1_attn_ln1_w': _L1_attn_in['ln1_w'], 'L1_attn_ln1_b': _L1_attn_in['ln1_b'], 'L1_attn_qw': _L1_attn_in['qw'], 'L1_attn_qb': _L1_attn_in['qb'], 'L1_attn_kw': _L1_attn_in['kw'], 'L1_attn_kb': _L1_attn_in['kb'], 'L1_attn_vw': _L1_attn_in['vw'], 'L1_attn_vb': _L1_attn_in['vb'], 'L1_attn_w1': _L1_attn_in['w1'], 'L1_attn_b1': _L1_attn_in['b1'], 'L1_attn_w2': _L1_attn_in['w2'], 'L1_attn_b2': _L1_attn_in['b2'], 'L1_ffn_router_w': _L1_ffn_in['router_w'], 'L1_ffn_w_gate': _L1_ffn_in['w_gate'], 'L1_ffn_w_up': _L1_ffn_in['w_up'], 'L1_ffn_w_down': _L1_ffn_in['w_down']}

def reference(x, L0_tok_embed_matrix, L0_attn_qkv_w, L0_attn_qkv_b, L0_attn_out_w, L0_attn_out_b, L0_ffn_Wr, L0_ffn_br, L0_ffn_W1, L0_ffn_b1, L0_ffn_W2, L0_ffn_b2, L1_attn_ln0_w, L1_attn_ln0_b, L1_attn_ln1_w, L1_attn_ln1_b, L1_attn_qw, L1_attn_qb, L1_attn_kw, L1_attn_kb, L1_attn_vw, L1_attn_vb, L1_attn_w1, L1_attn_b1, L1_attn_w2, L1_attn_b2, L1_ffn_router_w, L1_ffn_w_gate, L1_ffn_w_up, L1_ffn_w_down):
    import jax
    import jax.numpy as jnp

    def _L0_tok_ref(x, embed_matrix):
        import jax, jax.numpy as jnp
        import numpy as np
        NUM_EMBEDDINGS = 50257
        EMBED_SIZE = 128
        return jnp.take(embed_matrix, x, axis=0)

    def _L0_attn_ref(x, qkv_w, qkv_b, out_w, out_b):
        import jax, jax.numpy as jnp
        import numpy as np
        N_HEADS = 8
        b, s, d = x.shape
        h = N_HEADS
        c = d // h
        factor = 1.0 / jnp.sqrt(jnp.asarray(c, dtype=x.dtype))
        qkv = x @ qkv_w.T + qkv_b
        qkv = qkv.reshape(b, s, h, 3, c)
        q, k, v = (qkv[..., 0, :], qkv[..., 1, :], qkv[..., 2, :])
        scores = jnp.einsum('bshc,bthc->bhst', q, k) * factor
        attn = jax.nn.softmax(scores, axis=-1)
        ctx = jnp.einsum('bhst,bthc->bshc', attn, v).reshape(b, s, d)
        return ctx @ out_w.T + out_b

    def _L0_ffn_ref(x, Wr, br, W1, b1, W2, b2):
        import jax, jax.numpy as jnp
        import numpy as np
        import math
        E, K, CAPF = (8, 2, 1.25)
        D, DFF = (128, 512)

        def _moe(x, Wr, br, W1, b1, W2, b2):
            orig = x.shape
            d = orig[-1]
            xf = x.reshape(-1, d)
            N = xf.shape[0]
            logits = xf @ Wr + br
            probs = jax.nn.softmax(logits, axis=-1)
            topk_p, topk_i = jax.lax.top_k(probs, K)
            topk_w = topk_p / (jnp.sum(topk_p, axis=-1, keepdims=True) + 1e-09)
            cap = max(1, int(math.ceil(CAPF * float(N * K) / float(E))))
            flat_e = topk_i.reshape(-1)
            flat_w = topk_w.reshape(-1)
            tok = jnp.repeat(jnp.arange(N), K)
            one_hot = jax.nn.one_hot(flat_e, E, dtype=xf.dtype)
            pos = (jnp.cumsum(one_hot, axis=0) - one_hot)[jnp.arange(N * K), flat_e]
            pos = pos.astype(jnp.int32)
            keep = pos < cap
            w_k = jnp.where(keep, flat_w, 0.0)
            sum_w = jnp.zeros((N,), xf.dtype).at[tok].add(w_k)
            w_norm = w_k / (sum_w[tok] + 1e-09)
            slot = flat_e * cap + pos
            slot_safe = jnp.where(keep, slot, E * cap)
            expert_in = jnp.zeros((E * cap, d), xf.dtype).at[slot_safe].set(xf[tok], mode='drop').reshape(E, cap, d)
            h = jax.nn.gelu(jnp.einsum('ecd,edf->ecf', expert_in, W1) + b1[:, None, :], approximate=False)
            expert_out = (jnp.einsum('ecf,efd->ecd', h, W2) + b2[:, None, :]).reshape(E * cap, d)
            contrib = expert_out[jnp.where(keep, slot, 0)]
            y = jnp.zeros((N, d), xf.dtype).at[tok].add(contrib * w_norm[:, None])
            return y.reshape(orig)
        return _moe(x, Wr, br, W1, b1, W2, b2)

    def _L1_attn_ref(x, ln0_w, ln0_b, ln1_w, ln1_b, qw, qb, kw, kb, vw, vb, w1, b1, w2, b2):
        import jax, jax.numpy as jnp
        import numpy as np
        EPS = 1e-05

        def _ln(x, w, b, axes):
            mu = jnp.mean(x, axis=axes, keepdims=True)
            var = jnp.mean((x - mu) ** 2, axis=axes, keepdims=True)
            return (x - mu) / jnp.sqrt(var + EPS) * w + b
        B, L, D = x.shape
        H = ln1_w.shape[-1]
        _x = _ln(x, ln0_w, ln0_b, -1)
        q = jnp.exp(jnp.clip(_x @ qw + qb, -10.0, 10.0)).reshape(B, L, -1, H)
        k = jnp.exp(jnp.clip(_x @ kw + kb, -10.0, 10.0)).reshape(B, L, -1, H)
        v = (x @ vw + vb).reshape(B, L, D, H)
        kv = jnp.cumsum(jnp.einsum('blah,bldh->bladh', k, v), axis=1)
        qkv = jnp.einsum('blah,bladh->bldh', q, kv)
        den = jnp.einsum('blah,blah->blh', q, jnp.cumsum(k, axis=1))[..., None, :]
        y = x[..., None] + _ln(qkv / den, ln1_w, ln1_b, (-2, -1))
        y = y.reshape(B, L, D * H)
        h1 = jax.nn.relu(y @ w1 + b1)
        return jax.nn.relu(h1 @ w2 + b2) + x

    def _L1_ffn_ref(x, router_w, w_gate, w_up, w_down):
        import jax, jax.numpy as jnp
        import numpy as np
        B, S, D, H, E, K = (2, 512, 128, 256, 8, 2)

        def _moe(x, router_w, w_gate, w_up, w_down):
            bsz, seq, d = x.shape
            flat = x.reshape(-1, d)
            logits = flat @ router_w.T
            topk_vals, topk_idx = jax.lax.top_k(logits, K)
            topk_w = jax.nn.softmax(topk_vals, axis=-1)
            s = flat.shape[0]
            dense_w = jnp.zeros((s, E), dtype=flat.dtype).at[jnp.arange(s)[:, None], topk_idx].add(topk_w)
            g = jnp.einsum('sd,edh->esh', flat, w_gate)
            u = jnp.einsum('sd,edh->esh', flat, w_up)
            y = jnp.einsum('esh,ehd->esd', jax.nn.silu(g) * u, w_down)
            out = jnp.einsum('esd,se->sd', y, dense_w)
            return out.reshape(bsz, seq, d)
        return _moe(x, router_w, w_gate, w_up, w_down)
    h = _L0_tok_ref(x, L0_tok_embed_matrix)
    h = h + _L0_attn_ref(_layernorm(h, axis=-1), L0_attn_qkv_w, L0_attn_qkv_b, L0_attn_out_w, L0_attn_out_b)
    h = h + _L0_ffn_ref(_layernorm(h, axis=-1), L0_ffn_Wr, L0_ffn_br, L0_ffn_W1, L0_ffn_b1, L0_ffn_W2, L0_ffn_b2)
    h = h + _L1_attn_ref(_layernorm(h, axis=-1), L1_attn_ln0_w, L1_attn_ln0_b, L1_attn_ln1_w, L1_attn_ln1_b, L1_attn_qw, L1_attn_qb, L1_attn_kw, L1_attn_kb, L1_attn_vw, L1_attn_vb, L1_attn_w1, L1_attn_b1, L1_attn_w2, L1_attn_b2)
    h = h + _L1_ffn_ref(_layernorm(h, axis=-1), L1_ffn_router_w, L1_ffn_w_gate, L1_ffn_w_up, L1_ffn_w_down)
    return h

_drawn_inputs = setup_inputs


def setup_inputs(seed=0):
    import zlib

    import numpy as np

    out = dict(_drawn_inputs(seed))
    spreads = {'L0_ffn_br': (0.0, 0.1),
     'L0_ffn_b1': (0.0, 0.1),
     'L0_ffn_b2': (0.0, 0.1),
     'L1_attn_ln0_w': (1.0, 0.6),
     'L1_attn_ln0_b': (0.0, 0.8),
     'L1_attn_ln1_w': (1.0, 0.6),
     'L1_attn_ln1_b': (0.0, 0.518),
     'L1_attn_qb': (0.0, 0.8),
     'L1_attn_kb': (0.0, 0.8),
     'L1_attn_vb': (0.0, 0.1),
     'L1_attn_b1': (0.0, 0.403),
     'L1_attn_b2': (0.0, 0.1)}
    factors = {'L0_attn_qkv_w': 2.744, 'L1_attn_qw': 8.0, 'L1_attn_kw': 8.0}
    for name, (base, spread) in spreads.items():
        noise = np.random.default_rng([zlib.crc32(name.encode()), seed]).standard_normal(out[name].shape)
        drawn = base * np.exp(spread * noise) if base else spread * noise
        out[name] = jnp.asarray(drawn.astype(out[name].dtype))
    for name, factor in factors.items():
        out[name] = (out[name] * factor).astype(out[name].dtype)
    return out
```

```python
from contextlib import ExitStack

import numpy as np

import concourse.bass as bass
from concourse import mybir

F32 = mybir.dt.float32
F32R = mybir.dt.float32r
BF16 = mybir.dt.bfloat16
I32 = mybir.dt.int32
U32 = mybir.dt.uint32
ALU = mybir.AluOpType
ACT = mybir.ActivationFunctionType
AX = mybir.AxisListType.X

P = 128
B, L, D = 8, 256, 128
N = B * L
ST = L // P
NT = N // P
VOCAB = 50257
H0, C0 = 8, 16
G0 = 4
E, K = 8, 2
F0 = 512
CAP = 640
FT = F0 // P
CT = CAP // P
H1, A1 = 8, 32
G1 = 2
F1 = 512
HE = 256
HT = HE // P
REG = N
TILES2 = N * K // P + E
SPARE = TILES2 * P - 2 * REG
XW = D + 2
EPS = 1e-5
BIG = 1.0e6


class Steps:

    def __init__(self, sem, names, ahead=2):
        self.sem, self.names, self.ahead, self.next = sem, list(names), ahead, 0

    def step(self, name):
        assert self.names[self.next] == name, (self.names[self.next], name)
        self.next = (self.next + 1) % len(self.names)
        return self.sem, 1

    def at(self, rnd, name):
        return self.sem, len(self.names) * (rnd + self.ahead) + self.names.index(name) + 1

    def start(self, eng):
        eng.sem_inc(self.sem, len(self.names) * self.ahead)


def held(eng, sem, rnd):
    if not isinstance(rnd, int):
        eng.sem_inc(sem, 1)


def skewed(eng, stages, rounds):
    most = max(lag for _, lag in stages)
    first = most + most % 2
    turns = (rounds - first) // 2

    def time(t, j=None):
        for stage, lag in stages:
            p = (t - lag) % 2
            if j is None:
                if 0 <= t - lag < rounds:
                    stage(t - lag, p, (t - lag) // 2)
            else:
                stage(j * 2 + (t - lag), p, j + (t - lag) // 2)

    for t in range(first):
        time(t)
    with eng.Fori(0, turns) as j:
        time(first, j)
        time(first + 1, j)
    for t in range(first + 2 * turns, rounds + most):
        time(t)


def layouts(i):
    def c(x):
        return np.ascontiguousarray(x)

    return {
        "ids": c(i["x"].reshape(NT, P).T),
        "embed": c(i["L0_tok_embed_matrix"]),
        "wqkv": c(i["L0_attn_qkv_w"].reshape(H0, 3, C0, D).transpose(3, 1, 0, 2).reshape(D, 3 * D)),
        "bqkv": c(i["L0_attn_qkv_b"].reshape(H0, 3, C0).transpose(1, 0, 2).reshape(1, 3 * D)),
        "bv": c(i["L0_attn_qkv_b"].reshape(H0, 3, C0)[:, 2].reshape(D)),
        "wo": c(i["L0_attn_out_w"].T),
        "bo": c(i["L0_attn_out_b"]),
        "wr1": c(i["L0_ffn_Wr"]),
        "br": c(i["L0_ffn_br"]),
        "w1e": c(i["L0_ffn_W1"]),
        "b1e": c(i["L0_ffn_b1"].reshape(E, FT, P).transpose(0, 2, 1)),
        "w2e": c(i["L0_ffn_W2"].reshape(E, FT, P, D).transpose(0, 2, 1, 3)),
        "b2e": c(i["L0_ffn_b2"]),
        "ln0_w": c(i["L1_attn_ln0_w"].reshape(D, 1)),
        "ln0_b": c(i["L1_attn_ln0_b"].reshape(D, 1)),
        "ln1_w": c(i["L1_attn_ln1_w"]),
        "ln1_b": c(i["L1_attn_ln1_b"]),
        "qw": c(i["L1_attn_qw"].reshape(D, A1, H1).transpose(0, 2, 1).reshape(D, A1 * H1)),
        "kw": c(i["L1_attn_kw"].reshape(D, A1, H1).transpose(0, 2, 1).reshape(D, A1 * H1)),
        "qb": c(i["L1_attn_qb"].reshape(A1, H1).T.reshape(G1, P).T),
        "kb": c(i["L1_attn_kb"].reshape(A1, H1).T.reshape(G1, P).T),
        "vw": c(i["L1_attn_vw"].reshape(D, D, H1).transpose(0, 2, 1).reshape(D, H1 * D)),
        "vb": c(i["L1_attn_vb"].reshape(D, H1).T.reshape(H1 * D)),
        "w1": c(i["L1_attn_w1"].reshape(D, H1, F1)),
        "b1": c(i["L1_attn_b1"].reshape(F1 // P, P).T),
        "w2": c(i["L1_attn_w2"].reshape(F1 // P, P, D).transpose(1, 0, 2)),
        "b2": c(i["L1_attn_b2"]),
        "wr2": c(i["L1_ffn_router_w"].T),
        "wgu": c(np.concatenate([i["L1_ffn_w_gate"], i["L1_ffn_w_up"]], axis=2).transpose(1, 0, 2)),
        "wd": c(i["L1_ffn_w_down"].reshape(E, HT, P, D).transpose(2, 0, 1, 3)),
    }


def lm_tower(nc, a, out):
    with ExitStack() as ctx:
        def sb(name, shape, dt=F32):
            return ctx.enter_context(nc.sbuf_tensor(name, shape, dt))

        def sem(name):
            return ctx.enter_context(nc.semaphore(name))

        def dram(name, shape):
            return nc.dram_tensor(name, shape, F32, kind="Internal").ap()

        def steps(name, names, ahead=2):
            return Steps(sem(name), names, ahead)

        xe1 = dram("xe1", [E * CAP, XW])
        y1 = dram("y1", [K * N, D])
        xe2 = dram("xe2", [E * REG + SPARE, XW])
        y2 = dram("y2", [K * N, D])

        ps = ctx.enter_context(nc.psum_tensor("ps", [P, 8, 512], F32))

        ident = sb("ident", [P, P])
        before = sb("before", [P, P], BF16)
        ones_bf = sb("ones_bf", [P, P], BF16)
        causal = sb("causal", [P, P])
        zeros = sb("zeros", [P, 2048])
        half_neg = sb("half_neg", [P, 2])
        eps = sb("eps", [P, 2])
        iota_i = sb("iota_i", [P, 64], I32)
        expert_no = sb("expert_no", [P, E])
        slot_base1 = sb("slot_base1", [P, 1, E])
        slot_base2 = sb("slot_base2", [P, 1, E])
        row_id = sb("row_id", [P, NT, K])
        lo_rows = sb("lo_rows", [P, 2])
        tiny = sb("tiny", [P, 8], I32)

        h = sb("h", [P, NT, D])

        ids = sb("ids", [P, NT], I32)
        wqkv = sb("wqkv", [P, 3, H0, C0])
        bqkv = sb("bqkv", [1, 3, H0, C0])
        w_rep = sb("w_rep", [P, 2, G0, P])
        b_rep = sb("b_rep", [1, 2, G0, P])
        one = sb("one", [1, 1])
        bias_qk = sb("bias_qk", [P, 2, G0])
        bias_lo = sb("bias_lo", [P, 2, G0])
        wo = sb("wo", [P, D])
        bv_bc = sb("bv_bc", [P, D])
        bo_bc = sb("bo_bc", [P, D])
        stats_b = sb("stats_b", [P, ST, 6])
        mv_b = sb("mv_b", [P, ST, 2])
        rstd_b = sb("rstd_b", [P, ST])

        wr1 = sb("wr1", [P, E])
        br_bc = sb("br_bc", [P, E])
        xs = sb("xs", [P, 2, ST, K, XW])
        xsT = sb("xsT", [P, L])
        lg = sb("lg", [P, ST, E])
        top8 = sb("top8", [P, ST, 8])
        idx8 = sb("idx8", [P, ST, 8], U32)
        idx_f = sb("idx_f", [P, ST, K])
        neg_top = sb("neg_top", [P, ST])
        e_all = sb("e_all", [P, ST, E])
        z_all = sb("z_all", [P, ST])
        e_top = sb("e_top", [P, ST, K])
        rz = sb("rz", [P, ST])
        pk = sb("pk", [P, ST, K])
        psum_k = sb("psum_k", [P, ST])
        rk = sb("rk", [P, ST])
        onehot = sb("onehot", [P, ST, K, E])
        chosen = sb("chosen", [P, ST, E], BF16)
        counts = sb("counts", [P, 2, E])
        pos = sb("pos", [P, ST, E])
        over = sb("over", [P, ST, E])
        picked = sb("picked", [P, ST, K, E])
        slot = sb("slot", [P, ST, K])
        keep = sb("keep", [P, ST, K])
        slot_u = sb("slot_u", [P, 2, ST, K], U32)


        ln0 = sb("ln0", [P, 2])
        ln1 = sb("ln1", [P, 2, H1])
        qkw = sb("qkw", [P, 2, G1, P])
        qkb = sb("qkb", [P, 2, G1])
        vw = sb("vw", [P, H1, D])
        vb_bc = sb("vb_bc", [P, H1, D])
        w1 = sb("w1", [P, H1, F1])
        b1 = sb("b1", [P, F1 // P])
        b1_all = sb("b1_all", [P, F1 // P])
        w2 = sb("w2", [P, F1 // P, D])
        b2_bc = sb("b2_bc", [P, D])
        wr2 = sb("wr2", [P, E])
        mask = sb("mask", [P, L])

        wgu = sb("wgu", [P, E, 2 * HE])
        wd = sb("wd", [P, E, HT, D])
        n_i = sb("n_i", [1, E], I32)
        n_tiles = sb("n_tiles", [1, 1, E])
        ends = sb("ends", [1, 1, E])
        t_no = sb("t_no", [1, TILES2, 1])
        t_no_i = sb("t_no_i", [1, TILES2], I32)
        t_past = sb("t_past", [1, TILES2, E - 1])
        t_e = sb("t_e", [1, TILES2])
        t_start = sb("t_start", [1, TILES2])
        t_row = sb("t_row", [1, TILES2])
        tab_e = sb("tab_e", [1, TILES2], I32)
        tab_row = sb("tab_row", [1, TILES2], I32)

        layer0 = ExitStack()

        def sb0(name, shape, dt=F32):
            return layer0.enter_context(nc.sbuf_tensor(name, shape, dt))

        ids_s = sb0("ids_s", [P, 2, ST], I32)
        emb = sb0("emb", [P, 2, ST, D])
        stats = sb0("stats", [P, ST, 6])
        mv = sb0("mv", [P, ST, 2])
        rstd = sb0("rstd", [P, ST])
        xn = sb0("xn", [P, 2, ST, D])
        xT = sb0("xT", [P, 2, L])
        hi_t = sb0("hi_t", [P, 2 * G0, L], F32R)
        q_bd = sb0("q_bd", [P, 2, G0, 2, L], F32R)
        k_op = sb0("k_op", [P, 2, G0, L], F32R)
        v_ext = sb0("v_ext", [P, 2, ST, H0, 32])
        mx = sb0("mx", [P, 2, ST, G0, 2])
        m_sel = sb0("m_sel", [P, ST, G0, P])
        pT = sb0("pT", [P, G0, ST, 2, L])
        pv_sb = sb0("pv_sb", [P, 2, L])
        rden = sb0("rden", [P, ST, H0, 1])
        cn = sb0("cn", [P, ST, H0, C0])
        cT = sb0("cT", [P, L])
        w1e = sb0("w1e", [P, 2, F0])
        w2e = sb0("w2e", [P, 2, FT, D])
        b2e = sb0("b2e", [P, 2, D])
        b1e = sb0("b1e", [P, 2, FT])
        xe = sb0("xe", [P, 2, CT, XW])
        xeT = sb0("xeT", [P, 2, CAP])
        hT = sb0("hT", [P, 2, FT, CAP])
        yb = sb0("yb", [P, CT, D])
        ye = sb0("ye", [P, 2, CT, D])
        dst_u = sb0("dst_u", [P, 2, CT], U32)
        layer0.close()

        CH = 4
        yy = sb("yy", [P, 2, K, ST, D])
        stats_a = sb("stats_a", [P, ST, 6])
        mv_a = sb("mv_a", [P, ST, 2])
        rstd_a = sb("rstd_a", [P, ST])
        x1 = sb("x1", [P, 2, ST, D])
        n0 = sb("n0", [P, ST, D])
        x1T = sb("x1T", [P, 2, L])
        x0T = sb("x0T", [P, L])
        exp_q = sb("exp_q", [P, G1, L])
        exp_k = sb("exp_k", [P, G1, L])
        q_bd1 = sb("q_bd1", [P, 2, G1, 4, L])
        k_T1 = sb("k_T1", [P, 2, G1, L])
        v1 = sb("v1", [P, 2, ST, H1, D + 2])
        s_T0 = sb("s_T0", [P, H1, L])
        s_T1 = sb("s_T1", [P, H1, P])
        r_den = sb("r_den", [P, 6, 3])
        o = sb("o", [P, ST, H1 * D])
        stats_o = sb("stats_o", [P, ST, 2, 6])
        mv_o = sb("mv_o", [P, ST, 2])
        rstd_o = sb("rstd_o", [P, ST])
        on = sb("on", [P, ST, H1, D])
        yT = sb("yT", [P, H1, L])
        h1T = sb("h1T", [P, F1 // P, L])
        att = sb("att", [P, ST, D])
        xt = sb("xt", [P, 2, XW])
        xtT = sb("xtT", [P, 2, P])
        meta = sb("meta", [P, TILES2, 2])
        silu = sb("silu", [P, 2, HE])
        gu = sb("gu", [P, 2, HE])
        guT = sb("guT", [P, 2, HT, P])
        yo = sb("yo", [P, 2, D])
        dst2_u = sb("dst2_u", [P, 2, 1], U32)
        y_in = sb("y_in", [P, 2, K, CH, D])

        ld_const = sem("ld_const")
        ld_ids = sem("ld_ids")
        ld_w0 = sem("ld_w0")
        pool_const = sem("pool_const")
        dve_const = sem("dve_const")
        bias_ready = sem("bias_ready")
        zeroed = sem("zeroed")
        held_pool = sem("held_pool")
        held_dve = sem("held_dve")

        embedded = [sem("embedded0"), sem("embedded1")]
        scattered1 = [sem("scattered1_0"), sem("scattered1_1")]
        PG_POOL = steps("pg_pool", ["ids"])
        PA_POOL = steps("pa_pool", ["rstd eps", "rstd", "residual"])
        PA_DVE = steps("pa_dve", ["stats0", "stats1", "mean0", "mean1", "xn0", "xn1", "xT"]
                       + [f"k{g}" for g in range(G0)] + [f"q{g}{x}" for g in range(G0) for x in "ab"]
                       + ["v"] + [f"max{g}" for g in range(G0)])
        PA_ACT = steps("pa_act", [f"hi k{g}" for g in range(G0)] + [f"hi q{g}" for g in range(G0)])
        PA_PE = steps("pa_pe", ["xT"] + [f"k{g}" for g in range(G0)] + [f"q{g}" for g in range(G0)]
                      + ["v"] + [f"scores{g}" for g in range(G0)])
        PB_POOL = steps("pb_pool", ["rstd eps", "rstd"] + [f"onehot{i}" for i in range(4)]
                        + ["chosen", "over", "pos base", "pos over", "picked0", "picked1", "row ids", "sent"])
        PB_DVE = steps("pb_dve", ["max hi", "max lo", "q0", "q1", "rden", "cn", "residual", "stats0", "stats1",
                                  "mean0", "mean1", "xs0", "xs1", "xsT", "logits", "top0", "top1",
                                  "idx0", "idx1", "idx f", "neg top", "rz", "pk", "pair", "pair eps", "rk",
                                  "weights", "pos", "counts", "slot", "slot u", "keep", "kept", "kept sum",
                                  "kept eps", "rkept", "gate"])
        PB_ACT = steps("pb_act", [f"exp{g}" for g in range(G0)] + ["pv", "cT", "z0", "z1", "top0", "top1"])
        PB_PE = steps("pb_pe", ["maxT"] + [f"scores{g}" for g in range(G0)]
                      + ["pv", "ct", "cT", "out", "xsT", "logits", "pos"])

        ld_xe = [sem("ld_xe0"), sem("ld_xe1")]
        ld_we = [sem("ld_we0"), sem("ld_we1")]
        scattered_y1 = [sem("scattered_y1_0"), sem("scattered_y1_1")]
        EX_T = steps("ex_t", ["xT", "xT tail"])
        EX_U = steps("ex_u", [f"up{u}" for u in range(2 * FT)])
        EX_D = steps("ex_d", ["down", "down tail"])
        EX_TD = steps("ex_td", ["xT", "xT tail"])
        EX_UA = steps("ex_ua", [f"gelu{u}" for u in range(2 * FT)])
        EX_DD = steps("ex_dd", ["b2", "b2 tail", "weighted", "dst"])
        EX_POOL = steps("ex_pool", ["sent"])

        ld_w1 = sem("ld_w1")
        ld_yy = [sem("ld_yy0"), sem("ld_yy1")]
        scattered2 = [sem("scattered2_0"), sem("scattered2_1")]
        l1_const = sem("l1_const")
        b1_ready = sem("b1_ready")
        QA_DVE = steps("qa_dve", ["add", "h2", "stats0", "stats1", "mean0", "mean1", "x1_0", "x1_1", "n stats0",
                                  "n stats1", "n mean0", "n mean1", "n0_0", "n0_1", "x1T", "x0T", "k0", "k1"]
                       + [f"q{g}{q}" for g in range(G1) for q in range(4)])
        QA_POOL = steps("qa_pool", ["rstd eps", "rstd", "n rstd eps", "n rstd"])
        QA_PE = steps("qa_pe", ["xT", "k", "q"] + [f"v{n}" for n in range(4)])
        QA_ACT = steps("qa_act", ["k0", "k1", "q0", "q1"] + [f"v{n}" for n in range(4)])
        OUTS = [(s, heads) for s in range(ST) for heads in ((0, 1, 2), (3, 4, 5), (6, 7))]
        QB_PE = steps("qb_pe", [f"s{n}" for n in range(6)] + [f"o{n}" for n in range(6)])
        QB_DVE = steps("qb_dve", [f"s{n}" for n in range(6)]
                       + [x for n, (_, hs) in enumerate(OUTS) for x in [f"r{n}"] + [f"o{n}{i}" for i in range(len(hs))]]
                       + [f"stats{s}{c}" for s in range(ST) for c in range(2)] + ["mean0", "mean1", "n0", "n1"])
        QB_POOL = steps("qb_pool", ["rstd eps", "rstd"])
        QC_PE = steps("qc_pe", [f"y{n}" for n in range(4)] + [f"f{n}" for n in range(4)]
                      + ["out", "xsT", "logits", "pos"])
        QC_DVE = steps("qc_dve", [f"y{n}" for n in range(H1)]
                       + ["b2", "relu", "h3", "stats0", "stats1", "mean0", "mean1", "xs0", "xs1", "xsT", "logits",
                          "top0", "top1", "idx0", "idx1", "idx f", "neg top", "pair", "rk", "pos", "counts",
                          "slot", "slot u", "gate"])
        QC_ACT = steps("qc_act", [f"f{n}" for n in range(4)] + ["top0", "top1"])
        QC_POOL = steps("qc_pool", ["rstd eps", "rstd"] + [f"onehot{i}" for i in range(4)]
                        + ["chosen", "pos base", "picked0", "picked1", "row ids", "sent"])

        table = sem("table")
        ld_xt = [sem("ld_xt0"), sem("ld_xt1")]
        scattered_y2 = [sem("scattered_y2_0"), sem("scattered_y2_1")]
        FT_PE = steps("ft_pe", ["xT"])
        FT_DVE = steps("ft_dve", ["xT", "meta"])
        FU_PE = steps("fu_pe", ["gu"])
        FU_ACT = steps("fu_act", ["silu"])
        FU_DVE = steps("fu_dve", ["gu"])
        FH_PE = steps("fh_pe", ["guT"])
        FH_ACT = steps("fh_act", ["guT"])
        FD_PE = steps("fd_pe", ["out"])
        FD_DVE = steps("fd_dve", ["y", "dst"])
        FD_POOL = steps("fd_pool", ["sent"])

        ld_y2 = [sem("ld_y2_0"), sem("ld_y2_1")]
        summed = sem("summed")
        stored = sem("stored")

        block = ctx.enter_context(nc.Block())

        @block.sync
        def _(sp):
            sp.dma_start(ids[:], a["ids"]).then_inc(ld_ids, 16)
            sp.dma_start(wqkv[:].rearrange("p a h c -> p (a h c)"), a["wqkv"]).then_inc(ld_w0, 16)
            sp.dma_start(bqkv[:].rearrange("p a h c -> p (a h c)"), a["bqkv"]).then_inc(ld_w0, 16)
            sp.dma_start(wo[:], a["wo"]).then_inc(ld_w0, 16)
            sp.dma_start(bv_bc[:], a["bv"].partition_broadcast(P)).then_inc(ld_w0, 16)
            sp.dma_start(bo_bc[:], a["bo"].partition_broadcast(P)).then_inc(ld_w0, 16)
            sp.dma_start(wr1[:], a["wr1"]).then_inc(ld_w0, 16)
            sp.dma_start(br_bc[:], a["br"].partition_broadcast(P)).then_inc(ld_w0, 16)
            sp.wait_ge(pool_const, 2)
            for buf in (xe1, y1, xe2):
                flat = buf.rearrange("(p r) x -> p (r x)", p=P)
                width = flat.shape[1]
                for c in range(0, width, 2048):
                    n = min(2048, width - c)
                    sp.dma_start(flat[:, c:c + n], zeros[:, 0:n]).then_inc(zeroed, 16)
        n_zero = sum(-(-buf.shape[0] * buf.shape[1] // P // 2048) for buf in (xe1, y1, xe2))
        N_W0 = 7 * 16

        @block.gpsimd
        def _(pool):
            for s in (PG_POOL, PA_POOL, PB_POOL, EX_POOL, QA_POOL, QB_POOL, QC_POOL, FD_POOL):
                s.start(pool)
            pool.memset(ident[:], 0.0).then_inc(pool_const, 1)
            pool.memset(zeros[:], 0.0).then_inc(pool_const, 1)
            pool.wait_ge(pool_const, 2)
            pool.affine_select(out=ident[:], in_=ident[:], compare_op=ALU.not_equal, fill=1.0, base=0,
                               pattern=[[-1, P]], channel_multiplier=1).then_inc(pool_const, 1)
            pool.memset(half_neg[:], -0.5).then_inc(pool_const, 1)
            pool.memset(eps[:], EPS).then_inc(pool_const, 1)
            pool.iota(iota_i[:, 0:E], [[1, E]], base=0, channel_multiplier=0).then_inc(pool_const, 1)
            pool.iota(iota_i[:, 8:16], [[CAP, E]], base=0, channel_multiplier=0).then_inc(pool_const, 1)
            pool.iota(iota_i[:, 16:24], [[REG, E]], base=0, channel_multiplier=0).then_inc(pool_const, 1)
            pool.iota(iota_i[:, 32:64], [[P, NT], [N, K]], base=-K * N,
                      channel_multiplier=1).then_inc(pool_const, 1)
            pool.iota(tiny[:, 0:1], [[0, 1]], base=0, channel_multiplier=1).then_inc(pool_const, 1)
            pool.memset(before[:], 1.0).then_inc(pool_const, 1)
            pool.memset(causal[:], 1.0).then_inc(pool_const, 1)
            pool.wait_ge(pool_const, 12)
            pool.affine_select(out=before[:], in_=before[:], compare_op=ALU.is_gt, fill=0.0, base=0,
                               pattern=[[1, P]], channel_multiplier=-1).then_inc(pool_const, 1)
            pool.affine_select(out=causal[:], in_=causal[:], compare_op=ALU.is_ge, fill=0.0, base=0,
                               pattern=[[1, P]], channel_multiplier=-1).then_inc(pool_const, 1)
            pool.wait_ge(ld_ids, 16)

        POOL_CONSTS = 14

        @block.vector
        def _(dve):
            for s in (PA_DVE, PB_DVE, EX_TD, EX_DD, QA_DVE, QB_DVE, QC_DVE, FT_DVE, FU_DVE, FD_DVE):
                s.start(dve)
            dve.memset(w_rep[:], 0.0).then_inc(dve_const, 1)
            dve.memset(b_rep[:], 0.0).then_inc(dve_const, 1)
            dve.memset(one[:], 1.0).then_inc(dve_const, 1)
            dve.memset(ones_bf[:], 1.0).then_inc(dve_const, 1)
            dve.memset(v_ext[:], 1.0).then_inc(dve_const, 1)
            dve.memset(m_sel[:], 0.0).then_inc(dve_const, 1)
            dve.memset(counts[:], 0.0).then_inc(dve_const, 1)
            dve.memset(q_bd[:].bitcast(F32), 0.0).then_inc(dve_const, 1)
            dve.wait_ge(pool_const, 10)
            dve.tensor_copy(expert_no[:], iota_i[:, 0:E]).then_inc(dve_const, 1)
            dve.tensor_copy(slot_base1[:, 0], iota_i[:, 8:16]).then_inc(dve_const, 1)
            dve.tensor_copy(slot_base2[:, 0], iota_i[:, 16:24]).then_inc(dve_const, 1)
            dve.tensor_copy(row_id[:].rearrange("p t k -> p (t k)"), iota_i[:, 32:64]).then_inc(dve_const, 1)
            dve.tensor_scalar(tiny[:, 1:2], tiny[:, 0:1], 48, None, ALU.bitwise_and).then_inc(dve_const, 1)
            dve.wait_ge(dve_const, 13)
            dve.tensor_scalar(lo_rows[:, 0:1], tiny[:, 1:2], 32.0, None, ALU.is_equal).then_inc(dve_const, 1)
            dve.tensor_scalar(lo_rows[:, 1:2], tiny[:, 1:2], 16.0, None, ALU.is_equal).then_inc(dve_const, 1)
            dve.wait_ge(ld_w0, N_W0)
            for x in range(2):
                for dst, src in ((w_rep, wqkv), (b_rep, bqkv)):
                    rows = dst[:, x].rearrange("p g (q r) -> p (g q) r", q=2)
                    for r in range(3):
                        dve.tensor_copy(rows[:, :, 16 * r:16 * r + 16], src[:, x]).then_inc(dve_const, 1)
            dve.memset(b_rep[:, 1].rearrange("p g (q r) -> p (g q) r", q=2)[:, :, 48:50], 1.0)\
               .then_inc(dve_const, 1)
            dve.wait_ge(bias_ready, 1)
            dve.tensor_copy(bias_qk[:].rearrange("p x g -> p (x g)"), ps[:, 0, 0:8]).then_inc(dve_const, 1)
            dve.wait_ge(dve_const, 29)
            for x in range(2):
                dve.tensor_scalar(bias_lo[:, x], bias_qk[:, x], lo_rows[:, x:x + 1], None, ALU.mult)\
                   .then_inc(dve_const, 1)

        DVE_CONSTS = 31

        @block.tensor
        def _(pe):
            for s in (PA_PE, PB_PE, EX_T, EX_U, EX_D, QA_PE, QB_PE, QC_PE, FT_PE, FU_PE, FH_PE, FD_PE):
                s.start(pe)
            pe.wait_ge(dve_const, 28)
            for x in range(2):
                for g in range(G0):
                    mm = pe.matmul(ps[:, 0, x * G0 + g:x * G0 + g + 1], b_rep[:, x, g, :], one[:],
                                   start=True, stop=True)
            mm.then_inc(bias_ready, 1)
            pe.wait_ge(pool_const, POOL_CONSTS)

        @block.scalar
        def _(act):
            for s in (PA_ACT, PB_ACT, EX_UA, QA_ACT, QC_ACT, FU_ACT, FH_ACT):
                s.start(act)
            act.wait_ge(dve_const, DVE_CONSTS)

        def route(pool, own, dve_steps, b, p, cap, base):
            pool.wait_ge(*dve_steps.at(b, "idx f"))
            held(pool, held_pool, b)
            for s in range(ST):
                for k in range(K):
                    pool.tensor_scalar(onehot[:, s, k], expert_no[:], idx_f[:, s, k:k + 1], None,
                                       ALU.is_equal).then_inc(*own.step(f"onehot{s * K + k}"))
            pool.wait_ge(*own.at(b, "onehot3"))
            pool.tensor_tensor(chosen[:], onehot[:, :, 0], onehot[:, :, 1], ALU.add)\
                .then_inc(*own.step("chosen"))
            pool.wait_ge(*dve_steps.at(b, "pos"))
            if cap is not None:
                held(pool, held_pool, b)
                pool.tensor_scalar(over[:], pos[:], cap, BIG, ALU.is_ge, ALU.mult)\
                    .then_inc(*own.step("over"))
                pool.wait_ge(*own.at(b, "over"))
            pool.tensor_tensor(pos[:], pos[:], base[:].broadcast_to([P, ST, E]), ALU.add)\
                .then_inc(*own.step("pos base"))
            pool.wait_ge(*own.at(b, "pos base"))
            if cap is not None:
                pool.tensor_tensor(pos[:], pos[:], over[:], ALU.add).then_inc(*own.step("pos over"))
                pool.wait_ge(*own.at(b, "pos over"))
            for s in range(ST):
                pool.tensor_tensor(picked[:, s], onehot[:, s],
                                   pos[:, s:s + 1, :].broadcast_to([P, K, E]), ALU.mult)\
                    .then_inc(*own.step(f"picked{s}"))
            pool.tensor_copy(xs[:, p, :, :, D], row_id[:, bass.ds(b * ST, ST), :])\
                .then_inc(*own.step("row ids"))

        def scatter(pool, b, p, u, own, dve_steps, rows, n_rows, done):
            pool.wait_ge(*dve_steps.at(b, "gate"))
            held(pool, held_pool, b)
            for s in range(ST):
                for k in range(K):
                    pool.indirect_dma_start(
                        out=rows, out_offset=bass.IndirectOffsetOnAxis(ap=slot_u[:, p, s, k:k + 1], axis=0),
                        in_=xs[:, p, s, k], in_offset=None, bounds_check=n_rows - 1, oob_is_err=False,
                    ).then_inc(done[p], 16)
            pool.wait_ge(done[p], 16 * ST * K * (u + 1))
            pool.sem_inc(*own.step("sent"))

        def norm_rows(dve, own, pool_steps, b, p, rows):
            for s in range(ST):
                dve.bn_stats(stats_b[:, s], rows[s].rearrange("p a d -> p (a d)"))\
                   .then_inc(*own.step(f"stats{s}"))
            dve.wait_ge(*own.at(b, "stats1"))
            held(dve, held_dve, b)
            for s in range(ST):
                dve.bn_aggr(mv_b[:, s], stats_b[:, s]).then_inc(*own.step(f"mean{s}"))
            dve.wait_ge(*pool_steps.at(b, "rstd"))
            for s in range(ST):
                dve.tensor_scalar(xs[:, p, s, :, 0:D], rows[s].broadcast_to([P, K, D]), mv_b[:, s, 0:1],
                                  rstd_b[:, s:s + 1], ALU.subtract, ALU.mult)\
                   .then_inc(*own.step(f"xs{s}"))

        def router(dve, own, pe_steps, act_steps, pool_steps, b, p):
            dve.wait_ge(*pe_steps.at(b, "xsT"))
            dve.tensor_copy(xsT[:], ps[:, 7, 0:L]).then_inc(*own.step("xsT"))
            dve.wait_ge(*pe_steps.at(b, "logits"))
            dve.tensor_tensor(lg[:], ps[:, 7, L:L + ST * E].rearrange("p (s e) -> p s e", s=ST),
                              br_bc[:].unsqueeze(1).broadcast_to([P, ST, E]), ALU.add)\
               .then_inc(*own.step("logits"))
            dve.wait_ge(*own.at(b, "logits"))
            held(dve, held_dve, b)
            for s in range(ST):
                dve.max(top8[:, s], lg[:, s]).then_inc(*own.step(f"top{s}"))
            dve.wait_ge(*own.at(b, "top1"))
            held(dve, held_dve, b)
            for s in range(ST):
                dve.max_index(idx8[:, s], top8[:, s], lg[:, s]).then_inc(*own.step(f"idx{s}"))
            dve.wait_ge(*own.at(b, "idx1"))
            dve.tensor_copy(idx_f[:], idx8[:, :, 0:K]).then_inc(*own.step("idx f"))
            dve.tensor_scalar(neg_top[:], top8[:, :, 0], -1.0, None, ALU.mult)\
               .then_inc(*own.step("neg top"))
            dve.wait_ge(*act_steps.at(b, "top1"))
            dve.reciprocal(rz[:], z_all[:]).then_inc(*own.step("rz"))
            dve.wait_ge(*own.at(b, "rz"))
            dve.tensor_tensor(pk[:], e_top[:], rz[:].unsqueeze(2).broadcast_to([P, ST, K]), ALU.mult)\
               .then_inc(*own.step("pk"))
            dve.wait_ge(*own.at(b, "pk"))
            dve.tensor_reduce(psum_k[:], pk[:], AX, ALU.add).then_inc(*own.step("pair"))
            dve.wait_ge(*own.at(b, "pair"))
            dve.tensor_scalar(psum_k[:], psum_k[:], 1e-9, None, ALU.add).then_inc(*own.step("pair eps"))
            dve.wait_ge(*own.at(b, "pair eps"))
            dve.reciprocal(rk[:], psum_k[:]).then_inc(*own.step("rk"))
            dve.wait_ge(*own.at(b, "rk"))
            dve.tensor_tensor(pk[:], pk[:], rk[:].unsqueeze(2).broadcast_to([P, ST, K]), ALU.mult)\
               .then_inc(*own.step("weights"))
            place(dve, own, pe_steps, b, 0)
            dve.wait_ge(*pool_steps.at(b, "row ids"))
            dve.tensor_reduce(slot[:], picked[:], AX, ALU.add).then_inc(*own.step("slot"))
            dve.wait_ge(*own.at(b, "slot"))
            dve.tensor_copy(slot_u[:, p], slot[:]).then_inc(*own.step("slot u"))
            dve.tensor_scalar(keep[:], slot[:], BIG / 2, None, ALU.is_lt).then_inc(*own.step("keep"))
            dve.wait_ge(*own.at(b, "keep"))
            dve.tensor_tensor(pk[:], pk[:], keep[:], ALU.mult).then_inc(*own.step("kept"))
            dve.wait_ge(*own.at(b, "kept"))
            dve.tensor_reduce(psum_k[:], pk[:], AX, ALU.add).then_inc(*own.step("kept sum"))
            dve.wait_ge(*own.at(b, "kept sum"))
            dve.tensor_scalar(psum_k[:], psum_k[:], 1e-9, None, ALU.add).then_inc(*own.step("kept eps"))
            dve.wait_ge(*own.at(b, "kept eps"))
            dve.reciprocal(rk[:], psum_k[:]).then_inc(*own.step("rkept"))
            dve.wait_ge(*own.at(b, "rkept"))
            dve.tensor_tensor(xs[:, p, :, :, D + 1], pk[:], rk[:].unsqueeze(2).broadcast_to([P, ST, K]),
                              ALU.mult).then_inc(*own.step("gate"))

        def place(dve, own, pe_steps, b, layer):
            dve.wait_ge(*pe_steps.at(b, "pos"))
            o = L + 32
            dve.tensor_tensor(pos[:], ps[:, 7, o:o + ST * E].rearrange("p (s e) -> p s e", s=ST),
                              counts[:, layer:layer + 1].broadcast_to([P, ST, E]), ALU.add)\
               .then_inc(*own.step("pos"))
            dve.wait_ge(*own.at(b, "pos"))
            dve.tensor_tensor(counts[:, layer], ps[:, 7, o + ST * E:o + (ST + 1) * E], counts[:, layer],
                              ALU.add).then_inc(*own.step("counts"))

        def route_pe(pe, own, dve_steps, pool_steps, b, p, wr):
            pe.wait_ge(*dve_steps.at(b, "xs1"))
            for s in range(ST):
                mm = pe.transpose(ps[:, 7, s * P:(s + 1) * P], xs[:, p, s, 0, 0:D], ident[:])
            mm.then_inc(*own.step("xsT"))
            pe.wait_ge(*dve_steps.at(b, "xsT"))
            for s in range(ST):
                mm = pe.matmul(ps[:, 7, L + s * E:L + (s + 1) * E], xsT[:, s * P:(s + 1) * P], wr[:],
                               start=True, stop=True)
            mm.then_inc(*own.step("logits"))
            pe.wait_ge(*pool_steps.at(b, "chosen"))
            o = L + 32
            pe.matmul(ps[:, 7, o:o + E], before[:], chosen[:, 0], start=True, stop=True)
            pe.matmul(ps[:, 7, o + E:o + 2 * E], before[:], chosen[:, 1], start=True, stop=False)
            pe.matmul(ps[:, 7, o + E:o + 2 * E], ones_bf[:], chosen[:, 0], start=False, stop=True)
            pe.matmul(ps[:, 7, o + 2 * E:o + 3 * E], ones_bf[:], chosen[:, 0], start=True, stop=False)
            pe.matmul(ps[:, 7, o + 2 * E:o + 3 * E], ones_bf[:], chosen[:, 1], start=False, stop=True)\
              .then_inc(*own.step("pos"))
        @block.gpsimd
        def _(pool):
            def gather(b, p, u):
                pool.wait_ge(*PA_DVE.at(b - 2, "xn1"))
                pool.wait_ge(*PA_POOL.at(b - 2, "residual"))
                pool.tensor_copy(ids_s[:, p], ids[:, bass.ds(b * ST, ST)]).then_inc(*PG_POOL.step("ids"))
                pool.wait_ge(*PG_POOL.at(b, "ids"))
                held(pool, held_pool, b)
                for s in range(ST):
                    pool.indirect_dma_start(
                        out=emb[:, p, s], out_offset=None, in_=a["embed"],
                        in_offset=bass.IndirectOffsetOnAxis(ap=ids_s[:, p, s:s + 1].bitcast(U32), axis=0),
                    ).then_inc(embedded[p], 16)

            def front(b, p, u):
                pool.wait_ge(*PA_DVE.at(b, "mean1"))
                pool.tensor_tensor(rstd[:], mv[:, :, 1], eps[:], ALU.add)\
                    .then_inc(*PA_POOL.step("rstd eps"))
                pool.wait_ge(*PA_POOL.at(b, "rstd eps"))
                pool.tensor_tensor(rstd[:], rstd[:], half_neg[:], ALU.pow).then_inc(*PA_POOL.step("rstd"))
                pool.wait_ge(embedded[p], 16 * ST * (u + 1))
                pool.tensor_tensor(h[:, bass.ds(b * ST, ST), :], emb[:, p],
                                   bo_bc[:].unsqueeze(1).broadcast_to([P, ST, D]), ALU.add)\
                    .then_inc(*PA_POOL.step("residual"))

            def back(b, p, u):
                pool.wait_ge(*PB_DVE.at(b, "mean1"))
                pool.tensor_tensor(rstd_b[:], mv_b[:, :, 1], eps[:], ALU.add)\
                    .then_inc(*PB_POOL.step("rstd eps"))
                pool.wait_ge(*PB_POOL.at(b, "rstd eps"))
                pool.tensor_tensor(rstd_b[:], rstd_b[:], half_neg[:], ALU.pow)\
                    .then_inc(*PB_POOL.step("rstd"))
                route(pool, PB_POOL, PB_DVE, b, p, float(CAP), slot_base1)
                pool.wait_ge(zeroed, 16 * n_zero)
                scatter(pool, b, p, u, PB_POOL, PB_DVE, xe1, E * CAP, scattered1)

            pool.wait_ge(ld_w0, N_W0)
            skewed(pool, [(gather, 0), (front, 1), (back, 2)], B)

        @block.vector
        def _(dve):
            def front(b, p, u):
                dve.wait_ge(*PA_DVE.at(b - 1, f"max{G0 - 1}"))
                dve.wait_ge(*PB_DVE.at(b - 2, "gate"))
                dve.wait_ge(embedded[p], 16 * ST * (u + 1))
                for s in range(ST):
                    dve.bn_stats(stats[:, s], emb[:, p, s]).then_inc(*PA_DVE.step(f"stats{s}"))
                dve.wait_ge(*PA_DVE.at(b, "stats1"))
                held(dve, held_dve, b)
                for s in range(ST):
                    dve.bn_aggr(mv[:, s], stats[:, s]).then_inc(*PA_DVE.step(f"mean{s}"))
                dve.wait_ge(*PA_POOL.at(b, "rstd"))
                for s in range(ST):
                    dve.tensor_scalar(xn[:, p, s], emb[:, p, s], mv[:, s, 0:1], rstd[:, s:s + 1],
                                      ALU.subtract, ALU.mult).then_inc(*PA_DVE.step(f"xn{s}"))
                dve.wait_ge(*PA_PE.at(b, "xT"))
                dve.tensor_copy(xT[:, p], ps[:, 0, 0:L]).then_inc(*PA_DVE.step("xT"))
                for g in range(G0):
                    dve.wait_ge(*PA_ACT.at(b, f"hi k{g | 1}"))
                    dve.scalar_tensor_tensor(k_op[:, p, g], ps[:, 1 + g // 2, (g % 2) * L:(g % 2 + 1) * L],
                                             bias_qk[:, 1, g:g + 1], hi_t[:, g].bitcast(F32), ALU.add,
                                             ALU.subtract).then_inc(*PA_DVE.step(f"k{g}"))
                for g in range(G0):
                    dve.wait_ge(*PA_ACT.at(b, f"hi q{g | 1}"))
                    for q in range(2):
                        r = slice(64 * q, 64 * q + 64)
                        dve.scalar_tensor_tensor(
                            q_bd[r, p, g, q], ps[r, 1 + g // 2, (g % 2) * L:(g % 2 + 1) * L],
                            bias_qk[r, 0, g:g + 1], hi_t[r, G0 + g].bitcast(F32), ALU.add, ALU.subtract,
                        ).then_inc(*PA_DVE.step(f"q{g}{'ab'[q]}"))
                dve.wait_ge(*PA_PE.at(b, "v"))
                dve.tensor_tensor(v_ext[:, p, :, :, 0:C0],
                                  ps[:, 0, L:2 * L].rearrange("p (s h c) -> p s h c", s=ST, h=H0),
                                  bv_bc[:].rearrange("p (s h c) -> p s h c", s=1, h=H0)
                                  .broadcast_to([P, ST, H0, C0]), ALU.add).then_inc(*PA_DVE.step("v"))
                for g in range(G0):
                    dve.wait_ge(*PA_PE.at(b, f"scores{g}"))
                    bank = 3 + 2 * (g % 2)
                    dve.tensor_reduce(mx[:, p, :, g, :],
                                      ps[:, bank:bank + 2].rearrange("p s (q t) -> p s q t", q=2), AX,
                                      ALU.max).then_inc(*PA_DVE.step(f"max{g}"))

            def back(b, p, u):
                dve.wait_ge(*PA_DVE.at(b, f"max{G0 - 1}"))
                dve.wait_ge(*PB_DVE.at(b - 1, "gate"))
                maxima = mx[:, p].rearrange("p s g q -> p (s g q)")
                sel = m_sel[:].rearrange("p s g (q r) -> p (s g q) r", q=2)
                dve.tensor_scalar(sel[:, :, 48].bitcast(F32R), maxima, -1.0, None, ALU.mult)\
                   .then_inc(*PB_DVE.step("max hi"))
                dve.wait_ge(*PB_DVE.at(b, "max hi"))
                dve.scalar_tensor_tensor(sel[:, :, 49].bitcast(F32R), maxima, -1.0, sel[:, :, 48],
                                         ALU.mult, ALU.subtract).then_inc(*PB_DVE.step("max lo"))
                dve.wait_ge(*PB_PE.at(b, "maxT"))
                for q in range(2):
                    r = slice(64 * q, 64 * q + 64)
                    dve.tensor_tensor(q_bd[r, p, :, q],
                                      ps[r, 1:3].rearrange("p k (g t) -> p (k g) t", g=2),
                                      q_bd[r, p, :, q].bitcast(F32), ALU.add)\
                       .then_inc(*PB_DVE.step(f"q{q}"))
                dve.wait_ge(*PB_PE.at(b, "ct"))
                heads = ps[:, 7].rearrange("p (s h c) -> p (s h) c", s=ST, h=H0)
                dve.reciprocal(rden[:].rearrange("p s h c -> p (s h) c"), heads[:, :, C0:C0 + 1])\
                   .then_inc(*PB_DVE.step("rden"))
                dve.wait_ge(*PB_DVE.at(b, "rden"))
                dve.tensor_tensor(cn[:].rearrange("p s h c -> p (s h) c"), heads[:, :, 0:C0],
                                  rden[:].rearrange("p s h c -> p (s h) c").broadcast_to([P, ST * H0, C0]),
                                  ALU.mult).then_inc(*PB_DVE.step("cn"))
                rows = h[:, bass.ds(b * ST, ST), :]
                dve.wait_ge(*PB_PE.at(b, "out"))
                dve.wait_ge(*PA_POOL.at(b, "residual"))
                dve.tensor_tensor(rows, ps[:, 7, L:2 * L].rearrange("p (s d) -> p s d", s=ST), rows, ALU.add)\
                   .then_inc(*PB_DVE.step("residual"))
                dve.wait_ge(*PB_DVE.at(b, "residual"))
                held(dve, held_dve, b)
                norm_rows(dve, PB_DVE, PB_POOL, b, p, [h[:, bass.ds(b * ST + s, 1), :] for s in range(ST)])
                router(dve, PB_DVE, PB_PE, PB_ACT, PB_POOL, b, p)

            skewed(dve, [(front, 1), (back, 2)], B)

        @block.scalar
        def _(act):
            def front(b, p, u):
                for x, name in ((1, "k"), (0, "q")):
                    for g in range(G0):
                        act.wait_ge(*PA_PE.at(b, f"{name}{g | 1}"))
                        act.activation(hi_t[:, (1 - x) * G0 + g],
                                       ps[:, 1 + g // 2, (g % 2) * L:(g % 2 + 1) * L], ACT.Identity,
                                       bias=bias_lo[:, x, g:g + 1], scale=lo_rows[:, x:x + 1])\
                           .then_inc(*PA_ACT.step(f"hi {name}{g}"))

            def back(b, p, u):
                for g in range(G0):
                    act.wait_ge(*PB_PE.at(b, f"scores{g}"))
                    bank = 3 + 2 * (g % 2)
                    act.activation(pT[:, g].rearrange("p s q t -> p (s q t)"),
                                   ps[:, bank:bank + 2].rearrange("p s t -> p (s t)"), ACT.Exp,
                                   scale=float(C0) ** -0.5).then_inc(*PB_ACT.step(f"exp{g}"))
                act.wait_ge(*PB_PE.at(b, "pv"))
                act.activation(pv_sb[:].rearrange("p g t -> p (g t)"), ps[:, 7], ACT.Identity)\
                   .then_inc(*PB_ACT.step("pv"))
                act.wait_ge(*PB_PE.at(b, "cT"))
                act.activation(cT[:], ps[:, 7, 0:L], ACT.Identity).then_inc(*PB_ACT.step("cT"))
                act.wait_ge(*PB_DVE.at(b, "neg top"))
                for s in range(ST):
                    act.activation(e_all[:, s], lg[:, s], ACT.Exp, bias=neg_top[:, s:s + 1],
                                   accum_out=z_all[:, s:s + 1]).then_inc(*PB_ACT.step(f"z{s}"))
                for s in range(ST):
                    act.activation(e_top[:, s], top8[:, s, 0:K], ACT.Exp, bias=neg_top[:, s:s + 1])\
                       .then_inc(*PB_ACT.step(f"top{s}"))

            skewed(act, [(front, 1), (back, 2)], B)

        @block.tensor
        def _(pe):
            def front(b, p, u):
                pe.wait_ge(*PA_DVE.at(b, "xn1"))
                for s in range(ST):
                    mm = pe.transpose(ps[:, 0, s * P:(s + 1) * P], xn[:, p, s], ident[:])
                mm.then_inc(*PA_PE.step("xT"))
                pe.wait_ge(*PA_DVE.at(b, "xT"))
                pe.wait_ge(*PB_DVE.at(b - 2, "q1"))
                for x, name in ((1, "k"), (0, "q")):
                    for g in range(G0):
                        if name == "q":
                            pe.wait_ge(*PA_DVE.at(b, f"k{g | 1}"))
                        pe.matmul(ps[:, 1 + g // 2, (g % 2) * L:(g % 2 + 1) * L], w_rep[:, x, g], xT[:, p],
                                  start=True, stop=True).then_inc(*PA_PE.step(f"{name}{g}"))
                for s in range(ST):
                    mm = pe.matmul(ps[:, 0, L + s * P:L + (s + 1) * P], xT[:, p, s * P:(s + 1) * P],
                                   wqkv[:, 2].rearrange("p h c -> p (h c)"), start=True, stop=True)
                mm.then_inc(*PA_PE.step("v"))
                for g in range(G0):
                    pe.wait_ge(*PA_DVE.at(b, f"q{g}b"))
                    if g < 2:
                        pe.wait_ge(*PB_ACT.at(b - 2, f"exp{g + 2}"))
                    else:
                        pe.wait_ge(*PA_DVE.at(b, f"max{g - 2}"))
                    for s in range(ST):
                        for q in range(2):
                            mm = pe.matmul(ps[:, 3 + 2 * (g % 2) + s, q * L:(q + 1) * L],
                                           q_bd[:, p, g, q, s * P:(s + 1) * P], k_op[:, p, g],
                                           start=True, stop=True)
                    mm.then_inc(*PA_PE.step(f"scores{g}"))

            def back(b, p, u):
                pe.wait_ge(*PB_DVE.at(b, "max lo"))
                if not isinstance(b, int) or b + 1 < B:
                    pe.wait_ge(*PA_DVE.at(b + 1, f"max{G0 - 1}"))
                for g in range(G0):
                    for s in range(ST):
                        mm = pe.transpose(ps[:, 1 + g // 2, (g % 2) * L + s * P:(g % 2) * L + (s + 1) * P],
                                          m_sel[:, s, g], ident[:])
                mm.then_inc(*PB_PE.step("maxT"))
                pe.wait_ge(*PB_DVE.at(b, "q1"))
                for g in range(G0):
                    if g < 2:
                        pe.wait_ge(*PB_ACT.at(b - 1, f"exp{g + 2}"))
                    else:
                        pe.wait_ge(*PB_ACT.at(b, f"exp{g - 2}"))
                    for s in range(ST):
                        mm = pe.matmul(ps[:, 3 + 2 * (g % 2) + s], k_op[:, p, g, s * P:(s + 1) * P],
                                       q_bd[:, p, g].rearrange("p q t -> p (q t)"), start=True, stop=True)
                    mm.then_inc(*PB_PE.step(f"scores{g}"))
                pe.wait_ge(*PB_ACT.at(b, "exp3"))
                pe.wait_ge(*PB_DVE.at(b - 1, "counts"))
                for hd in range(H0):
                    j = hd % 4
                    for s in range(ST):
                        mm = pe.matmul(ps[32 * j:32 * j + 32, 7, (hd // 4) * L:(hd // 4 + 1) * L],
                                       v_ext[:, p, s, hd], pT[:, hd // 2, s, hd % 2], start=(s == 0),
                                       stop=(s == ST - 1))
                mm.then_inc(*PB_PE.step("pv"))
                pe.wait_ge(*PB_ACT.at(b, "pv"))
                for s in range(ST):
                    for g in range(2):
                        mm = pe.transpose(ps[:, 7, s * L + g * P:s * L + (g + 1) * P],
                                          pv_sb[:, g, s * P:(s + 1) * P], ident[:])
                mm.then_inc(*PB_PE.step("ct"))
                pe.wait_ge(*PB_DVE.at(b, "cn"))
                for s in range(ST):
                    mm = pe.transpose(ps[:, 7, s * P:(s + 1) * P], cn[:, s].rearrange("p h c -> p (h c)"),
                                      ident[:])
                mm.then_inc(*PB_PE.step("cT"))
                pe.wait_ge(*PB_ACT.at(b, "cT"))
                for s in range(ST):
                    mm = pe.matmul(ps[:, 7, L + s * P:L + (s + 1) * P], cT[:, s * P:(s + 1) * P], wo[:],
                                   start=True, stop=True)
                mm.then_inc(*PB_PE.step("out"))
                route_pe(pe, PB_PE, PB_DVE, PB_POOL, b, p, wr1)

            skewed(pe, [(front, 1), (back, 2)], B)


        N_SENT1 = 16 * ST * K * B // 2
        HALF = CAP // 2

        @block.sync
        def _(sp):
            def load(e, p, u):
                sp.wait_ge(*EX_D.at(e - 2, "down tail"))
                sp.wait_ge(*EX_DD.at(e - 2, "dst"))
                sp.dma_start(w1e[:, p], a["w1e"][bass.ds(e, 1)].rearrange("e d f -> d (e f)"))\
                  .then_inc(ld_we[p], 16)
                sp.dma_start(w2e[:, p].rearrange("p c d -> p (c d)"),
                             a["w2e"][bass.ds(e, 1)].rearrange("e p c d -> p (e c d)"))\
                  .then_inc(ld_we[p], 16)
                sp.dma_start(b2e[:, p], a["b2e"][bass.ds(e, 1)].rearrange("e d -> (e d)").partition_broadcast(P))\
                  .then_inc(ld_we[p], 16)
                sp.dma_start(b1e[:, p], a["b1e"][bass.ds(e, 1)].rearrange("e p f -> p (e f)"))\
                  .then_inc(ld_we[p], 16)
                for q in range(2):
                    sp.wait_ge(scattered1[q], N_SENT1)
                sp.dma_start(xe[:, p], xe1.rearrange("(e j p) x -> e p j x", e=E, j=CT)[bass.ds(e, 1)]
                             .rearrange("e p j x -> (e p) j x")).then_inc(ld_xe[p], 16)

            skewed(sp, [(load, 0)], E)

        @block.tensor
        def _(pe):
            def turn(e, p, u):
                pe.wait_ge(ld_xe[p], 16 * (u + 1))
                pe.wait_ge(*EX_TD.at(e - 1, "xT tail"))
                for j in range(4):
                    mm = pe.transpose(ps[:, 0, j * P:(j + 1) * P], xe[:, p, j, 0:D], ident[:])
                mm.then_inc(*EX_T.step("xT"))
                pe.transpose(ps[:, 1, 0:P], xe[:, p, 4, 0:D], ident[:]).then_inc(*EX_T.step("xT tail"))

            def up(e, p, u):
                pe.wait_ge(*EX_TD.at(e, "xT tail"))
                pe.wait_ge(ld_we[p], 64 * (u + 1))
                for n in range(2 * FT):
                    f, half = n // 2, n % 2
                    pe.wait_ge(*(EX_UA.at(e - 1, f"gelu{n + 4}") if n < 4 else EX_UA.at(e, f"gelu{n - 4}")))
                    pe.matmul(ps[:, 2 + n % 4, 0:HALF], w1e[:, p, f * P:(f + 1) * P],
                              xeT[:, p, half * HALF:(half + 1) * HALF], start=True, stop=True)\
                      .then_inc(*EX_U.step(f"up{n}"))

            def down(e, p, u):
                pe.wait_ge(*EX_UA.at(e, f"gelu{2 * FT - 1}"))
                for j in range(CT):
                    pe.wait_ge(*EX_DD.at(e - 1, "b2 tail"))
                    for f in range(FT):
                        mm = pe.matmul(ps[:, 6 + j // 4, (j % 4) * P:(j % 4 + 1) * P],
                                       hT[:, p, f, j * P:(j + 1) * P], w2e[:, p, f], start=(f == 0),
                                       stop=(f == FT - 1))
                    if j == 3:
                        mm.then_inc(*EX_D.step("down"))
                mm.then_inc(*EX_D.step("down tail"))

            skewed(pe, [(up, 1), (turn, 0), (down, 1)], E)

        @block.scalar
        def _(act):
            def up(e, p, u):
                act.wait_ge(*EX_D.at(e - 2, "down tail"))
                act.wait_ge(ld_we[p], 64 * (u + 1))
                for n in range(2 * FT):
                    f, half = n // 2, n % 2
                    act.wait_ge(*EX_U.at(e, f"up{n}"))
                    act.activation(hT[:, p, f, half * HALF:(half + 1) * HALF], ps[:, 2 + n % 4, 0:HALF],
                                   ACT.Gelu, bias=b1e[:, p, f:f + 1]).then_inc(*EX_UA.step(f"gelu{n}"))

            skewed(act, [(up, 1)], E)

        @block.vector
        def _(dve):
            def turn(e, p, u):
                dve.wait_ge(*EX_U.at(e - 2, f"up{2 * FT - 1}"))
                dve.wait_ge(*EX_T.at(e, "xT"))
                dve.tensor_copy(xeT[:, p, 0:4 * P], ps[:, 0]).then_inc(*EX_TD.step("xT"))
                dve.wait_ge(*EX_T.at(e, "xT tail"))
                dve.tensor_copy(xeT[:, p, 4 * P:], ps[:, 1, 0:P]).then_inc(*EX_TD.step("xT tail"))

            def down(e, p, u):
                b2 = b2e[:, p:p + 1].broadcast_to([P, 4, D])
                dve.wait_ge(*EX_DD.at(e - 1, "dst"))
                dve.wait_ge(*EX_D.at(e, "down"))
                dve.tensor_tensor(yb[:, 0:4], ps[:, 6].rearrange("p (j d) -> p j d", j=4), b2, ALU.add)\
                   .then_inc(*EX_DD.step("b2"))
                dve.wait_ge(*EX_D.at(e, "down tail"))
                dve.tensor_tensor(yb[:, 4], ps[:, 7, 0:D], b2e[:, p], ALU.add)\
                   .then_inc(*EX_DD.step("b2 tail"))
                dve.wait_ge(*EX_DD.at(e, "b2 tail"))
                dve.wait_ge(*EX_POOL.at(e - 2, "sent"))
                dve.tensor_tensor(ye[:, p], yb[:], xe[:, p, :, D + 1:D + 2].broadcast_to([P, CT, D]),
                                  ALU.mult).then_inc(*EX_DD.step("weighted"))
                dve.tensor_scalar(dst_u[:, p], xe[:, p, :, D], float(K * N), None, ALU.add)\
                   .then_inc(*EX_DD.step("dst"))

            skewed(dve, [(turn, 0), (down, 1)], E)

        @block.gpsimd
        def _(pool):
            def send(e, p, u):
                pool.wait_ge(*EX_DD.at(e, "dst"))
                held(pool, held_pool, e)
                for j in range(CT):
                    pool.indirect_dma_start(
                        out=y1, out_offset=bass.IndirectOffsetOnAxis(ap=dst_u[:, p, j:j + 1], axis=0),
                        in_=ye[:, p, j], in_offset=None, bounds_check=K * N - 1, oob_is_err=False,
                    ).then_inc(scattered_y1[p], 16)
                pool.wait_ge(scattered_y1[p], 16 * CT * (u + 1))
                pool.sem_inc(*EX_POOL.step("sent"))

            skewed(pool, [(send, 1)], E)

        N_SENT_Y1 = 16 * CT * E // 2

        @block.sync
        def _(sp):
            for dst, src in ((ln0[:, 0:1], "ln0_w"), (ln0[:, 1:2], "ln0_b"), (ln1[:, 0], "ln1_w"), (ln1[:, 1], "ln1_b"),
                             (qkw[:, 0].rearrange("p g c -> p (g c)"), "qw"),
                             (qkw[:, 1].rearrange("p g c -> p (g c)"), "kw"), (qkb[:, 0], "qb"), (qkb[:, 1], "kb"),
                             (vw[:].rearrange("p h c -> p (h c)"), "vw"), (w1[:], "w1"), (b1[:], "b1"),
                             (w2[:], "w2"), (wr2[:], "wr2"), (wgu[:], "wgu"), (wd[:], "wd")):
                sp.dma_start(dst, a[src]).then_inc(ld_w1, 16)
            sp.dma_start(vb_bc[:].rearrange("p h c -> p (h c)"), a["vb"].partition_broadcast(P)).then_inc(ld_w1, 16)
            sp.dma_start(b2_bc[:], a["b2"].partition_broadcast(P)).then_inc(ld_w1, 16)
            for q in range(2):
                sp.wait_ge(scattered_y1[q], N_SENT_Y1)

            def load(b, p, u):
                sp.wait_ge(*QA_DVE.at(b - 2, "h2"))
                for k in range(K):
                    sp.dma_start(yy[:, p, k], y1.rearrange("(k t p) d -> k p t d", k=K, t=NT)
                                 [k][:, bass.ds(b * ST, ST), :]).then_inc(ld_yy[p], 16)

            skewed(sp, [(load, 0)], B)

        N_W1 = 17 * 16

        @block.gpsimd
        def _(pool):
            def keys(b, p, u):
                for name in ("", "n "):
                    pool.wait_ge(*QA_DVE.at(b, name + "mean1"))
                    pool.tensor_tensor(rstd_a[:], mv_a[:, :, 1], eps[:], ALU.add)\
                        .then_inc(*QA_POOL.step(name + "rstd eps"))
                    pool.wait_ge(*QA_POOL.at(b, name + "rstd eps"))
                    pool.tensor_tensor(rstd_a[:], rstd_a[:], half_neg[:], ALU.pow)\
                        .then_inc(*QA_POOL.step(name + "rstd"))

            def outputs(b, p, u):
                pool.wait_ge(*QB_DVE.at(b, "mean1"))
                pool.tensor_tensor(rstd_o[:], mv_o[:, :, 1], eps[:], ALU.add)\
                    .then_inc(*QB_POOL.step("rstd eps"))
                pool.wait_ge(*QB_POOL.at(b, "rstd eps"))
                pool.tensor_tensor(rstd_o[:], rstd_o[:], half_neg[:], ALU.pow).then_inc(*QB_POOL.step("rstd"))

            def after(b, p, u):
                pool.wait_ge(*QC_DVE.at(b, "mean1"))
                pool.tensor_tensor(rstd_b[:], mv_b[:, :, 1], eps[:], ALU.add)\
                    .then_inc(*QC_POOL.step("rstd eps"))
                pool.wait_ge(*QC_POOL.at(b, "rstd eps"))
                pool.tensor_tensor(rstd_b[:], rstd_b[:], half_neg[:], ALU.pow)\
                    .then_inc(*QC_POOL.step("rstd"))
                route(pool, QC_POOL, QC_DVE, b, p, None, slot_base2)
                scatter(pool, b, p, u, QC_POOL, QC_DVE, xe2, E * REG, scattered2)

            skewed(pool, [(outputs, 1), (keys, 0), (after, 1)], B)

        @block.vector
        def _(dve):
            dve.wait_ge(pool_const, POOL_CONSTS)
            dve.memset(q_bd1[:], 0.0).then_inc(l1_const, 1)
            dve.memset(v1[:, :, :, :, D:], 1.0).then_inc(l1_const, 1)
            dve.memset(mask[:, P:], 1.0).then_inc(l1_const, 1)
            dve.tensor_copy(mask[:, 0:P], causal[:]).then_inc(l1_const, 1)
            dve.wait_ge(ld_w1, N_W1)
            dve.wait_ge(b1_ready, 1)
            dve.tensor_tensor(b1_all[:], ps[:, 0, 0:4], b1[:], ALU.add).then_inc(l1_const, 1)
            dve.wait_ge(l1_const, 5)

            def keys(b, p, u):
                rows = h[:, bass.ds(b * ST, ST), :]
                dve.wait_ge(*QA_DVE.at(b - 1, "q13"))
                dve.wait_ge(*QC_DVE.at(b - 2, "gate"))
                dve.wait_ge(ld_yy[p], 16 * K * (u + 1))
                dve.tensor_tensor(yy[:, p, 0], yy[:, p, 0], yy[:, p, 1], ALU.add).then_inc(*QA_DVE.step("add"))
                dve.wait_ge(*QA_DVE.at(b, "add"))
                dve.tensor_tensor(rows, yy[:, p, 0], rows, ALU.add).then_inc(*QA_DVE.step("h2"))
                dve.wait_ge(*QA_DVE.at(b, "h2"))
                held(dve, held_dve, b)
                for s in range(ST):
                    dve.bn_stats(stats_a[:, s], h[:, bass.ds(b * ST + s, 1), :].rearrange("p a d -> p (a d)"))\
                       .then_inc(*QA_DVE.step(f"stats{s}"))
                dve.wait_ge(*QA_DVE.at(b, "stats1"))
                held(dve, held_dve, b)
                for s in range(ST):
                    dve.bn_aggr(mv_a[:, s], stats_a[:, s]).then_inc(*QA_DVE.step(f"mean{s}"))
                dve.wait_ge(*QA_POOL.at(b, "rstd"))
                for s in range(ST):
                    dve.tensor_scalar(x1[:, p, s:s + 1], h[:, bass.ds(b * ST + s, 1), :], mv_a[:, s, 0:1],
                                      rstd_a[:, s:s + 1], ALU.subtract, ALU.mult)\
                       .then_inc(*QA_DVE.step(f"x1_{s}"))
                dve.wait_ge(*QA_DVE.at(b, "x1_1"))
                for s in range(ST):
                    dve.bn_stats(stats_a[:, s], x1[:, p, s]).then_inc(*QA_DVE.step(f"n stats{s}"))
                dve.wait_ge(*QA_DVE.at(b, "n stats1"))
                held(dve, held_dve, b)
                for s in range(ST):
                    dve.bn_aggr(mv_a[:, s], stats_a[:, s]).then_inc(*QA_DVE.step(f"n mean{s}"))
                dve.wait_ge(*QA_POOL.at(b, "n rstd"))
                for s in range(ST):
                    dve.tensor_scalar(n0[:, s], x1[:, p, s], mv_a[:, s, 0:1], rstd_a[:, s:s + 1],
                                      ALU.subtract, ALU.mult).then_inc(*QA_DVE.step(f"n0_{s}"))
                dve.wait_ge(*QA_PE.at(b, "xT"))
                dve.tensor_copy(x1T[:, p], ps[:, 0, 0:L]).then_inc(*QA_DVE.step("x1T"))
                dve.tensor_scalar(x0T[:], ps[:, 0, L:], ln0[:, 0:1], ln0[:, 1:2], ALU.mult, ALU.add)\
                   .then_inc(*QA_DVE.step("x0T"))
                lo, hi = float(np.exp(np.float32(-10))), float(np.exp(np.float32(10)))
                for g in range(G1):
                    dve.wait_ge(*QA_ACT.at(b, f"k{g}"))
                    dve.tensor_scalar(k_T1[:, p, g], exp_k[:, g], hi, lo, ALU.min, ALU.max)\
                       .then_inc(*QA_DVE.step(f"k{g}"))
                for g in range(G1):
                    dve.wait_ge(*QA_ACT.at(b, f"q{g}"))
                    for q in range(4):
                        r = slice(32 * q, 32 * q + 32)
                        dve.tensor_scalar(q_bd1[r, p, g, q], exp_q[r, g], hi, lo, ALU.min, ALU.max)\
                           .then_inc(*QA_DVE.step(f"q{g}{q}"))

            def outputs(b, p, u):
                dve.wait_ge(*QB_DVE.at(b - 1, "n1"))
                for n in range(6):
                    g, m = n // 3, n % 3
                    dve.wait_ge(*QB_PE.at(b, f"s{n}"))
                    bank = ps[:, 3 + n % 2]
                    if m < 2:
                        hs = slice(4 * g + 2 * m, 4 * g + 2 * m + 2)
                        dve.tensor_tensor(s_T0[:, hs], bank.rearrange("p (h l) -> p h l", h=2),
                                          mask[:].unsqueeze(1).broadcast_to([P, 2, L]), ALU.mult)\
                           .then_inc(*QB_DVE.step(f"s{n}"))
                    else:
                        dve.tensor_tensor(s_T1[:, 4 * g:4 * g + 4], bank.rearrange("p (h l) -> p h l", h=4),
                                          causal[:].unsqueeze(1).broadcast_to([P, 4, P]), ALU.mult)\
                           .then_inc(*QB_DVE.step(f"s{n}"))
                for n, (s, hs) in enumerate(OUTS):
                    dve.wait_ge(*QB_PE.at(b, f"o{n}"))
                    bank = ps[:, 5 + n % 2, 0:(D + 1) * len(hs)].rearrange("p (h d) -> p h d", d=D + 1)
                    dve.reciprocal(r_den[:, n, 0:len(hs)].unsqueeze(2), bank[:, :, D:D + 1])\
                       .then_inc(*QB_DVE.step(f"r{n}"))
                    dve.wait_ge(*QB_DVE.at(b, f"r{n}"))
                    for i, hd in enumerate(hs):
                        dve.scalar_tensor_tensor(o[:, s, hd * D:(hd + 1) * D], bank[:, i, 0:D],
                                                 r_den[:, n, i:i + 1], vb_bc[:, hd], ALU.mult, ALU.add)\
                           .then_inc(*QB_DVE.step(f"o{n}{i}"))
                dve.wait_ge(*QB_DVE.at(b, "o51"))
                for s in range(ST):
                    for c in range(2):
                        dve.bn_stats(stats_o[:, s, c], o[:, s, 512 * c:512 * c + 512])\
                           .then_inc(*QB_DVE.step(f"stats{s}{c}"))
                dve.wait_ge(*QB_DVE.at(b, "stats11"))
                held(dve, held_dve, b)
                for s in range(ST):
                    dve.bn_aggr(mv_o[:, s], stats_o[:, s].rearrange("p c x -> p (c x)"))\
                       .then_inc(*QB_DVE.step(f"mean{s}"))
                dve.wait_ge(*QB_POOL.at(b, "rstd"))
                dve.wait_ge(*QC_PE.at(b - 1, "y3"))
                for s in range(ST):
                    dve.tensor_scalar(on[:, s].rearrange("p h d -> p (h d)"), o[:, s], mv_o[:, s, 0:1],
                                      rstd_o[:, s:s + 1], ALU.subtract, ALU.mult)\
                       .then_inc(*QB_DVE.step(f"n{s}"))

            def after(b, p, u):
                rows = h[:, bass.ds(b * ST, ST), :]
                dve.wait_ge(*QC_DVE.at(b - 1, "gate"))
                for n in range(H1):
                    dve.wait_ge(*QC_PE.at(b, f"y{n // 2}"))
                    dve.scalar_tensor_tensor(yT[:, n], ps[:, (7, 0)[n // 2 % 2], (n % 2) * L:(n % 2 + 1) * L],
                                             ln1[:, 0, n:n + 1], x1T[:, p], ALU.mult, ALU.add)\
                       .then_inc(*QC_DVE.step(f"y{n}"))
                dve.wait_ge(*QC_PE.at(b, "out"))
                dve.tensor_tensor(att[:], ps[:, 7, 0:L].rearrange("p (s d) -> p s d", s=ST),
                                  b2_bc[:].unsqueeze(1).broadcast_to([P, ST, D]), ALU.add)\
                   .then_inc(*QC_DVE.step("b2"))
                dve.wait_ge(*QC_DVE.at(b, "b2"))
                dve.scalar_tensor_tensor(att[:], att[:], 0.0, x1[:, p], ALU.max, ALU.add)\
                   .then_inc(*QC_DVE.step("relu"))
                dve.wait_ge(*QC_DVE.at(b, "relu"))
                dve.tensor_tensor(rows, att[:], rows, ALU.add).then_inc(*QC_DVE.step("h3"))
                dve.wait_ge(*QC_DVE.at(b, "h3"))
                held(dve, held_dve, b)
                norm_rows(dve, QC_DVE, QC_POOL, b, p, [h[:, bass.ds(b * ST + s, 1), :] for s in range(ST)])
                own = QC_DVE
                dve.wait_ge(*QC_PE.at(b, "xsT"))
                dve.tensor_copy(xsT[:], ps[:, 7, 0:L]).then_inc(*own.step("xsT"))
                dve.wait_ge(*QC_PE.at(b, "logits"))
                dve.tensor_copy(lg[:].rearrange("p s e -> p (s e)"), ps[:, 7, L:L + ST * E])\
                   .then_inc(*own.step("logits"))
                dve.wait_ge(*own.at(b, "logits"))
                held(dve, held_dve, b)
                for s in range(ST):
                    dve.max(top8[:, s], lg[:, s]).then_inc(*own.step(f"top{s}"))
                dve.wait_ge(*own.at(b, "top1"))
                held(dve, held_dve, b)
                for s in range(ST):
                    dve.max_index(idx8[:, s], top8[:, s], lg[:, s]).then_inc(*own.step(f"idx{s}"))
                dve.wait_ge(*own.at(b, "idx1"))
                dve.tensor_copy(idx_f[:], idx8[:, :, 0:K]).then_inc(*own.step("idx f"))
                dve.tensor_scalar(neg_top[:], top8[:, :, 0], -1.0, None, ALU.mult)\
                   .then_inc(*own.step("neg top"))
                dve.wait_ge(*QC_ACT.at(b, "top1"))
                dve.tensor_reduce(psum_k[:], e_top[:], AX, ALU.add).then_inc(*own.step("pair"))
                dve.wait_ge(*own.at(b, "pair"))
                dve.reciprocal(rk[:], psum_k[:]).then_inc(*own.step("rk"))
                place(dve, own, QC_PE, b, 1)
                dve.wait_ge(*QC_POOL.at(b, "row ids"))
                dve.tensor_reduce(slot[:], picked[:], AX, ALU.add).then_inc(*own.step("slot"))
                dve.wait_ge(*own.at(b, "slot"))
                dve.tensor_copy(slot_u[:, p], slot[:]).then_inc(*own.step("slot u"))
                dve.tensor_tensor(xs[:, p, :, :, D + 1], e_top[:], rk[:].unsqueeze(2).broadcast_to([P, ST, K]),
                                  ALU.mult).then_inc(*own.step("gate"))

            skewed(dve, [(outputs, 1), (keys, 0), (after, 1)], B)

        @block.scalar
        def _(act):
            act.wait_ge(l1_const, 5)

            def keys(b, p, u):
                act.wait_ge(*QA_DVE.at(b - 1, "q13"))
                for x, dst, name, bank in ((1, exp_k, "k", 2), (0, exp_q, "q", 1)):
                    act.wait_ge(*QA_PE.at(b, name))
                    for g in range(G1):
                        act.activation(dst[:, g], ps[:, bank, g * L:(g + 1) * L], ACT.Exp,
                                       bias=qkb[:, x, g:g + 1]).then_inc(*QA_ACT.step(f"{name}{g}"))
                for n in range(4):
                    s, half = n // 2, n % 2
                    act.wait_ge(*QA_PE.at(b, f"v{n}"))
                    act.activation(v1[:, p, s, 4 * half:4 * half + 4, 0:D],
                                   ps[:, 2 - n % 2].rearrange("p (h d) -> p h d", h=4), ACT.Identity)\
                       .then_inc(*QA_ACT.step(f"v{n}"))

            def after(b, p, u):
                for n in range(4):
                    act.wait_ge(*QC_PE.at(b, f"f{n}"))
                    act.activation(h1T[:, n], ps[:, (7, 0)[n % 2], 0:L], ACT.Relu, bias=b1_all[:, n:n + 1])\
                       .then_inc(*QC_ACT.step(f"f{n}"))
                act.wait_ge(*QC_DVE.at(b, "neg top"))
                for s in range(ST):
                    act.activation(e_top[:, s], top8[:, s, 0:K], ACT.Exp, bias=neg_top[:, s:s + 1])\
                       .then_inc(*QC_ACT.step(f"top{s}"))

            skewed(act, [(keys, 0), (after, 1)], B)

        @block.tensor
        def _(pe):
            pe.wait_ge(ld_w1, N_W1)
            pe.wait_ge(*EX_TD.at(E - 1, "xT tail"))
            for f in range(F1 // P):
                for hd in range(H1):
                    mm = pe.matmul(ps[:, 0, f:f + 1], w1[:, hd, f * P:(f + 1) * P], ln1[:, 1, hd:hd + 1],
                                   start=(hd == 0), stop=(hd == H1 - 1))
            mm.then_inc(b1_ready, 1)
            pe.wait_ge(l1_const, 5)
            pe.wait_ge(*EX_DD.at(E - 1, "b2 tail"))

            def keys(b, p, u):
                pe.wait_ge(*QA_DVE.at(b, "n0_1"))
                pe.wait_ge(*QC_ACT.at(b - 2, "f3"))
                for s in range(ST):
                    pe.transpose(ps[:, 0, s * P:(s + 1) * P], x1[:, p, s], ident[:])
                for s in range(ST):
                    mm = pe.transpose(ps[:, 0, L + s * P:L + (s + 1) * P], n0[:, s], ident[:])
                mm.then_inc(*QA_PE.step("xT"))
                pe.wait_ge(*QA_DVE.at(b, "x0T"))
                pe.wait_ge(*QA_ACT.at(b - 1, "v3"))
                for x, name, bank in ((1, "k", 2), (0, "q", 1)):
                    for g in range(G1):
                        mm = pe.matmul(ps[:, bank, g * L:(g + 1) * L], qkw[:, x, g], x0T[:], start=True,
                                       stop=True)
                    mm.then_inc(*QA_PE.step(name))
                for n in range(4):
                    s, half = n // 2, n % 2
                    pe.wait_ge(*QA_ACT.at(b, ("k1", "q1", "v0", "v1")[n]))
                    pe.matmul(ps[:, 2 - n % 2], x1T[:, p, s * P:(s + 1) * P],
                              vw[:, 4 * half:4 * half + 4].rearrange("p h d -> p (h d)"), start=True,
                              stop=True).then_inc(*QA_PE.step(f"v{n}"))

            def outputs(b, p, u):
                pe.wait_ge(*QA_DVE.at(b, "q13"))
                for n in range(6):
                    g, m = n // 3, n % 3
                    pe.wait_ge(*(QB_DVE.at(b - 1, f"s{n + 4}") if n < 2 else QB_DVE.at(b, f"s{n - 2}")))
                    if m < 2:
                        rhs, key = q_bd1[:, p, g, 2 * m:2 * m + 2], k_T1[:, p, g, 0:P]
                    else:
                        rhs, key = q_bd1[:, p, g, :, P:L], k_T1[:, p, g, P:L]
                    pe.matmul(ps[:, 3 + n % 2].rearrange("p (h l) -> p h l", h=rhs.shape[1]), key, rhs,
                              start=True, stop=True).then_inc(*QB_PE.step(f"s{n}"))
                pe.wait_ge(*QA_ACT.at(b, "v3"))
                pe.wait_ge(*QB_DVE.at(b, "s5"))
                for n, (s, hs) in enumerate(OUTS):
                    if n >= 2:
                        pe.wait_ge(*QB_DVE.at(b, f"o{n - 2}{len(OUTS[n - 2][1]) - 1}"))
                    for i, hd in enumerate(hs):
                        dst = ps[:, 5 + n % 2, (D + 1) * i:(D + 1) * (i + 1)]
                        mm = pe.matmul(dst, s_T0[:, hd, s * P:(s + 1) * P], v1[:, p, 0, hd, 0:D + 1],
                                       start=True, stop=(s == 0))
                        if s:
                            mm = pe.matmul(dst, s_T1[:, hd], v1[:, p, 1, hd, 0:D + 1], start=False, stop=True)
                    mm.then_inc(*QB_PE.step(f"o{n}"))

            def after(b, p, u):
                pe.wait_ge(*QB_DVE.at(b, "n1"))
                pe.wait_ge(*QC_DVE.at(b - 1, "counts"))
                if not isinstance(b, int) or b + 1 < B:
                    pe.wait_ge(*QA_DVE.at(b + 1, "x0T"))
                for n in range(4):
                    if n >= 2:
                        pe.wait_ge(*QC_DVE.at(b, f"y{2 * (n - 2) + 1}"))
                    for i in range(2):
                        for s in range(ST):
                            mm = pe.transpose(ps[:, (7, 0)[n % 2], i * L + s * P:i * L + (s + 1) * P],
                                              on[:, s, 2 * n + i], ident[:])
                    mm.then_inc(*QC_PE.step(f"y{n}"))
                for n in range(4):
                    pe.wait_ge(*(QC_DVE.at(b, "y7") if n < 2 else QC_ACT.at(b, f"f{n - 2}")))
                    for hd in range(H1):
                        mm = pe.matmul(ps[:, (7, 0)[n % 2], 0:L], w1[:, hd, n * P:(n + 1) * P], yT[:, hd],
                                       start=(hd == 0), stop=(hd == H1 - 1))
                    mm.then_inc(*QC_PE.step(f"f{n}"))
                pe.wait_ge(*QC_ACT.at(b, "f3"))
                for s in range(ST):
                    for f in range(F1 // P):
                        mm = pe.matmul(ps[:, 7, s * P:(s + 1) * P], h1T[:, f, s * P:(s + 1) * P], w2[:, f],
                                       start=(f == 0), stop=(f == F1 // P - 1))
                mm.then_inc(*QC_PE.step("out"))
                route_pe(pe, QC_PE, QC_DVE, QC_POOL, b, p, wr2)

            skewed(pe, [(outputs, 1), (keys, 0), (after, 1)], B)

        N_SENT2 = 16 * ST * K * B // 2
        N_TABLE = 15

        @block.gpsimd
        def _(pool):
            pool.iota(t_no_i[:], [[1, TILES2]], base=0, channel_multiplier=0).then_inc(table, 1)

            def send(t, p, u):
                pool.wait_ge(*FD_DVE.at(t, "dst"))
                held(pool, held_pool, t)
                pool.indirect_dma_start(
                    out=y2, out_offset=bass.IndirectOffsetOnAxis(ap=dst2_u[:, p, 0:1], axis=0),
                    in_=yo[:, p], in_offset=None, bounds_check=K * N - 1, oob_is_err=False,
                ).then_inc(scattered_y2[p], 16)
                pool.wait_ge(scattered_y2[p], 16 * (u + 1))
                pool.sem_inc(*FD_POOL.step("sent"))

            skewed(pool, [(send, 2)], TILES2)

        @block.vector
        def _(dve):
            n = [1]

            def then(ins):
                n[0] += 1
                ins.then_inc(table, 1)
                dve.wait_ge(table, n[0])

            dve.wait_ge(*QC_DVE.at(B - 1, "gate"))
            dve.wait_ge(table, 1)
            then(dve.tensor_copy(t_no[:, :, 0], t_no_i[:]))
            then(dve.tensor_scalar(n_tiles[:, 0], counts[0:1, 1], float(P - 1), None, ALU.add))
            then(dve.tensor_copy(n_i[:], n_tiles[:, 0]))
            then(dve.tensor_scalar(n_i[:], n_i[:], 7, None, ALU.arith_shift_right))
            then(dve.tensor_copy(n_tiles[:, 0], n_i[:]))
            then(dve.memset(t_start[:], 0.0))
            then(dve.tensor_tensor_scan(ends[:, 0], n_tiles[:, 0], t_start[:, 0:E], 0.0, ALU.add, ALU.add))
            then(dve.tensor_tensor(t_past[:], t_no[:].broadcast_to([1, TILES2, E - 1]),
                                   ends[:, :, 0:E - 1].broadcast_to([1, TILES2, E - 1]), ALU.is_ge))
            then(dve.tensor_reduce(t_e[:], t_past[:], AX, ALU.add))
            then(dve.tensor_tensor(t_past[:], t_past[:], n_tiles[:, :, 0:E - 1].broadcast_to([1, TILES2, E - 1]),
                                   ALU.mult))
            then(dve.tensor_reduce(t_start[:], t_past[:], AX, ALU.add))
            then(dve.tensor_copy(tab_e[:], t_e[:]))
            then(dve.scalar_tensor_tensor(t_row[:], t_e[:], float(REG // P), t_start[:], ALU.mult, ALU.subtract))
            then(dve.tensor_tensor(t_row[:], t_row[:], t_no[:, :, 0], ALU.add))
            then(dve.tensor_scalar(tab_row[:], t_row[:], float(P), None, ALU.mult))

            def turn(t, p, u):
                dve.wait_ge(*FU_PE.at(t - 2, "gu"))
                dve.wait_ge(*FT_PE.at(t, "xT"))
                dve.tensor_copy(xtT[:, p], ps[:, p, 0:P]).then_inc(*FT_DVE.step("xT"))
                dve.tensor_copy(meta[:, bass.ds(t, 1), :], xt[:, p:p + 1, D:]).then_inc(*FT_DVE.step("meta"))

            def up(t, p, u):
                dve.wait_ge(*FH_PE.at(t - 2, "guT"))
                dve.wait_ge(*FU_ACT.at(t, "silu"))
                dve.tensor_tensor(gu[:, p], ps[:, 2 + p, HE:], silu[:, p], ALU.mult)\
                   .then_inc(*FU_DVE.step("gu"))

            def down(t, p, u):
                dve.wait_ge(*FD_POOL.at(t - 2, "sent"))
                dve.wait_ge(*FT_DVE.at(t, "meta"))
                dve.wait_ge(*FD_PE.at(t, "out"))
                dve.tensor_tensor(yo[:, p:p + 1], ps[:, 6 + p:7 + p, 0:D],
                                  meta[:, bass.ds(t, 1), 1:2].broadcast_to([P, 1, D]), ALU.mult)\
                   .then_inc(*FD_DVE.step("y"))
                dve.tensor_scalar(dst2_u[:, p:p + 1, :], meta[:, bass.ds(t, 1), 0:1], float(K * N), None,
                                  ALU.add).then_inc(*FD_DVE.step("dst"))

            skewed(dve, [(turn, 0), (up, 1), (down, 2)], TILES2)

        @block.sync
        def _(sp):
            sp.wait_ge(table, N_TABLE + 1)
            for q in range(2):
                sp.wait_ge(scattered2[q], N_SENT2)

            def load(t, p, u):
                sp.wait_ge(*FT_DVE.at(t - 2, "meta"))
                row = sp.value_load(tab_row[0:1, bass.ds(t, 1)], min_val=0, max_val=E * REG + SPARE - P)
                sp.dma_start(xt[:, p], xe2[bass.ds(row, P), :]).then_inc(ld_xt[p], 16)

            skewed(sp, [(load, 0)], TILES2)

        @block.scalar
        def _(act):
            def up(t, p, u):
                act.wait_ge(*FU_DVE.at(t - 2, "gu"))
                act.wait_ge(*FU_PE.at(t, "gu"))
                act.activation(silu[:, p], ps[:, 2 + p, 0:HE], ACT.Silu).then_inc(*FU_ACT.step("silu"))

            def turn(t, p, u):
                act.wait_ge(*FD_PE.at(t - 2, "out"))
                act.wait_ge(*FH_PE.at(t, "guT"))
                act.activation(guT[:, p].rearrange("p c t -> p (c t)"), ps[:, 4 + p, 0:HE], ACT.Identity)\
                   .then_inc(*FH_ACT.step("guT"))

            skewed(act, [(turn, 2), (up, 1)], TILES2)

        @block.tensor
        def _(pe):
            pe.wait_ge(table, N_TABLE + 1)
            pe.wait_ge(*QC_DVE.at(B - 1, "gate"))

            def turn(t, p, u):
                pe.wait_ge(ld_xt[p], 16 * (u + 1))
                pe.wait_ge(*FT_DVE.at(t - 2, "xT"))
                pe.transpose(ps[:, p, 0:P], xt[:, p, 0:D], ident[:]).then_inc(*FT_PE.step("xT"))

            def up(t, p, u):
                e = pe.value_load(tab_e[0:1, bass.ds(t, 1)], min_val=0, max_val=E - 1)
                pe.wait_ge(*FT_DVE.at(t, "xT"))
                pe.wait_ge(*FU_DVE.at(t - 2, "gu"))
                pe.matmul(ps[:, 2 + p], xtT[:, p], wgu[:, bass.ds(e, 1)].rearrange("p e f -> p (e f)"),
                          start=True, stop=True).then_inc(*FU_PE.step("gu"))

            def turn_gu(t, p, u):
                pe.wait_ge(*FU_DVE.at(t, "gu"))
                pe.wait_ge(*FH_ACT.at(t - 2, "guT"))
                for c in range(HT):
                    mm = pe.transpose(ps[:, 4 + p, c * P:(c + 1) * P], gu[:, p, c * P:(c + 1) * P], ident[:])
                mm.then_inc(*FH_PE.step("guT"))

            def down(t, p, u):
                e = pe.value_load(tab_e[0:1, bass.ds(t, 1)], min_val=0, max_val=E - 1)
                pe.wait_ge(*FH_ACT.at(t, "guT"))
                pe.wait_ge(*FD_DVE.at(t - 2, "y"))
                for c in range(HT):
                    mm = pe.matmul(ps[:, 6 + p, 0:D], guT[:, p, c],
                                   wd[:, bass.ds(e, 1), c].rearrange("p e d -> p (e d)"), start=(c == 0),
                                   stop=(c == HT - 1))
                mm.then_inc(*FD_PE.step("out"))

            skewed(pe, [(turn, 0), (turn_gu, 2), (up, 1), (down, 2)], TILES2)

        @block.sync
        def _(sp):
            for q in range(2):
                sp.wait_ge(scattered_y2[q], 16 * TILES2 // 2)
            for c in range(NT // CH):
                if c >= 2:
                    sp.wait_ge(summed, 2 * (c - 1))
                for k in range(K):
                    sp.dma_start(y_in[:, c % 2, k], y2.rearrange("(k c t p) d -> k c p t d", k=K, t=CH, p=P)[k, c])\
                      .then_inc(ld_y2[c % 2], 16)
            for c in range(NT // CH):
                sp.wait_ge(summed, 2 * (c + 1))
                sp.dma_start(out.rearrange("(c t p) d -> c p t d", t=CH, p=P)[c], h[:, c * CH:(c + 1) * CH])\
                  .then_inc(stored, 16)
            sp.wait_ge(stored, 16 * (NT // CH))

        @block.vector
        def _(dve):
            for c in range(NT // CH):
                dve.wait_ge(ld_y2[c % 2], 32 * (c // 2 + 1))
                for k in range(K):
                    rows = h[:, c * CH:(c + 1) * CH]
                    dve.tensor_tensor(rows, y_in[:, c % 2, k], rows, ALU.add).then_inc(summed, 1)
                    dve.wait_ge(summed, 2 * c + k + 1)

def kernel(**inputs):
    import concourse.bacc as bacc
    from concourse.bass_utils import run_bass_kernel_spmd

    arrays = layouts({k: np.asarray(v) for k, v in inputs.items()})
    nc = bacc.Bacc("TRN2", target_bir_lowering=False, num_devices=1)
    aps = {n: nc.dram_tensor(f"in_{n}", v.shape, mybir.dt.from_np(v.dtype), kind="ExternalInput").ap()
           for n, v in arrays.items()}
    out = nc.dram_tensor("out", [N, D], F32, kind="ExternalOutput").ap()
    lm_tower(nc, aps, out)
    r = run_bass_kernel_spmd(nc, [{f"in_{n}": v for n, v in arrays.items()}], core_ids=[0])
    return r.results[0]["out"].reshape(B, L, D)
```

```python
from contextlib import ExitStack

import numpy as np

import concourse.bass as bass
from concourse import mybir

F32 = mybir.dt.float32
F32R = mybir.dt.float32r
BF16 = mybir.dt.bfloat16
I32 = mybir.dt.int32
U32 = mybir.dt.uint32
ALU = mybir.AluOpType
ACT = mybir.ActivationFunctionType
AX = mybir.AxisListType.X

P = 128
B, L, D = 8, 256, 128
N = B * L
ST = L // P
NT = N // P
VOCAB = 50257
H0, C0 = 8, 16
G0 = 4
E, K = 8, 2
F0 = 512
CAP = 640
FT = F0 // P
CT = CAP // P
H1, A1 = 8, 32
G1 = 2
F1 = 512
HE = 256
HT = HE // P
REG = N
TILES2 = N * K // P + E
SPARE = TILES2 * P - 2 * REG
XW = D + 2
EPS = 1e-5
BIG = 1.0e6


class Steps:

    def __init__(self, sem, names, ahead=3):
        self.sem, self.names, self.ahead, self.next = sem, list(names), ahead, 0

    def step(self, name):
        assert self.names[self.next] == name, (self.names[self.next], name)
        self.next = (self.next + 1) % len(self.names)
        return self.sem, 1

    def at(self, rnd, name):
        return self.sem, len(self.names) * (rnd + self.ahead) + self.names.index(name) + 1

    def start(self, eng):
        eng.sem_inc(self.sem, len(self.names) * self.ahead)


def held(eng, sem, rnd):
    if not isinstance(rnd, int):
        eng.sem_inc(sem, 1)


def skewed(eng, stages, rounds):
    most = max(lag for _, lag in stages)
    first = most + most % 2
    turns = (rounds - first) // 2

    def time(t, j=None):
        for stage, lag in stages:
            p = (t - lag) % 2
            if j is None:
                if 0 <= t - lag < rounds:
                    stage(t - lag, p, (t - lag) // 2)
            else:
                stage(j * 2 + (t - lag), p, j + (t - lag) // 2)

    for t in range(first):
        time(t)
    with eng.Fori(0, turns) as j:
        time(first, j)
        time(first + 1, j)
    for t in range(first + 2 * turns, rounds + most):
        time(t)


def layouts(i):
    def c(x):
        return np.ascontiguousarray(x)

    return {
        "ids": c(i["x"].reshape(NT, P).T),
        "embed": c(i["L0_tok_embed_matrix"]),
        "wqkv": c(i["L0_attn_qkv_w"].reshape(H0, 3, C0, D).transpose(3, 1, 0, 2).reshape(D, 3 * D)),
        "bqkv": c(i["L0_attn_qkv_b"].reshape(H0, 3, C0).transpose(1, 0, 2).reshape(1, 3 * D)),
        "bv": c(i["L0_attn_qkv_b"].reshape(H0, 3, C0)[:, 2].reshape(D)),
        "wo": c(i["L0_attn_out_w"].T),
        "bo": c(i["L0_attn_out_b"]),
        "wr1": c(i["L0_ffn_Wr"]),
        "br": c(i["L0_ffn_br"]),
        "w1e": c(i["L0_ffn_W1"]),
        "b1e": c(i["L0_ffn_b1"].reshape(E, FT, P).transpose(0, 2, 1)),
        "w2e": c(i["L0_ffn_W2"].reshape(E, FT, P, D).transpose(0, 2, 1, 3)),
        "b2e": c(i["L0_ffn_b2"]),
        "ln0_w": c(i["L1_attn_ln0_w"].reshape(D, 1)),
        "ln0_b": c(i["L1_attn_ln0_b"].reshape(D, 1)),
        "ln1_w": c(i["L1_attn_ln1_w"]),
        "ln1_b": c(i["L1_attn_ln1_b"]),
        "qw": c(i["L1_attn_qw"].reshape(D, A1, H1).transpose(0, 2, 1).reshape(D, A1 * H1)),
        "kw": c(i["L1_attn_kw"].reshape(D, A1, H1).transpose(0, 2, 1).reshape(D, A1 * H1)),
        "qb": c(i["L1_attn_qb"].reshape(A1, H1).T.reshape(G1, P).T),
        "kb": c(i["L1_attn_kb"].reshape(A1, H1).T.reshape(G1, P).T),
        "vw": c(i["L1_attn_vw"].reshape(D, D, H1).transpose(0, 2, 1).reshape(D, H1 * D)),
        "vb": c(i["L1_attn_vb"].reshape(D, H1).T.reshape(H1 * D)),
        "w1": c(i["L1_attn_w1"].reshape(D, H1, F1)),
        "b1": c(i["L1_attn_b1"].reshape(F1 // P, P).T),
        "w2": c(i["L1_attn_w2"].reshape(F1 // P, P, D).transpose(1, 0, 2)),
        "b2": c(i["L1_attn_b2"]),
        "wr2": c(i["L1_ffn_router_w"].T),
        "wgu": c(np.concatenate([i["L1_ffn_w_gate"], i["L1_ffn_w_up"]], axis=2).transpose(1, 0, 2)),
        "wd": c(i["L1_ffn_w_down"].reshape(E, HT, P, D).transpose(2, 0, 1, 3)),
    }


def lm_tower(nc, a, out):
    with ExitStack() as ctx:
        def sb(name, shape, dt=F32):
            return ctx.enter_context(nc.sbuf_tensor(name, shape, dt))

        def sem(name):
            return ctx.enter_context(nc.semaphore(name))

        def dram(name, shape):
            return nc.dram_tensor(name, shape, F32, kind="Internal").ap()

        def steps(name, names):
            return Steps(sem(name), names)

        xe1 = dram("xe1", [E * CAP, XW])
        y1 = dram("y1", [K * N, D])
        xe2 = dram("xe2", [E * REG + SPARE, XW])
        y2 = dram("y2", [K * N, D])

        ps = ctx.enter_context(nc.psum_tensor("ps", [P, 8, 512], F32))

        ident = sb("ident", [P, P])
        before = sb("before", [P, P], BF16)
        ones_bf = sb("ones_bf", [P, P], BF16)
        causal = sb("causal", [P, P])
        zeros = sb("zeros", [P, 2048])
        half_neg = sb("half_neg", [P, 2])
        eps = sb("eps", [P, 2])
        iota_i = sb("iota_i", [P, 64], I32)
        expert_no = sb("expert_no", [P, E])
        slot_base1 = sb("slot_base1", [P, 1, E])
        slot_base2 = sb("slot_base2", [P, 1, E])
        row_id = sb("row_id", [P, NT, K])
        lo_rows = sb("lo_rows", [P, 2])
        tiny = sb("tiny", [P, 8], I32)

        h = sb("h", [P, NT, D])

        ids = sb("ids", [P, NT], I32)
        wqkv = sb("wqkv", [P, 3, H0, C0])
        bqkv = sb("bqkv", [1, 3, H0, C0])
        w_rep = sb("w_rep", [P, 2, G0, P])
        b_rep = sb("b_rep", [1, 2, G0, P])
        one = sb("one", [1, 1])
        bias_qk = sb("bias_qk", [P, 2, G0])
        bias_lo = sb("bias_lo", [P, 2, G0])
        wo = sb("wo", [P, D])
        bv_bc = sb("bv_bc", [P, D])
        bo_bc = sb("bo_bc", [P, D])
        stats_b = sb("stats_b", [P, ST, 6])
        mv_b = sb("mv_b", [P, ST, 2])
        rstd_b = sb("rstd_b", [P, ST])

        wr1 = sb("wr1", [P, E])
        br_bc = sb("br_bc", [P, E])
        xs = sb("xs", [P, 2, ST, K, XW])
        xsT = sb("xsT", [P, L])
        lg = sb("lg", [P, ST, E])
        top8 = sb("top8", [P, ST, 8])
        idx8 = sb("idx8", [P, ST, 8], U32)
        idx_f = sb("idx_f", [P, ST, K])
        neg_top = sb("neg_top", [P, ST])
        e_all = sb("e_all", [P, ST, E])
        z_all = sb("z_all", [P, ST])
        e_top = sb("e_top", [P, ST, K])
        kept = sb("kept", [P, ST, K])
        psum_k = sb("psum_k", [P, ST])
        kept_sum = sb("kept_sum", [P, ST])
        rk = sb("rk", [P, ST])
        onehot = sb("onehot", [P, ST, K, E])
        chosen = sb("chosen", [P, ST, E], BF16)
        counts = sb("counts", [P, 2, E])
        pos = sb("pos", [P, ST, E])
        over = sb("over", [P, ST, E])
        picked = sb("picked", [P, ST, K, E])
        slot = sb("slot", [P, ST, K])
        keep = sb("keep", [P, ST, K])
        slot_u = sb("slot_u", [P, 2, ST, K], U32)


        ln0 = sb("ln0", [P, 2])
        ln1 = sb("ln1", [P, 2, H1])
        qkw = sb("qkw", [P, 2, G1, P])
        qkb = sb("qkb", [P, 2, G1])
        vw = sb("vw", [P, H1, D])
        vb_bc = sb("vb_bc", [P, H1, D])
        w1 = sb("w1", [P, H1, F1])
        b1 = sb("b1", [P, F1 // P])
        b1_all = sb("b1_all", [P, F1 // P])
        w2 = sb("w2", [P, F1 // P, D])
        b2_bc = sb("b2_bc", [P, D])
        wr2 = sb("wr2", [P, E])
        mask = sb("mask", [P, L])

        wgu = sb("wgu", [P, E, 2 * HE])
        wd = sb("wd", [P, E, HT, D])
        n_i = sb("n_i", [1, E], I32)
        n_tiles = sb("n_tiles", [1, 1, E])
        ends = sb("ends", [1, 1, E])
        t_no = sb("t_no", [1, TILES2, 1])
        t_no_i = sb("t_no_i", [1, TILES2], I32)
        t_past = sb("t_past", [1, TILES2, E - 1])
        t_e = sb("t_e", [1, TILES2])
        t_start = sb("t_start", [1, TILES2])
        t_row = sb("t_row", [1, TILES2])
        tab_e = sb("tab_e", [1, TILES2], I32)
        tab_row = sb("tab_row", [1, TILES2], I32)

        layer0 = ExitStack()

        def sb0(name, shape, dt=F32):
            return layer0.enter_context(nc.sbuf_tensor(name, shape, dt))

        ids_s = sb0("ids_s", [P, 2, ST], I32)
        emb = sb0("emb", [P, 2, ST, D])
        stats = sb0("stats", [P, ST, 6])
        mv = sb0("mv", [P, ST, 2])
        rstd = sb0("rstd", [P, ST])
        xn = sb0("xn", [P, 2, ST, D])
        xT = sb0("xT", [P, 2, L])
        hi_t = sb0("hi_t", [P, 2 * G0, L], F32R)
        q_bd = sb0("q_bd", [P, 2, G0, 2, L], F32R)
        k_op = sb0("k_op", [P, 2, G0, L], F32R)
        v_ext = sb0("v_ext", [P, 2, ST, H0, 32])
        mx = sb0("mx", [P, 2, ST, G0, 2])
        m_sel = sb0("m_sel", [P, ST, G0, P])
        pT = sb0("pT", [P, G0, ST, 2, L])
        pv_sb = sb0("pv_sb", [P, 2, L])
        rden = sb0("rden", [P, ST, H0, 1])
        cn = sb0("cn", [P, ST, H0, C0])
        cT = sb0("cT", [P, L])
        w1e = sb0("w1e", [P, 2, F0])
        w2e = sb0("w2e", [P, 2, FT, D])
        b2e = sb0("b2e", [P, 2, D])
        b1e = sb0("b1e", [P, 2, FT])
        xe = sb0("xe", [P, 2, CT, XW])
        xeT = sb0("xeT", [P, 2, CAP])
        hT = sb0("hT", [P, 2, FT, CAP])
        yb = sb0("yb", [P, CT, D])
        ye = sb0("ye", [P, 2, CT, D])
        dst_u = sb0("dst_u", [P, 2, CT], U32)
        layer0.close()

        CH = 4
        yy = sb("yy", [P, 2, K, ST, D])
        stats_a = sb("stats_a", [P, ST, 6])
        mv_a = sb("mv_a", [P, ST, 2])
        rstd_a = sb("rstd_a", [P, ST])
        x1 = sb("x1", [P, 2, ST, D])
        n0 = sb("n0", [P, ST, D])
        x1T = sb("x1T", [P, 2, L])
        x0T = sb("x0T", [P, L])
        exp_q = sb("exp_q", [P, G1, L])
        exp_k = sb("exp_k", [P, G1, L])
        q_bd1 = sb("q_bd1", [P, 2, G1, 4, L])
        k_T1 = sb("k_T1", [P, 2, G1, L])
        v1 = sb("v1", [P, 2, ST, H1, D + 2])
        s_T0 = sb("s_T0", [P, H1, L])
        s_T1 = sb("s_T1", [P, H1, P])
        r_den = sb("r_den", [P, 6, 3])
        o = sb("o", [P, ST, H1 * D])
        stats_o = sb("stats_o", [P, ST, 2, 6])
        mv_o = sb("mv_o", [P, ST, 2])
        rstd_o = sb("rstd_o", [P, ST])
        on = sb("on", [P, ST, H1, D])
        yT = sb("yT", [P, H1, L])
        h1T = sb("h1T", [P, F1 // P, L])
        att = sb("att", [P, ST, D])
        xt = sb("xt", [P, 2, XW])
        xtT = sb("xtT", [P, 2, P])
        meta = sb("meta", [P, TILES2, 2])
        silu = sb("silu", [P, 2, HE])
        gu = sb("gu", [P, 2, HE])
        guT = sb("guT", [P, 2, HT, P])
        yo = sb("yo", [P, 2, D])
        dst2_u = sb("dst2_u", [P, 2, 1], U32)
        y_in = sb("y_in", [P, 2, K, CH, D])

        ld_const = sem("ld_const")
        ld_ids = sem("ld_ids")
        ld_w0 = sem("ld_w0")
        pool_const = sem("pool_const")
        dve_const = sem("dve_const")
        bias_ready = sem("bias_ready")
        zeroed = sem("zeroed")
        held_pool = sem("held_pool")
        held_dve = sem("held_dve")

        embedded = [sem("embedded0"), sem("embedded1")]
        scattered1 = [sem("scattered1_0"), sem("scattered1_1")]
        PG_POOL = steps("pg_pool", ["ids"])
        PA_POOL = steps("pa_pool", ["rstd eps", "rstd", "residual"])
        PA_DVE = steps("pa_dve", ["stats0", "stats1", "mean0", "mean1", "xn0", "xn1", "xT"]
                       + [f"k{g}" for g in range(G0)] + [f"q{g}{x}" for g in range(G0) for x in "ab"]
                       + ["v"] + [f"max{g}" for g in range(G0)] + ["max hi", "max lo"])
        PA_ACT = steps("pa_act", [f"hi k{g}" for g in range(G0)] + [f"hi q{g}" for g in range(G0)])
        PA_PE = steps("pa_pe", ["xT"] + [f"k{g}" for g in range(G0)] + [f"q{g}" for g in range(G0)]
                      + ["v"] + [f"scores{g}" for g in range(G0)])
        PB_DVE = steps("pb_dve", ["q0", "q1", "rden", "cn"])
        PB_ACT = steps("pb_act", [f"exp{g}" for g in range(G0)] + ["pv", "cT"])
        PB_PE = steps("pb_pe", ["maxT"] + [f"scores{g}" for g in range(G0)] + ["pv", "ct", "cT", "out"])
        PR_DVE = steps("pr_dve", ["residual", "stats0", "stats1", "mean0", "mean1", "xs0", "xs1", "xsT", "logits",
                                  "top0", "top1", "idx0", "idx1", "idx f", "neg top", "pos", "counts"])
        PR_ACT = steps("pr_act", ["z0", "z1", "top0", "top1"])
        PR_PE = steps("pr_pe", ["xsT", "logits", "pos"])
        PR_POOL = steps("pr_pool", ["rstd eps", "rstd"] + [f"onehot{i}" for i in range(4)]
                        + ["chosen", "over", "pos base", "pos over", "picked0", "picked1", "row ids"])
        PF_DVE = steps("pf_dve", ["pair", "slot", "pair eps", "keep", "slot u", "kept", "kept sum", "kept eps",
                                  "rkept", "gate"])
        PF_POOL = steps("pf_pool", ["sent"])

        ld_xe = [sem("ld_xe0"), sem("ld_xe1")]
        ld_we = [sem("ld_we0"), sem("ld_we1")]
        scattered_y1 = [sem("scattered_y1_0"), sem("scattered_y1_1")]
        EX_T = steps("ex_t", ["xT", "xT tail"])
        EX_U = steps("ex_u", [f"up{u}" for u in range(2 * FT)])
        EX_D = steps("ex_d", ["down", "down tail"])
        EX_TD = steps("ex_td", ["xT", "xT tail"])
        EX_UA = steps("ex_ua", [f"gelu{u}" for u in range(2 * FT)])
        EX_DD = steps("ex_dd", ["b2", "b2 tail", "weighted", "dst"])
        EX_POOL = steps("ex_pool", ["sent"])

        ld_w1 = sem("ld_w1")
        ld_yy = [sem("ld_yy0"), sem("ld_yy1")]
        scattered2 = [sem("scattered2_0"), sem("scattered2_1")]
        l1_const = sem("l1_const")
        b1_ready = sem("b1_ready")
        QA_DVE = steps("qa_dve", ["add", "h2", "stats0", "stats1", "mean0", "mean1", "x1_0", "x1_1", "n stats0",
                                  "n stats1", "n mean0", "n mean1", "n0_0", "n0_1", "x1T", "x0T", "k0", "k1"]
                       + [f"q{g}{q}" for g in range(G1) for q in range(4)])
        QA_POOL = steps("qa_pool", ["rstd eps", "rstd", "h x1", "n rstd eps", "n rstd"])
        QA_PE = steps("qa_pe", ["xT", "k", "q"] + [f"v{n}" for n in range(4)])
        QA_ACT = steps("qa_act", ["k0", "k1", "q0", "q1"] + [f"v{n}" for n in range(4)])
        OUTS = [(s, heads) for s in range(ST) for heads in ((0, 1, 2), (3, 4, 5), (6, 7))]
        QB_PE = steps("qb_pe", [f"s{n}" for n in range(6)] + [f"o{n}" for n in range(6)])
        QB_DVE = steps("qb_dve", [f"s{n}" for n in range(6)]
                       + [x for n, (_, hs) in enumerate(OUTS) for x in [f"r{n}"] + [f"o{n}{i}" for i in range(len(hs))]]
                       + [f"stats{s}{c}" for s in range(ST) for c in range(2)] + ["mean0", "mean1", "n0", "n1"])
        QB_POOL = steps("qb_pool", ["rstd eps", "rstd"])
        QC_PE = steps("qc_pe", [f"y{n}" for n in range(4)] + [f"f{n}" for n in range(4)] + ["out"])
        QC_DVE = steps("qc_dve", [f"y{n}" for n in range(H1)])
        QC_ACT = steps("qc_act", [f"f{n}" for n in range(4)])
        QR_PE = steps("qr_pe", ["xsT", "logits", "pos"])
        QR_DVE = steps("qr_dve", ["b2", "h3", "stats0", "stats1", "mean0", "mean1", "xs0", "xs1", "xsT", "logits",
                                  "top0", "top1", "idx0", "idx1", "idx f", "neg top", "pos", "counts"])
        QR_ACT = steps("qr_act", ["top0", "top1"])
        QR_POOL = steps("qr_pool", ["rstd eps", "rstd"] + [f"onehot{i}" for i in range(4)]
                        + ["chosen", "pos base", "picked0", "picked1", "row ids"])
        QF_DVE = steps("qf_dve", ["pair", "rk", "slot", "slot u", "gate"])
        QF_POOL = steps("qf_pool", ["sent"])

        table = sem("table")
        ld_xt = [sem("ld_xt0"), sem("ld_xt1")]
        scattered_y2 = [sem("scattered_y2_0"), sem("scattered_y2_1")]
        FT_PE = steps("ft_pe", ["xT"])
        FT_DVE = steps("ft_dve", ["xT", "meta"])
        FU_PE = steps("fu_pe", ["gu"])
        FU_ACT = steps("fu_act", ["silu"])
        FU_DVE = steps("fu_dve", ["gu"])
        FH_PE = steps("fh_pe", ["guT"])
        FH_ACT = steps("fh_act", ["guT"])
        FD_PE = steps("fd_pe", ["out"])
        FD_DVE = steps("fd_dve", ["y", "dst"])
        FD_POOL = steps("fd_pool", ["sent"])

        ld_y2 = [sem("ld_y2_0"), sem("ld_y2_1")]
        summed = sem("summed")
        stored = sem("stored")

        block = ctx.enter_context(nc.Block())

        @block.sync
        def _(sp):
            sp.dma_start(ids[:], a["ids"]).then_inc(ld_ids, 16)
            sp.dma_start(wqkv[:].rearrange("p a h c -> p (a h c)"), a["wqkv"]).then_inc(ld_w0, 16)
            sp.dma_start(bqkv[:].rearrange("p a h c -> p (a h c)"), a["bqkv"]).then_inc(ld_w0, 16)
            sp.dma_start(wo[:], a["wo"]).then_inc(ld_w0, 16)
            sp.dma_start(bv_bc[:], a["bv"].partition_broadcast(P)).then_inc(ld_w0, 16)
            sp.dma_start(bo_bc[:], a["bo"].partition_broadcast(P)).then_inc(ld_w0, 16)
            sp.dma_start(wr1[:], a["wr1"]).then_inc(ld_w0, 16)
            sp.dma_start(br_bc[:], a["br"].partition_broadcast(P)).then_inc(ld_w0, 16)
            sp.wait_ge(pool_const, 2)
            for buf in (xe1, y1, xe2):
                flat = buf.rearrange("(p r) x -> p (r x)", p=P)
                width = flat.shape[1]
                for c in range(0, width, 2048):
                    n = min(2048, width - c)
                    sp.dma_start(flat[:, c:c + n], zeros[:, 0:n]).then_inc(zeroed, 16)
        n_zero = sum(-(-buf.shape[0] * buf.shape[1] // P // 2048) for buf in (xe1, y1, xe2))
        N_W0 = 7 * 16

        @block.gpsimd
        def _(pool):
            for s in (PG_POOL, PA_POOL, PR_POOL, PF_POOL, EX_POOL, QA_POOL, QB_POOL, QR_POOL, QF_POOL, FD_POOL):
                s.start(pool)
            pool.memset(ident[:], 0.0).then_inc(pool_const, 1)
            pool.memset(zeros[:], 0.0).then_inc(pool_const, 1)
            pool.wait_ge(pool_const, 2)
            pool.affine_select(out=ident[:], in_=ident[:], compare_op=ALU.not_equal, fill=1.0, base=0,
                               pattern=[[-1, P]], channel_multiplier=1).then_inc(pool_const, 1)
            pool.memset(half_neg[:], -0.5).then_inc(pool_const, 1)
            pool.memset(eps[:], EPS).then_inc(pool_const, 1)
            pool.iota(iota_i[:, 0:E], [[1, E]], base=0, channel_multiplier=0).then_inc(pool_const, 1)
            pool.iota(iota_i[:, 8:16], [[CAP, E]], base=0, channel_multiplier=0).then_inc(pool_const, 1)
            pool.iota(iota_i[:, 16:24], [[REG, E]], base=0, channel_multiplier=0).then_inc(pool_const, 1)
            pool.iota(iota_i[:, 32:64], [[P, NT], [N, K]], base=-K * N,
                      channel_multiplier=1).then_inc(pool_const, 1)
            pool.iota(tiny[:, 0:1], [[0, 1]], base=0, channel_multiplier=1).then_inc(pool_const, 1)
            pool.memset(before[:], 1.0).then_inc(pool_const, 1)
            pool.memset(causal[:], 1.0).then_inc(pool_const, 1)
            pool.wait_ge(pool_const, 12)
            pool.affine_select(out=before[:], in_=before[:], compare_op=ALU.is_gt, fill=0.0, base=0,
                               pattern=[[1, P]], channel_multiplier=-1).then_inc(pool_const, 1)
            pool.affine_select(out=causal[:], in_=causal[:], compare_op=ALU.is_ge, fill=0.0, base=0,
                               pattern=[[1, P]], channel_multiplier=-1).then_inc(pool_const, 1)
            pool.wait_ge(ld_ids, 16)

        POOL_CONSTS = 14

        @block.vector
        def _(dve):
            for s in (PA_DVE, PB_DVE, PR_DVE, PF_DVE, EX_TD, EX_DD, QA_DVE, QB_DVE, QC_DVE, QR_DVE, QF_DVE, FT_DVE, FU_DVE, FD_DVE):
                s.start(dve)
            dve.memset(w_rep[:], 0.0).then_inc(dve_const, 1)
            dve.memset(b_rep[:], 0.0).then_inc(dve_const, 1)
            dve.memset(one[:], 1.0).then_inc(dve_const, 1)
            dve.memset(ones_bf[:], 1.0).then_inc(dve_const, 1)
            dve.memset(v_ext[:], 1.0).then_inc(dve_const, 1)
            dve.memset(m_sel[:], 0.0).then_inc(dve_const, 1)
            dve.memset(counts[:], 0.0).then_inc(dve_const, 1)
            dve.memset(q_bd[:].bitcast(F32), 0.0).then_inc(dve_const, 1)
            dve.wait_ge(pool_const, 10)
            dve.tensor_copy(expert_no[:], iota_i[:, 0:E]).then_inc(dve_const, 1)
            dve.tensor_copy(slot_base1[:, 0], iota_i[:, 8:16]).then_inc(dve_const, 1)
            dve.tensor_copy(slot_base2[:, 0], iota_i[:, 16:24]).then_inc(dve_const, 1)
            dve.tensor_copy(row_id[:].rearrange("p t k -> p (t k)"), iota_i[:, 32:64]).then_inc(dve_const, 1)
            dve.tensor_scalar(tiny[:, 1:2], tiny[:, 0:1], 48, None, ALU.bitwise_and).then_inc(dve_const, 1)
            dve.wait_ge(dve_const, 13)
            dve.tensor_scalar(lo_rows[:, 0:1], tiny[:, 1:2], 32.0, None, ALU.is_equal).then_inc(dve_const, 1)
            dve.tensor_scalar(lo_rows[:, 1:2], tiny[:, 1:2], 16.0, None, ALU.is_equal).then_inc(dve_const, 1)
            dve.wait_ge(ld_w0, N_W0)
            for x in range(2):
                for dst, src in ((w_rep, wqkv), (b_rep, bqkv)):
                    rows = dst[:, x].rearrange("p g (q r) -> p (g q) r", q=2)
                    for r in range(3):
                        dve.tensor_copy(rows[:, :, 16 * r:16 * r + 16], src[:, x]).then_inc(dve_const, 1)
            dve.memset(b_rep[:, 1].rearrange("p g (q r) -> p (g q) r", q=2)[:, :, 48:50], 1.0)\
               .then_inc(dve_const, 1)
            dve.wait_ge(bias_ready, 1)
            dve.tensor_copy(bias_qk[:].rearrange("p x g -> p (x g)"), ps[:, 0, 0:8]).then_inc(dve_const, 1)
            dve.wait_ge(dve_const, 29)
            for x in range(2):
                dve.tensor_scalar(bias_lo[:, x], bias_qk[:, x], lo_rows[:, x:x + 1], None, ALU.mult)\
                   .then_inc(dve_const, 1)

        DVE_CONSTS = 31

        @block.tensor
        def _(pe):
            for s in (PA_PE, PB_PE, PR_PE, EX_T, EX_U, EX_D, QA_PE, QB_PE, QC_PE, QR_PE, FT_PE, FU_PE, FH_PE, FD_PE):
                s.start(pe)
            pe.wait_ge(dve_const, 28)
            for x in range(2):
                for g in range(G0):
                    mm = pe.matmul(ps[:, 0, x * G0 + g:x * G0 + g + 1], b_rep[:, x, g, :], one[:],
                                   start=True, stop=True)
            mm.then_inc(bias_ready, 1)
            pe.wait_ge(pool_const, POOL_CONSTS)

        @block.scalar
        def _(act):
            for s in (PA_ACT, PB_ACT, PR_ACT, EX_UA, QA_ACT, QC_ACT, QR_ACT, FU_ACT, FH_ACT):
                s.start(act)
            act.wait_ge(dve_const, DVE_CONSTS)

        def route(pool, own, dve_steps, b, p, cap, base):
            pool.wait_ge(*dve_steps.at(b, "idx f"))
            held(pool, held_pool, b)
            for s in range(ST):
                for k in range(K):
                    pool.tensor_scalar(onehot[:, s, k], expert_no[:], idx_f[:, s, k:k + 1], None,
                                       ALU.is_equal).then_inc(*own.step(f"onehot{s * K + k}"))
            pool.wait_ge(*own.at(b, "onehot3"))
            pool.tensor_tensor(chosen[:], onehot[:, :, 0], onehot[:, :, 1], ALU.add)\
                .then_inc(*own.step("chosen"))
            pool.wait_ge(*dve_steps.at(b, "pos"))
            if cap is not None:
                held(pool, held_pool, b)
                pool.tensor_scalar(over[:], pos[:], cap, BIG, ALU.is_ge, ALU.mult)\
                    .then_inc(*own.step("over"))
                pool.wait_ge(*own.at(b, "over"))
            pool.tensor_tensor(pos[:], pos[:], base[:].broadcast_to([P, ST, E]), ALU.add)\
                .then_inc(*own.step("pos base"))
            pool.wait_ge(*own.at(b, "pos base"))
            if cap is not None:
                pool.tensor_tensor(pos[:], pos[:], over[:], ALU.add).then_inc(*own.step("pos over"))
                pool.wait_ge(*own.at(b, "pos over"))
            for s in range(ST):
                pool.tensor_tensor(picked[:, s], onehot[:, s],
                                   pos[:, s:s + 1, :].broadcast_to([P, K, E]), ALU.mult)\
                    .then_inc(*own.step(f"picked{s}"))
            pool.tensor_copy(xs[:, p, :, :, D], row_id[:, bass.ds(b * ST, ST), :])\
                .then_inc(*own.step("row ids"))

        def scatter(pool, b, p, u, own, dve_steps, rows, n_rows, done):
            pool.wait_ge(*dve_steps.at(b, "gate"))
            held(pool, held_pool, b)
            for s in range(ST):
                for k in range(K):
                    pool.indirect_dma_start(
                        out=rows, out_offset=bass.IndirectOffsetOnAxis(ap=slot_u[:, p, s, k:k + 1], axis=0),
                        in_=xs[:, p, s, k], in_offset=None, bounds_check=n_rows - 1, oob_is_err=False,
                    ).then_inc(done[p], 16)
            pool.wait_ge(done[p], 16 * ST * K * (u + 1))
            pool.sem_inc(*own.step("sent"))

        def row_stats(dve, own, b, rows):
            for s in range(ST):
                dve.bn_stats(stats_b[:, s], rows[s].rearrange("p a d -> p (a d)"))\
                   .then_inc(*own.step(f"stats{s}"))
            dve.wait_ge(*own.at(b, "stats1"))
            held(dve, held_dve, b)
            for s in range(ST):
                dve.bn_aggr(mv_b[:, s], stats_b[:, s]).then_inc(*own.step(f"mean{s}"))

        def norm_rows(dve, own, pool_steps, send_steps, b, p, rows):
            dve.wait_ge(*pool_steps.at(b, "rstd"))
            dve.wait_ge(*send_steps.at(b - 2, "sent"))
            for s in range(ST):
                dve.tensor_scalar(xs[:, p, s, :, 0:D], rows[s].broadcast_to([P, K, D]), mv_b[:, s, 0:1],
                                  rstd_b[:, s:s + 1], ALU.subtract, ALU.mult)\
                   .then_inc(*own.step(f"xs{s}"))

        def choose(dve, own, b):
            dve.wait_ge(*own.at(b, "logits"))
            held(dve, held_dve, b)
            for s in range(ST):
                dve.max(top8[:, s], lg[:, s]).then_inc(*own.step(f"top{s}"))
            dve.wait_ge(*own.at(b, "top1"))
            held(dve, held_dve, b)
            for s in range(ST):
                dve.max_index(idx8[:, s], top8[:, s], lg[:, s]).then_inc(*own.step(f"idx{s}"))
            dve.wait_ge(*own.at(b, "idx1"))
            dve.tensor_copy(idx_f[:], idx8[:, :, 0:K]).then_inc(*own.step("idx f"))
            dve.tensor_scalar(neg_top[:], top8[:, :, 0], -1.0, None, ALU.mult)\
               .then_inc(*own.step("neg top"))

        def place(dve, own, pe_steps, b, layer, bank):
            dve.wait_ge(*pe_steps.at(b, "pos"))
            o = L + 32
            dve.tensor_tensor(pos[:], ps[:, bank, o:o + ST * E].rearrange("p (s e) -> p s e", s=ST),
                              counts[:, layer:layer + 1].broadcast_to([P, ST, E]), ALU.add)\
               .then_inc(*own.step("pos"))
            dve.wait_ge(*own.at(b, "pos"))
            dve.tensor_tensor(counts[:, layer], ps[:, bank, o + ST * E:o + (ST + 1) * E], counts[:, layer],
                              ALU.add).then_inc(*own.step("counts"))

        def route_turn(pe, own, dve_steps, b, p):
            pe.wait_ge(*dve_steps.at(b, "xs1"))
            for s in range(ST):
                mm = pe.transpose(ps[:, 7, s * P:(s + 1) * P], xs[:, p, s, 0, 0:D], ident[:])
            mm.then_inc(*own.step("xsT"))

        def route_logits(pe, own, dve_steps, b, wr):
            pe.wait_ge(*dve_steps.at(b, "xsT"))
            for s in range(ST):
                mm = pe.matmul(ps[:, 7, L + s * E:L + (s + 1) * E], xsT[:, s * P:(s + 1) * P], wr[:],
                               start=True, stop=True)
            mm.then_inc(*own.step("logits"))

        def route_places(pe, own, pool_steps, b, bank):
            pe.wait_ge(*pool_steps.at(b, "chosen"))
            o = L + 32
            pe.matmul(ps[:, bank, o:o + E], before[:], chosen[:, 0], start=True, stop=True)
            pe.matmul(ps[:, bank, o + E:o + 2 * E], before[:], chosen[:, 1], start=True, stop=False)
            pe.matmul(ps[:, bank, o + E:o + 2 * E], ones_bf[:], chosen[:, 0], start=False, stop=True)
            pe.matmul(ps[:, bank, o + 2 * E:o + 3 * E], ones_bf[:], chosen[:, 0], start=True, stop=False)
            pe.matmul(ps[:, bank, o + 2 * E:o + 3 * E], ones_bf[:], chosen[:, 1], start=False, stop=True)\
              .then_inc(*own.step("pos"))

        @block.gpsimd
        def _(pool):
            def gather(b, p, u):
                pool.wait_ge(*PA_DVE.at(b - 2, "xn1"))
                pool.wait_ge(*PA_POOL.at(b - 2, "residual"))
                pool.tensor_copy(ids_s[:, p], ids[:, bass.ds(b * ST, ST)]).then_inc(*PG_POOL.step("ids"))
                pool.wait_ge(*PG_POOL.at(b, "ids"))
                held(pool, held_pool, b)
                for s in range(ST):
                    pool.indirect_dma_start(
                        out=emb[:, p, s], out_offset=None, in_=a["embed"],
                        in_offset=bass.IndirectOffsetOnAxis(ap=ids_s[:, p, s:s + 1].bitcast(U32), axis=0),
                    ).then_inc(embedded[p], 16)

            def norm_keys(b, p, u):
                pool.wait_ge(*PA_DVE.at(b, "mean1"))
                pool.tensor_tensor(rstd[:], mv[:, :, 1], eps[:], ALU.add).then_inc(*PA_POOL.step("rstd eps"))
                pool.wait_ge(*PA_POOL.at(b, "rstd eps"))
                pool.tensor_tensor(rstd[:], rstd[:], half_neg[:], ALU.pow).then_inc(*PA_POOL.step("rstd"))

            def residual(b, p, u):
                pool.wait_ge(embedded[p], 16 * ST * (u + 1))
                pool.tensor_tensor(h[:, bass.ds(b * ST, ST), :], emb[:, p],
                                   bo_bc[:].unsqueeze(1).broadcast_to([P, ST, D]), ALU.add)\
                    .then_inc(*PA_POOL.step("residual"))

            def norm_route(b, p, u):
                pool.wait_ge(*PR_DVE.at(b, "mean1"))
                pool.tensor_tensor(rstd_b[:], mv_b[:, :, 1], eps[:], ALU.add)\
                    .then_inc(*PR_POOL.step("rstd eps"))
                pool.wait_ge(*PR_POOL.at(b, "rstd eps"))
                pool.tensor_tensor(rstd_b[:], rstd_b[:], half_neg[:], ALU.pow)\
                    .then_inc(*PR_POOL.step("rstd"))

            def rows_of(b, p, u):
                route(pool, PR_POOL, PR_DVE, b, p, float(CAP), slot_base1)

            def send(b, p, u):
                pool.wait_ge(zeroed, 16 * n_zero)
                scatter(pool, b, p, u, PF_POOL, PF_DVE, xe1, E * CAP, scattered1)

            pool.wait_ge(ld_w0, N_W0)
            skewed(pool, [(gather, 0), (norm_keys, 1), (norm_route, 3), (residual, 1), (rows_of, 3), (send, 4)], B)

        @block.vector
        def _(dve):
            def stats_keys(b, p, u):
                dve.wait_ge(embedded[p], 16 * ST * (u + 1))
                for s in range(ST):
                    dve.bn_stats(stats[:, s], emb[:, p, s]).then_inc(*PA_DVE.step(f"stats{s}"))
                dve.wait_ge(*PA_DVE.at(b, "stats1"))
                held(dve, held_dve, b)
                for s in range(ST):
                    dve.bn_aggr(mv[:, s], stats[:, s]).then_inc(*PA_DVE.step(f"mean{s}"))

            def norm_keys(b, p, u):
                dve.wait_ge(*PA_POOL.at(b, "rstd"))
                for s in range(ST):
                    dve.tensor_scalar(xn[:, p, s], emb[:, p, s], mv[:, s, 0:1], rstd[:, s:s + 1],
                                      ALU.subtract, ALU.mult).then_inc(*PA_DVE.step(f"xn{s}"))

            def turned(b, p, u):
                dve.wait_ge(*PA_PE.at(b, "xT"))
                dve.tensor_copy(xT[:, p], ps[:, 0, 0:L]).then_inc(*PA_DVE.step("xT"))

            def keys(b, p, u):
                for g in range(G0):
                    dve.wait_ge(*PA_ACT.at(b, f"hi k{g | 1}"))
                    dve.scalar_tensor_tensor(k_op[:, p, g], ps[:, 1 + g // 2, (g % 2) * L:(g % 2 + 1) * L],
                                             bias_qk[:, 1, g:g + 1], hi_t[:, g].bitcast(F32), ALU.add,
                                             ALU.subtract).then_inc(*PA_DVE.step(f"k{g}"))

            def queries(b, p, u):
                for g in range(G0):
                    dve.wait_ge(*PA_ACT.at(b, f"hi q{g | 1}"))
                    for q in range(2):
                        r = slice(64 * q, 64 * q + 64)
                        dve.scalar_tensor_tensor(
                            q_bd[r, p, g, q], ps[r, 1 + g // 2, (g % 2) * L:(g % 2 + 1) * L],
                            bias_qk[r, 0, g:g + 1], hi_t[r, G0 + g].bitcast(F32), ALU.add, ALU.subtract,
                        ).then_inc(*PA_DVE.step(f"q{g}{'ab'[q]}"))

            def values(b, p, u):
                dve.wait_ge(*PA_PE.at(b, "v"))
                dve.tensor_tensor(v_ext[:, p, :, :, 0:C0],
                                  ps[:, 0, L:2 * L].rearrange("p (s h c) -> p s h c", s=ST, h=H0),
                                  bv_bc[:].rearrange("p (s h c) -> p s h c", s=1, h=H0)
                                  .broadcast_to([P, ST, H0, C0]), ALU.add).then_inc(*PA_DVE.step("v"))

            def maxima(groups):
                def part(b, p, u):
                    for g in groups:
                        dve.wait_ge(*PA_PE.at(b, f"scores{g}"))
                        bank = 3 + 2 * (g % 2)
                        dve.tensor_reduce(mx[:, p, :, g, :],
                                          ps[:, bank:bank + 2].rearrange("p s (q t) -> p s q t", q=2), AX,
                                          ALU.max).then_inc(*PA_DVE.step(f"max{g}"))
                return part

            def less_parts(b, p, u):
                dve.wait_ge(*PB_PE.at(b - 1, "maxT"))
                dve.wait_ge(*PA_DVE.at(b, f"max{G0 - 1}"))
                rows = mx[:, p].rearrange("p s g q -> p (s g q)")
                sel = m_sel[:].rearrange("p s g (q r) -> p (s g q) r", q=2)
                dve.tensor_scalar(sel[:, :, 48].bitcast(F32R), rows, -1.0, None, ALU.mult)\
                   .then_inc(*PA_DVE.step("max hi"))
                dve.wait_ge(*PA_DVE.at(b, "max hi"))
                dve.scalar_tensor_tensor(sel[:, :, 49].bitcast(F32R), rows, -1.0, sel[:, :, 48],
                                         ALU.mult, ALU.subtract).then_inc(*PA_DVE.step("max lo"))

            def less_max(b, p, u):
                dve.wait_ge(*PB_PE.at(b, "maxT"))
                for q in range(2):
                    r = slice(64 * q, 64 * q + 64)
                    dve.tensor_tensor(q_bd[r, p, :, q],
                                      ps[r, 1:3].rearrange("p k (g t) -> p (k g) t", g=2),
                                      q_bd[r, p, :, q].bitcast(F32), ALU.add)\
                       .then_inc(*PB_DVE.step(f"q{q}"))

            def contexts(b, p, u):
                dve.wait_ge(*PB_PE.at(b, "ct"))
                heads = ps[:, 7].rearrange("p (s h c) -> p (s h) c", s=ST, h=H0)
                dve.reciprocal(rden[:].rearrange("p s h c -> p (s h) c"), heads[:, :, C0:C0 + 1])\
                   .then_inc(*PB_DVE.step("rden"))
                dve.wait_ge(*PB_DVE.at(b, "rden"))
                dve.tensor_tensor(cn[:].rearrange("p s h c -> p (s h) c"), heads[:, :, 0:C0],
                                  rden[:].rearrange("p s h c -> p (s h) c").broadcast_to([P, ST * H0, C0]),
                                  ALU.mult).then_inc(*PB_DVE.step("cn"))

            def residual(b, p, u):
                rows = h[:, bass.ds(b * ST, ST), :]
                dve.wait_ge(*PB_PE.at(b, "out"))
                dve.wait_ge(*PA_POOL.at(b, "residual"))
                dve.tensor_tensor(rows, ps[:, 7, L:2 * L].rearrange("p (s d) -> p s d", s=ST), rows, ALU.add)\
                   .then_inc(*PR_DVE.step("residual"))
                dve.wait_ge(*PR_DVE.at(b, "residual"))
                held(dve, held_dve, b)
                row_stats(dve, PR_DVE, b, [h[:, bass.ds(b * ST + s, 1), :] for s in range(ST)])

            def rows_norm(b, p, u):
                norm_rows(dve, PR_DVE, PR_POOL, PF_POOL, b, p, [h[:, bass.ds(b * ST + s, 1), :] for s in range(ST)])

            def rows_turned(b, p, u):
                dve.wait_ge(*PR_PE.at(b, "xsT"))
                dve.tensor_copy(xsT[:], ps[:, 7, 0:L]).then_inc(*PR_DVE.step("xsT"))

            def pick(b, p, u):
                dve.wait_ge(*PR_PE.at(b, "logits"))
                dve.tensor_tensor(lg[:], ps[:, 7, L:L + ST * E].rearrange("p (s e) -> p s e", s=ST),
                                  br_bc[:].unsqueeze(1).broadcast_to([P, ST, E]), ALU.add)\
                   .then_inc(*PR_DVE.step("logits"))
                choose(dve, PR_DVE, b)

            def placed(b, p, u):
                place(dve, PR_DVE, PR_PE, b, 0, 0)

            def finish(b, p, u):
                own = PF_DVE
                dve.wait_ge(*PR_ACT.at(b, "top1"))
                dve.tensor_reduce(psum_k[:], e_top[:], AX, ALU.add).then_inc(*own.step("pair"))
                dve.wait_ge(*PR_POOL.at(b, "row ids"))
                dve.tensor_reduce(slot[:], picked[:], AX, ALU.add).then_inc(*own.step("slot"))
                dve.wait_ge(*own.at(b, "slot"))
                dve.scalar_tensor_tensor(psum_k[:], z_all[:], 1e-9, psum_k[:], ALU.mult, ALU.add)\
                   .then_inc(*own.step("pair eps"))
                dve.tensor_scalar(keep[:], slot[:], BIG / 2, None, ALU.is_lt).then_inc(*own.step("keep"))
                dve.tensor_copy(slot_u[:, p], slot[:]).then_inc(*own.step("slot u"))
                dve.wait_ge(*own.at(b, "keep"))
                dve.tensor_tensor(kept[:], e_top[:], keep[:], ALU.mult).then_inc(*own.step("kept"))
                dve.wait_ge(*own.at(b, "kept"))
                dve.tensor_reduce(kept_sum[:], kept[:], AX, ALU.add).then_inc(*own.step("kept sum"))
                dve.wait_ge(*own.at(b, "kept sum"))
                dve.scalar_tensor_tensor(kept_sum[:], psum_k[:], 1e-9, kept_sum[:], ALU.mult, ALU.add)\
                   .then_inc(*own.step("kept eps"))
                dve.wait_ge(*own.at(b, "kept eps"))
                dve.reciprocal(rk[:], kept_sum[:]).then_inc(*own.step("rkept"))
                dve.wait_ge(*own.at(b, "rkept"))
                dve.tensor_tensor(xs[:, p, :, :, D + 1], kept[:], rk[:].unsqueeze(2).broadcast_to([P, ST, K]),
                                  ALU.mult).then_inc(*own.step("gate"))

            skewed(dve, [(stats_keys, 1), (residual, 3), (less_max, 2), (norm_keys, 1), (rows_norm, 3),
                         (turned, 1), (rows_turned, 3), (finish, 4), (keys, 1), (pick, 3), (queries, 1),
                         (values, 1), (contexts, 2), (maxima((0,)), 1), (placed, 3), (maxima((1, 2, 3)), 1),
                         (less_parts, 1)], B)

        @block.scalar
        def _(act):
            def high(name, x, groups):
                def part(b, p, u):
                    for g in groups:
                        act.wait_ge(*PA_PE.at(b, f"{name}{g | 1}"))
                        act.activation(hi_t[:, (1 - x) * G0 + g],
                                       ps[:, 1 + g // 2, (g % 2) * L:(g % 2 + 1) * L], ACT.Identity,
                                       bias=bias_lo[:, x, g:g + 1], scale=lo_rows[:, x:x + 1])\
                           .then_inc(*PA_ACT.step(f"hi {name}{g}"))
                return part

            def exps(groups):
                def part(b, p, u):
                    for g in groups:
                        act.wait_ge(*PB_PE.at(b, f"scores{g}"))
                        bank = 3 + 2 * (g % 2)
                        act.activation(pT[:, g].rearrange("p s q t -> p (s q t)"),
                                       ps[:, bank:bank + 2].rearrange("p s t -> p (s t)"), ACT.Exp,
                                       scale=float(C0) ** -0.5).then_inc(*PB_ACT.step(f"exp{g}"))
                return part

            def sums(b, p, u):
                act.wait_ge(*PB_PE.at(b, "pv"))
                act.activation(pv_sb[:].rearrange("p g t -> p (g t)"), ps[:, 7], ACT.Identity)\
                   .then_inc(*PB_ACT.step("pv"))

            def contexts(b, p, u):
                act.wait_ge(*PB_PE.at(b, "cT"))
                act.activation(cT[:], ps[:, 7, 0:L], ACT.Identity).then_inc(*PB_ACT.step("cT"))

            def weights(b, p, u):
                act.wait_ge(*PR_DVE.at(b, "neg top"))
                for s in range(ST):
                    act.activation(e_all[:, s], lg[:, s], ACT.Exp, bias=neg_top[:, s:s + 1],
                                   accum_out=z_all[:, s:s + 1]).then_inc(*PR_ACT.step(f"z{s}"))
                for s in range(ST):
                    act.activation(e_top[:, s], top8[:, s, 0:K], ACT.Exp, bias=neg_top[:, s:s + 1])\
                       .then_inc(*PR_ACT.step(f"top{s}"))

            skewed(act, [(exps((0, 1)), 2), (high("k", 1, (0, 1)), 1), (exps((2,)), 2), (high("k", 1, (2, 3)), 1),
                         (exps((3,)), 2), (high("q", 0, range(G0)), 1), (sums, 2), (weights, 3),
                         (contexts, 2)], B)

        @block.tensor
        def _(pe):
            def turn(b, p, u):
                pe.wait_ge(*PA_DVE.at(b, "xn1"))
                for s in range(ST):
                    mm = pe.transpose(ps[:, 0, s * P:(s + 1) * P], xn[:, p, s], ident[:])
                mm.then_inc(*PA_PE.step("xT"))

            def project(name, x, groups):
                def part(b, p, u):
                    if name == "k" and groups[0] == 0:
                        pe.wait_ge(*PA_DVE.at(b, "xT"))
                        pe.wait_ge(*PB_DVE.at(b - 1, "q1"))
                    for g in groups:
                        if name == "q":
                            pe.wait_ge(*PA_DVE.at(b, f"k{g | 1}"))
                        pe.matmul(ps[:, 1 + g // 2, (g % 2) * L:(g % 2 + 1) * L], w_rep[:, x, g], xT[:, p],
                                  start=True, stop=True).then_inc(*PA_PE.step(f"{name}{g}"))
                return part

            def values(b, p, u):
                for s in range(ST):
                    mm = pe.matmul(ps[:, 0, L + s * P:L + (s + 1) * P], xT[:, p, s * P:(s + 1) * P],
                                   wqkv[:, 2].rearrange("p h c -> p (h c)"), start=True, stop=True)
                mm.then_inc(*PA_PE.step("v"))

            def row_scores(groups):
                def part(b, p, u):
                    for g in groups:
                        if g < 2:
                            pe.wait_ge(*PA_DVE.at(b, f"q{g}b"))
                            pe.wait_ge(*PB_ACT.at(b - 1, f"exp{g + 2}"))
                        else:
                            pe.wait_ge(*PA_DVE.at(b, f"max{g - 2}"))
                        for s in range(ST):
                            for q in range(2):
                                mm = pe.matmul(ps[:, 3 + 2 * (g % 2) + s, q * L:(q + 1) * L],
                                               q_bd[:, p, g, q, s * P:(s + 1) * P], k_op[:, p, g],
                                               start=True, stop=True)
                        mm.then_inc(*PA_PE.step(f"scores{g}"))
                return part

            def turn_max(b, p, u):
                pe.wait_ge(*PA_DVE.at(b, "max lo"))
                for g in range(G0):
                    for s in range(ST):
                        mm = pe.transpose(ps[:, 1 + g // 2, (g % 2) * L + s * P:(g % 2) * L + (s + 1) * P],
                                          m_sel[:, s, g], ident[:])
                mm.then_inc(*PB_PE.step("maxT"))

            def scores(groups):
                def part(b, p, u):
                    for g in groups:
                        if g < 2:
                            pe.wait_ge(*PB_DVE.at(b, "q1"))
                        else:
                            pe.wait_ge(*PB_ACT.at(b, f"exp{g - 2}"))
                        for s in range(ST):
                            mm = pe.matmul(ps[:, 3 + 2 * (g % 2) + s], k_op[:, p, g, s * P:(s + 1) * P],
                                           q_bd[:, p, g].rearrange("p q t -> p (q t)"), start=True, stop=True)
                        mm.then_inc(*PB_PE.step(f"scores{g}"))
                return part

            def weigh(b, p, u):
                pe.wait_ge(*PB_ACT.at(b, "exp3"))
                pe.wait_ge(*PR_DVE.at(b - 1, "logits"))
                for hd in range(H0):
                    j = hd % 4
                    for s in range(ST):
                        mm = pe.matmul(ps[32 * j:32 * j + 32, 7, (hd // 4) * L:(hd // 4 + 1) * L],
                                       v_ext[:, p, s, hd], pT[:, hd // 2, s, hd % 2], start=(s == 0),
                                       stop=(s == ST - 1))
                mm.then_inc(*PB_PE.step("pv"))

            def turn_sums(b, p, u):
                pe.wait_ge(*PB_ACT.at(b, "pv"))
                for s in range(ST):
                    for g in range(2):
                        mm = pe.transpose(ps[:, 7, s * L + g * P:s * L + (g + 1) * P],
                                          pv_sb[:, g, s * P:(s + 1) * P], ident[:])
                mm.then_inc(*PB_PE.step("ct"))

            def turn_contexts(b, p, u):
                pe.wait_ge(*PB_DVE.at(b, "cn"))
                for s in range(ST):
                    mm = pe.transpose(ps[:, 7, s * P:(s + 1) * P], cn[:, s].rearrange("p h c -> p (h c)"),
                                      ident[:])
                mm.then_inc(*PB_PE.step("cT"))

            def outputs(b, p, u):
                pe.wait_ge(*PB_ACT.at(b, "cT"))
                for s in range(ST):
                    mm = pe.matmul(ps[:, 7, L + s * P:L + (s + 1) * P], cT[:, s * P:(s + 1) * P], wo[:],
                                   start=True, stop=True)
                mm.then_inc(*PB_PE.step("out"))

            def rows_turn(b, p, u):
                route_turn(pe, PR_PE, PR_DVE, b, p)

            def logits(b, p, u):
                route_logits(pe, PR_PE, PR_DVE, b, wr1)

            def places(b, p, u):
                if not isinstance(b, int) or b + 2 < B:
                    pe.wait_ge(*PA_DVE.at(b + 2, "v"))
                route_places(pe, PR_PE, PR_POOL, b, 0)

            skewed(pe, [(turn_max, 2), (scores((0, 1)), 2), (turn, 1), (rows_turn, 3),
                        (project("k", 1, (0, 1)), 1), (scores((2,)), 2), (project("k", 1, (2, 3)), 1),
                        (scores((3,)), 2), (logits, 3), (project("q", 0, range(G0)), 1), (values, 1),
                        (weigh, 2), (row_scores((0, 1)), 1), (turn_sums, 2), (row_scores((2,)), 1), (places, 3),
                        (turn_contexts, 2), (row_scores((3,)), 1), (outputs, 2)], B)

        N_SENT1 = 16 * ST * K * B // 2
        HALF = CAP // 2

        @block.sync
        def _(sp):
            def load(e, p, u):
                sp.wait_ge(*EX_D.at(e - 2, "down tail"))
                sp.wait_ge(*EX_DD.at(e - 2, "dst"))
                sp.dma_start(w1e[:, p], a["w1e"][bass.ds(e, 1)].rearrange("e d f -> d (e f)"))\
                  .then_inc(ld_we[p], 16)
                sp.dma_start(w2e[:, p].rearrange("p c d -> p (c d)"),
                             a["w2e"][bass.ds(e, 1)].rearrange("e p c d -> p (e c d)"))\
                  .then_inc(ld_we[p], 16)
                sp.dma_start(b2e[:, p], a["b2e"][bass.ds(e, 1)].rearrange("e d -> (e d)").partition_broadcast(P))\
                  .then_inc(ld_we[p], 16)
                sp.dma_start(b1e[:, p], a["b1e"][bass.ds(e, 1)].rearrange("e p f -> p (e f)"))\
                  .then_inc(ld_we[p], 16)
                for q in range(2):
                    sp.wait_ge(scattered1[q], N_SENT1)
                sp.dma_start(xe[:, p], xe1.rearrange("(e j p) x -> e p j x", e=E, j=CT)[bass.ds(e, 1)]
                             .rearrange("e p j x -> (e p) j x")).then_inc(ld_xe[p], 16)

            skewed(sp, [(load, 0)], E)

        @block.tensor
        def _(pe):
            def turn(e, p, u):
                pe.wait_ge(ld_xe[p], 16 * (u + 1))
                pe.wait_ge(*EX_TD.at(e - 1, "xT tail"))
                for j in range(4):
                    mm = pe.transpose(ps[:, 0, j * P:(j + 1) * P], xe[:, p, j, 0:D], ident[:])
                mm.then_inc(*EX_T.step("xT"))
                pe.transpose(ps[:, 1, 0:P], xe[:, p, 4, 0:D], ident[:]).then_inc(*EX_T.step("xT tail"))

            def up(e, p, u):
                pe.wait_ge(*EX_TD.at(e, "xT tail"))
                pe.wait_ge(ld_we[p], 64 * (u + 1))
                for n in range(2 * FT):
                    f, half = n // 2, n % 2
                    pe.wait_ge(*(EX_UA.at(e - 1, f"gelu{n + 4}") if n < 4 else EX_UA.at(e, f"gelu{n - 4}")))
                    pe.matmul(ps[:, 2 + n % 4, 0:HALF], w1e[:, p, f * P:(f + 1) * P],
                              xeT[:, p, half * HALF:(half + 1) * HALF], start=True, stop=True)\
                      .then_inc(*EX_U.step(f"up{n}"))

            def down(e, p, u):
                pe.wait_ge(*EX_UA.at(e, f"gelu{2 * FT - 1}"))
                for j in range(CT):
                    pe.wait_ge(*EX_DD.at(e - 1, "b2 tail"))
                    for f in range(FT):
                        mm = pe.matmul(ps[:, 6 + j // 4, (j % 4) * P:(j % 4 + 1) * P],
                                       hT[:, p, f, j * P:(j + 1) * P], w2e[:, p, f], start=(f == 0),
                                       stop=(f == FT - 1))
                    if j == 3:
                        mm.then_inc(*EX_D.step("down"))
                mm.then_inc(*EX_D.step("down tail"))

            skewed(pe, [(up, 1), (turn, 0), (down, 1)], E)

        @block.scalar
        def _(act):
            def up(e, p, u):
                act.wait_ge(*EX_D.at(e - 2, "down tail"))
                act.wait_ge(ld_we[p], 64 * (u + 1))
                for n in range(2 * FT):
                    f, half = n // 2, n % 2
                    act.wait_ge(*EX_U.at(e, f"up{n}"))
                    act.activation(hT[:, p, f, half * HALF:(half + 1) * HALF], ps[:, 2 + n % 4, 0:HALF],
                                   ACT.Gelu, bias=b1e[:, p, f:f + 1]).then_inc(*EX_UA.step(f"gelu{n}"))

            skewed(act, [(up, 1)], E)

        @block.vector
        def _(dve):
            def turn(e, p, u):
                dve.wait_ge(*EX_U.at(e - 2, f"up{2 * FT - 1}"))
                dve.wait_ge(*EX_T.at(e, "xT"))
                dve.tensor_copy(xeT[:, p, 0:4 * P], ps[:, 0]).then_inc(*EX_TD.step("xT"))
                dve.wait_ge(*EX_T.at(e, "xT tail"))
                dve.tensor_copy(xeT[:, p, 4 * P:], ps[:, 1, 0:P]).then_inc(*EX_TD.step("xT tail"))

            def down(e, p, u):
                b2 = b2e[:, p:p + 1].broadcast_to([P, 4, D])
                dve.wait_ge(*EX_DD.at(e - 1, "dst"))
                dve.wait_ge(*EX_D.at(e, "down"))
                dve.tensor_tensor(yb[:, 0:4], ps[:, 6].rearrange("p (j d) -> p j d", j=4), b2, ALU.add)\
                   .then_inc(*EX_DD.step("b2"))
                dve.wait_ge(*EX_D.at(e, "down tail"))
                dve.tensor_tensor(yb[:, 4], ps[:, 7, 0:D], b2e[:, p], ALU.add)\
                   .then_inc(*EX_DD.step("b2 tail"))
                dve.wait_ge(*EX_DD.at(e, "b2 tail"))
                dve.wait_ge(*EX_POOL.at(e - 2, "sent"))
                dve.tensor_tensor(ye[:, p], yb[:], xe[:, p, :, D + 1:D + 2].broadcast_to([P, CT, D]),
                                  ALU.mult).then_inc(*EX_DD.step("weighted"))
                dve.tensor_scalar(dst_u[:, p], xe[:, p, :, D], float(K * N), None, ALU.add)\
                   .then_inc(*EX_DD.step("dst"))

            skewed(dve, [(turn, 0), (down, 1)], E)

        @block.gpsimd
        def _(pool):
            def send(e, p, u):
                pool.wait_ge(*EX_DD.at(e, "dst"))
                held(pool, held_pool, e)
                for j in range(CT):
                    pool.indirect_dma_start(
                        out=y1, out_offset=bass.IndirectOffsetOnAxis(ap=dst_u[:, p, j:j + 1], axis=0),
                        in_=ye[:, p, j], in_offset=None, bounds_check=K * N - 1, oob_is_err=False,
                    ).then_inc(scattered_y1[p], 16)
                pool.wait_ge(scattered_y1[p], 16 * CT * (u + 1))
                pool.sem_inc(*EX_POOL.step("sent"))

            skewed(pool, [(send, 1)], E)

        N_SENT_Y1 = 16 * CT * E // 2

        @block.sync
        def _(sp):
            for dst, src in ((ln0[:, 0:1], "ln0_w"), (ln0[:, 1:2], "ln0_b"), (ln1[:, 0], "ln1_w"), (ln1[:, 1], "ln1_b"),
                             (qkw[:, 0].rearrange("p g c -> p (g c)"), "qw"),
                             (qkw[:, 1].rearrange("p g c -> p (g c)"), "kw"), (qkb[:, 0], "qb"), (qkb[:, 1], "kb"),
                             (vw[:].rearrange("p h c -> p (h c)"), "vw"), (w1[:], "w1"), (b1[:], "b1"),
                             (w2[:], "w2"), (wr2[:], "wr2"), (wgu[:], "wgu"), (wd[:], "wd")):
                sp.dma_start(dst, a[src]).then_inc(ld_w1, 16)
            sp.dma_start(vb_bc[:].rearrange("p h c -> p (h c)"), a["vb"].partition_broadcast(P)).then_inc(ld_w1, 16)
            sp.dma_start(b2_bc[:], a["b2"].partition_broadcast(P)).then_inc(ld_w1, 16)
            for q in range(2):
                sp.wait_ge(scattered_y1[q], N_SENT_Y1)

            def load(b, p, u):
                sp.wait_ge(*QA_DVE.at(b - 2, "h2"))
                for k in range(K):
                    sp.dma_start(yy[:, p, k], y1.rearrange("(k t p) d -> k p t d", k=K, t=NT)
                                 [k][:, bass.ds(b * ST, ST), :]).then_inc(ld_yy[p], 16)

            skewed(sp, [(load, 0)], B)

        N_W1 = 17 * 16

        @block.gpsimd
        def _(pool):
            def norm_outputs(b, p, u):
                pool.wait_ge(*QB_DVE.at(b, "mean1"))
                pool.tensor_tensor(rstd_o[:], mv_o[:, :, 1], eps[:], ALU.add)\
                    .then_inc(*QB_POOL.step("rstd eps"))
                pool.wait_ge(*QB_POOL.at(b, "rstd eps"))
                pool.tensor_tensor(rstd_o[:], rstd_o[:], half_neg[:], ALU.pow).then_inc(*QB_POOL.step("rstd"))

            def norm_keys(name):
                def norm(b, p, u):
                    pool.wait_ge(*QA_DVE.at(b, name + "mean1"))
                    pool.tensor_tensor(rstd_a[:], mv_a[:, :, 1], eps[:], ALU.add)\
                        .then_inc(*QA_POOL.step(name + "rstd eps"))
                    pool.wait_ge(*QA_POOL.at(b, name + "rstd eps"))
                    pool.tensor_tensor(rstd_a[:], rstd_a[:], half_neg[:], ALU.pow)\
                        .then_inc(*QA_POOL.step(name + "rstd"))
                return norm

            def residual(b, p, u):
                rows = h[:, bass.ds(b * ST, ST), :]
                pool.wait_ge(*QA_DVE.at(b, "x1_1"))
                pool.tensor_tensor(rows, rows, x1[:, p], ALU.add).then_inc(*QA_POOL.step("h x1"))

            def norm_route(b, p, u):
                pool.wait_ge(*QR_DVE.at(b, "mean1"))
                pool.tensor_tensor(rstd_b[:], mv_b[:, :, 1], eps[:], ALU.add)\
                    .then_inc(*QR_POOL.step("rstd eps"))
                pool.wait_ge(*QR_POOL.at(b, "rstd eps"))
                pool.tensor_tensor(rstd_b[:], rstd_b[:], half_neg[:], ALU.pow)\
                    .then_inc(*QR_POOL.step("rstd"))

            def rows_of(b, p, u):
                route(pool, QR_POOL, QR_DVE, b, p, None, slot_base2)

            def send(b, p, u):
                scatter(pool, b, p, u, QF_POOL, QF_DVE, xe2, E * REG, scattered2)

            skewed(pool, [(send, 4), (norm_outputs, 1), (norm_keys(""), 0), (residual, 0), (norm_keys("n "), 0),
                          (norm_route, 3), (rows_of, 3)], B)

        @block.vector
        def _(dve):
            dve.wait_ge(pool_const, POOL_CONSTS)
            dve.memset(q_bd1[:], 0.0).then_inc(l1_const, 1)
            dve.memset(v1[:, :, :, :, D:], 1.0).then_inc(l1_const, 1)
            dve.memset(mask[:, P:], 1.0).then_inc(l1_const, 1)
            dve.tensor_copy(mask[:, 0:P], causal[:]).then_inc(l1_const, 1)
            dve.wait_ge(ld_w1, N_W1)
            dve.wait_ge(b1_ready, 1)
            dve.tensor_tensor(b1_all[:], ps[:, 0, 0:4], b1[:], ALU.add).then_inc(l1_const, 1)
            dve.wait_ge(l1_const, 5)

            def stream(b, p, u):
                rows = h[:, bass.ds(b * ST, ST), :]
                dve.wait_ge(ld_yy[p], 16 * K * (u + 1))
                dve.tensor_tensor(yy[:, p, 0], yy[:, p, 0], yy[:, p, 1], ALU.add).then_inc(*QA_DVE.step("add"))
                dve.wait_ge(*QA_DVE.at(b, "add"))
                dve.tensor_tensor(rows, yy[:, p, 0], rows, ALU.add).then_inc(*QA_DVE.step("h2"))
                dve.wait_ge(*QA_DVE.at(b, "h2"))
                held(dve, held_dve, b)
                for s in range(ST):
                    dve.bn_stats(stats_a[:, s], h[:, bass.ds(b * ST + s, 1), :].rearrange("p a d -> p (a d)"))\
                       .then_inc(*QA_DVE.step(f"stats{s}"))
                dve.wait_ge(*QA_DVE.at(b, "stats1"))
                held(dve, held_dve, b)
                for s in range(ST):
                    dve.bn_aggr(mv_a[:, s], stats_a[:, s]).then_inc(*QA_DVE.step(f"mean{s}"))

            def norm1(b, p, u):
                dve.wait_ge(*QA_POOL.at(b, "rstd"))
                for s in range(ST):
                    dve.tensor_scalar(x1[:, p, s:s + 1], h[:, bass.ds(b * ST + s, 1), :], mv_a[:, s, 0:1],
                                      rstd_a[:, s:s + 1], ALU.subtract, ALU.mult)\
                       .then_inc(*QA_DVE.step(f"x1_{s}"))
                dve.wait_ge(*QA_DVE.at(b, "x1_1"))
                for s in range(ST):
                    dve.bn_stats(stats_a[:, s], x1[:, p, s]).then_inc(*QA_DVE.step(f"n stats{s}"))
                dve.wait_ge(*QA_DVE.at(b, "n stats1"))
                held(dve, held_dve, b)
                for s in range(ST):
                    dve.bn_aggr(mv_a[:, s], stats_a[:, s]).then_inc(*QA_DVE.step(f"n mean{s}"))

            def norm2(b, p, u):
                dve.wait_ge(*QA_POOL.at(b, "n rstd"))
                for s in range(ST):
                    dve.tensor_scalar(n0[:, s], x1[:, p, s], mv_a[:, s, 0:1], rstd_a[:, s:s + 1],
                                      ALU.subtract, ALU.mult).then_inc(*QA_DVE.step(f"n0_{s}"))

            def turned(b, p, u):
                dve.wait_ge(*QA_PE.at(b, "xT"))
                dve.tensor_copy(x1T[:, p], ps[:, 0, 0:L]).then_inc(*QA_DVE.step("x1T"))
                dve.tensor_scalar(x0T[:], ps[:, 0, L:], ln0[:, 0:1], ln0[:, 1:2], ALU.mult, ALU.add)\
                   .then_inc(*QA_DVE.step("x0T"))

            def clip(b, p, u):
                lo, hi = float(np.exp(np.float32(-10))), float(np.exp(np.float32(10)))
                for g in range(G1):
                    dve.wait_ge(*QA_ACT.at(b, f"k{g}"))
                    dve.tensor_scalar(k_T1[:, p, g], exp_k[:, g], hi, lo, ALU.min, ALU.max)\
                       .then_inc(*QA_DVE.step(f"k{g}"))
                for g in range(G1):
                    dve.wait_ge(*QA_ACT.at(b, f"q{g}"))
                    for q in range(4):
                        r = slice(32 * q, 32 * q + 32)
                        dve.tensor_scalar(q_bd1[r, p, g, q], exp_q[r, g], hi, lo, ALU.min, ALU.max)\
                           .then_inc(*QA_DVE.step(f"q{g}{q}"))

            def outputs(b, p, u):
                dve.wait_ge(*QB_DVE.at(b - 1, "n1"))
                for n in range(6):
                    g, m = n // 3, n % 3
                    dve.wait_ge(*QB_PE.at(b, f"s{n}"))
                    bank = ps[:, 3 + n % 2]
                    if m < 2:
                        hs = slice(4 * g + 2 * m, 4 * g + 2 * m + 2)
                        dve.tensor_tensor(s_T0[:, hs], bank.rearrange("p (h l) -> p h l", h=2),
                                          mask[:].unsqueeze(1).broadcast_to([P, 2, L]), ALU.mult)\
                           .then_inc(*QB_DVE.step(f"s{n}"))
                    else:
                        dve.tensor_tensor(s_T1[:, 4 * g:4 * g + 4], bank.rearrange("p (h l) -> p h l", h=4),
                                          causal[:].unsqueeze(1).broadcast_to([P, 4, P]), ALU.mult)\
                           .then_inc(*QB_DVE.step(f"s{n}"))
                for n, (s, hs) in enumerate(OUTS):
                    dve.wait_ge(*QB_PE.at(b, f"o{n}"))
                    bank = ps[:, 5 + n % 2, 0:(D + 1) * len(hs)].rearrange("p (h d) -> p h d", d=D + 1)
                    dve.reciprocal(r_den[:, n, 0:len(hs)].unsqueeze(2), bank[:, :, D:D + 1])\
                       .then_inc(*QB_DVE.step(f"r{n}"))
                    dve.wait_ge(*QB_DVE.at(b, f"r{n}"))
                    for i, hd in enumerate(hs):
                        dve.scalar_tensor_tensor(o[:, s, hd * D:(hd + 1) * D], bank[:, i, 0:D],
                                                 r_den[:, n, i:i + 1], vb_bc[:, hd], ALU.mult, ALU.add)\
                           .then_inc(*QB_DVE.step(f"o{n}{i}"))

            def output_stats(b, p, u):
                dve.wait_ge(*QB_DVE.at(b, "o51"))
                for s in range(ST):
                    for c in range(2):
                        dve.bn_stats(stats_o[:, s, c], o[:, s, 512 * c:512 * c + 512])\
                           .then_inc(*QB_DVE.step(f"stats{s}{c}"))
                dve.wait_ge(*QB_DVE.at(b, "stats11"))
                held(dve, held_dve, b)
                for s in range(ST):
                    dve.bn_aggr(mv_o[:, s], stats_o[:, s].rearrange("p c x -> p (c x)"))\
                       .then_inc(*QB_DVE.step(f"mean{s}"))

            def norm_outputs(b, p, u):
                dve.wait_ge(*QB_POOL.at(b, "rstd"))
                dve.wait_ge(*QC_PE.at(b - 1, "y3"))
                for s in range(ST):
                    dve.tensor_scalar(on[:, s].rearrange("p h d -> p (h d)"), o[:, s], mv_o[:, s, 0:1],
                                      rstd_o[:, s:s + 1], ALU.subtract, ALU.mult)\
                       .then_inc(*QB_DVE.step(f"n{s}"))

            def features(b, p, u):
                for n in range(H1):
                    dve.wait_ge(*QC_PE.at(b, f"y{n // 2}"))
                    dve.scalar_tensor_tensor(yT[:, n], ps[:, 3 + n // 2, (n % 2) * L:(n % 2 + 1) * L],
                                             ln1[:, 0, n:n + 1], x1T[:, p], ALU.mult, ALU.add)\
                       .then_inc(*QC_DVE.step(f"y{n}"))

            def residual(b, p, u):
                rows = h[:, bass.ds(b * ST, ST), :]
                dve.wait_ge(*QC_PE.at(b, "out"))
                dve.tensor_tensor(att[:], ps[:, 0, 0:L].rearrange("p (s d) -> p s d", s=ST),
                                  b2_bc[:].unsqueeze(1).broadcast_to([P, ST, D]), ALU.add)\
                   .then_inc(*QR_DVE.step("b2"))
                dve.wait_ge(*QA_POOL.at(b, "h x1"))
                dve.wait_ge(*QR_DVE.at(b, "b2"))
                dve.scalar_tensor_tensor(rows, att[:], 0.0, rows, ALU.max, ALU.add)\
                   .then_inc(*QR_DVE.step("h3"))
                dve.wait_ge(*QR_DVE.at(b, "h3"))
                held(dve, held_dve, b)
                row_stats(dve, QR_DVE, b, [h[:, bass.ds(b * ST + s, 1), :] for s in range(ST)])

            def rows_norm(b, p, u):
                norm_rows(dve, QR_DVE, QR_POOL, QF_POOL, b, p, [h[:, bass.ds(b * ST + s, 1), :] for s in range(ST)])

            def rows_turned(b, p, u):
                dve.wait_ge(*QR_PE.at(b, "xsT"))
                dve.tensor_copy(xsT[:], ps[:, 7, 0:L]).then_inc(*QR_DVE.step("xsT"))

            def pick(b, p, u):
                dve.wait_ge(*QR_PE.at(b, "logits"))
                dve.tensor_copy(lg[:].rearrange("p s e -> p (s e)"), ps[:, 7, L:L + ST * E])\
                   .then_inc(*QR_DVE.step("logits"))
                choose(dve, QR_DVE, b)

            def placed(b, p, u):
                place(dve, QR_DVE, QR_PE, b, 1, 7)

            def finish(b, p, u):
                own = QF_DVE
                dve.wait_ge(*QR_ACT.at(b, "top1"))
                dve.tensor_reduce(psum_k[:], e_top[:], AX, ALU.add).then_inc(*own.step("pair"))
                dve.wait_ge(*own.at(b, "pair"))
                dve.reciprocal(rk[:], psum_k[:]).then_inc(*own.step("rk"))
                dve.wait_ge(*QR_POOL.at(b, "row ids"))
                dve.tensor_reduce(slot[:], picked[:], AX, ALU.add).then_inc(*own.step("slot"))
                dve.wait_ge(*own.at(b, "slot"))
                dve.tensor_copy(slot_u[:, p], slot[:]).then_inc(*own.step("slot u"))
                dve.tensor_tensor(xs[:, p, :, :, D + 1], e_top[:], rk[:].unsqueeze(2).broadcast_to([P, ST, K]),
                                  ALU.mult).then_inc(*own.step("gate"))

            skewed(dve, [(finish, 4), (outputs, 1), (features, 2), (output_stats, 1), (stream, 0),
                         (norm_outputs, 1), (norm1, 0), (residual, 3), (norm2, 0), (rows_norm, 3), (turned, 0),
                         (rows_turned, 3), (clip, 0), (pick, 3), (placed, 3)], B)

        @block.scalar
        def _(act):
            act.wait_ge(l1_const, 5)

            def exps(b, p, u):
                act.wait_ge(*QA_DVE.at(b - 1, "q13"))
                for x, dst, name, bank in ((1, exp_k, "k", 2), (0, exp_q, "q", 1)):
                    act.wait_ge(*QA_PE.at(b, name))
                    for g in range(G1):
                        act.activation(dst[:, g], ps[:, bank, g * L:(g + 1) * L], ACT.Exp,
                                       bias=qkb[:, x, g:g + 1]).then_inc(*QA_ACT.step(f"{name}{g}"))

            def values(b, p, u):
                for n in range(4):
                    s, half = n // 2, n % 2
                    act.wait_ge(*QA_PE.at(b, f"v{n}"))
                    act.activation(v1[:, p, s, 4 * half:4 * half + 4, 0:D],
                                   ps[:, 2 - n % 2].rearrange("p (h d) -> p h d", h=4), ACT.Identity)\
                       .then_inc(*QA_ACT.step(f"v{n}"))

            def features(b, p, u):
                for n in range(4):
                    act.wait_ge(*QC_PE.at(b, f"f{n}"))
                    act.activation(h1T[:, n], ps[:, 3 + n, 0:L], ACT.Relu, bias=b1_all[:, n:n + 1])\
                       .then_inc(*QC_ACT.step(f"f{n}"))

            def weights(b, p, u):
                act.wait_ge(*QR_DVE.at(b, "neg top"))
                for s in range(ST):
                    act.activation(e_top[:, s], top8[:, s, 0:K], ACT.Exp, bias=neg_top[:, s:s + 1])\
                       .then_inc(*QR_ACT.step(f"top{s}"))

            skewed(act, [(features, 2), (exps, 0), (values, 0), (weights, 3)], B)

        @block.tensor
        def _(pe):
            pe.wait_ge(ld_w1, N_W1)
            pe.wait_ge(*EX_TD.at(E - 1, "xT tail"))
            for f in range(F1 // P):
                for hd in range(H1):
                    mm = pe.matmul(ps[:, 0, f:f + 1], w1[:, hd, f * P:(f + 1) * P], ln1[:, 1, hd:hd + 1],
                                   start=(hd == 0), stop=(hd == H1 - 1))
            mm.then_inc(b1_ready, 1)
            pe.wait_ge(l1_const, 5)
            pe.wait_ge(*EX_DD.at(E - 1, "b2 tail"))

            def turn(b, p, u):
                pe.wait_ge(*QA_DVE.at(b, "n0_1"))
                pe.wait_ge(*QR_DVE.at(b - 3, "b2"))
                for s in range(ST):
                    pe.transpose(ps[:, 0, s * P:(s + 1) * P], x1[:, p, s], ident[:])
                for s in range(ST):
                    mm = pe.transpose(ps[:, 0, L + s * P:L + (s + 1) * P], n0[:, s], ident[:])
                mm.then_inc(*QA_PE.step("xT"))

            def keys(b, p, u):
                pe.wait_ge(*QA_DVE.at(b, "x0T"))
                pe.wait_ge(*QA_ACT.at(b - 1, "v3"))
                for x, name, bank in ((1, "k", 2), (0, "q", 1)):
                    for g in range(G1):
                        mm = pe.matmul(ps[:, bank, g * L:(g + 1) * L], qkw[:, x, g], x0T[:], start=True,
                                       stop=True)
                    mm.then_inc(*QA_PE.step(name))

            def values(b, p, u):
                for n in range(4):
                    s, half = n // 2, n % 2
                    pe.wait_ge(*QA_ACT.at(b, ("k1", "q1", "v0", "v1")[n]))
                    pe.matmul(ps[:, 2 - n % 2], x1T[:, p, s * P:(s + 1) * P],
                              vw[:, 4 * half:4 * half + 4].rearrange("p h d -> p (h d)"), start=True,
                              stop=True).then_inc(*QA_PE.step(f"v{n}"))

            def outputs(b, p, u):
                pe.wait_ge(*QA_DVE.at(b, "q13"))
                for n in range(6):
                    g, m = n // 3, n % 3
                    pe.wait_ge(*(QB_DVE.at(b - 1, f"s{n + 4}") if n < 2 else QB_DVE.at(b, f"s{n - 2}")))
                    if m < 2:
                        rhs, key = q_bd1[:, p, g, 2 * m:2 * m + 2], k_T1[:, p, g, 0:P]
                    else:
                        rhs, key = q_bd1[:, p, g, :, P:L], k_T1[:, p, g, P:L]
                    pe.matmul(ps[:, 3 + n % 2].rearrange("p (h l) -> p h l", h=rhs.shape[1]), key, rhs,
                              start=True, stop=True).then_inc(*QB_PE.step(f"s{n}"))
                pe.wait_ge(*QA_ACT.at(b, "v3"))
                for n, (s, hs) in enumerate(OUTS):
                    if n < 2:
                        pe.wait_ge(*QB_DVE.at(b, "s5"))
                    else:
                        pe.wait_ge(*QB_DVE.at(b, f"o{n - 2}{len(OUTS[n - 2][1]) - 1}"))
                    for i, hd in enumerate(hs):
                        dst = ps[:, 5 + n % 2, (D + 1) * i:(D + 1) * (i + 1)]
                        mm = pe.matmul(dst, s_T0[:, hd, s * P:(s + 1) * P], v1[:, p, 0, hd, 0:D + 1],
                                       start=True, stop=(s == 0))
                        if s:
                            mm = pe.matmul(dst, s_T1[:, hd], v1[:, p, 1, hd, 0:D + 1], start=False, stop=True)
                    mm.then_inc(*QB_PE.step(f"o{n}"))

            def features(b, p, u):
                if not isinstance(b, int) or b + 1 < B:
                    pe.wait_ge(*QB_DVE.at(b + 1, "o51"))
                else:
                    pe.wait_ge(*QB_DVE.at(b, "n1"))
                for n in range(4):
                    for i in range(2):
                        for s in range(ST):
                            mm = pe.transpose(ps[:, 3 + n, i * L + s * P:i * L + (s + 1) * P],
                                              on[:, s, 2 * n + i], ident[:])
                    mm.then_inc(*QC_PE.step(f"y{n}"))
                pe.wait_ge(*QC_DVE.at(b, "y7"))
                for n in range(4):
                    for hd in range(H1):
                        mm = pe.matmul(ps[:, 3 + n, 0:L], w1[:, hd, n * P:(n + 1) * P], yT[:, hd],
                                       start=(hd == 0), stop=(hd == H1 - 1))
                    mm.then_inc(*QC_PE.step(f"f{n}"))

            def project(b, p, u):
                pe.wait_ge(*QR_DVE.at(b - 1, "b2"))
                pe.wait_ge(*QC_ACT.at(b, "f3"))
                if not isinstance(b, int) or b + 2 < B:
                    pe.wait_ge(*QA_DVE.at(b + 2, "x0T"))
                for s in range(ST):
                    for f in range(F1 // P):
                        mm = pe.matmul(ps[:, 0, s * P:(s + 1) * P], h1T[:, f, s * P:(s + 1) * P], w2[:, f],
                                       start=(f == 0), stop=(f == F1 // P - 1))
                mm.then_inc(*QC_PE.step("out"))

            def rows_turn(b, p, u):
                route_turn(pe, QR_PE, QR_DVE, b, p)

            def logits(b, p, u):
                route_logits(pe, QR_PE, QR_DVE, b, wr2)

            def places(b, p, u):
                route_places(pe, QR_PE, QR_POOL, b, 7)

            skewed(pe, [(outputs, 1), (features, 2), (turn, 0), (rows_turn, 3), (keys, 0), (logits, 3),
                        (values, 0), (project, 2), (places, 3)], B)

        N_SENT2 = 16 * ST * K * B // 2
        N_TABLE = 15

        @block.gpsimd
        def _(pool):
            pool.iota(t_no_i[:], [[1, TILES2]], base=0, channel_multiplier=0).then_inc(table, 1)

            def send(t, p, u):
                pool.wait_ge(*FD_DVE.at(t, "dst"))
                held(pool, held_pool, t)
                pool.indirect_dma_start(
                    out=y2, out_offset=bass.IndirectOffsetOnAxis(ap=dst2_u[:, p, 0:1], axis=0),
                    in_=yo[:, p], in_offset=None, bounds_check=K * N - 1, oob_is_err=False,
                ).then_inc(scattered_y2[p], 16)
                pool.wait_ge(scattered_y2[p], 16 * (u + 1))
                pool.sem_inc(*FD_POOL.step("sent"))

            skewed(pool, [(send, 2)], TILES2)

        @block.vector
        def _(dve):
            n = [1]

            def then(ins):
                n[0] += 1
                ins.then_inc(table, 1)
                dve.wait_ge(table, n[0])

            dve.wait_ge(*QF_DVE.at(B - 1, "gate"))
            dve.wait_ge(table, 1)
            then(dve.tensor_copy(t_no[:, :, 0], t_no_i[:]))
            then(dve.tensor_scalar(n_tiles[:, 0], counts[0:1, 1], float(P - 1), None, ALU.add))
            then(dve.tensor_copy(n_i[:], n_tiles[:, 0]))
            then(dve.tensor_scalar(n_i[:], n_i[:], 7, None, ALU.arith_shift_right))
            then(dve.tensor_copy(n_tiles[:, 0], n_i[:]))
            then(dve.memset(t_start[:], 0.0))
            then(dve.tensor_tensor_scan(ends[:, 0], n_tiles[:, 0], t_start[:, 0:E], 0.0, ALU.add, ALU.add))
            then(dve.tensor_tensor(t_past[:], t_no[:].broadcast_to([1, TILES2, E - 1]),
                                   ends[:, :, 0:E - 1].broadcast_to([1, TILES2, E - 1]), ALU.is_ge))
            then(dve.tensor_reduce(t_e[:], t_past[:], AX, ALU.add))
            then(dve.tensor_tensor(t_past[:], t_past[:], n_tiles[:, :, 0:E - 1].broadcast_to([1, TILES2, E - 1]),
                                   ALU.mult))
            then(dve.tensor_reduce(t_start[:], t_past[:], AX, ALU.add))
            then(dve.tensor_copy(tab_e[:], t_e[:]))
            then(dve.scalar_tensor_tensor(t_row[:], t_e[:], float(REG // P), t_start[:], ALU.mult, ALU.subtract))
            then(dve.tensor_tensor(t_row[:], t_row[:], t_no[:, :, 0], ALU.add))
            then(dve.tensor_scalar(tab_row[:], t_row[:], float(P), None, ALU.mult))

            def turn(t, p, u):
                dve.wait_ge(*FU_PE.at(t - 2, "gu"))
                dve.wait_ge(*FT_PE.at(t, "xT"))
                dve.tensor_copy(xtT[:, p], ps[:, p, 0:P]).then_inc(*FT_DVE.step("xT"))
                dve.tensor_copy(meta[:, bass.ds(t, 1), :], xt[:, p:p + 1, D:]).then_inc(*FT_DVE.step("meta"))

            def up(t, p, u):
                dve.wait_ge(*FH_PE.at(t - 2, "guT"))
                dve.wait_ge(*FU_ACT.at(t, "silu"))
                dve.tensor_tensor(gu[:, p], ps[:, 2 + p, HE:], silu[:, p], ALU.mult)\
                   .then_inc(*FU_DVE.step("gu"))

            def down(t, p, u):
                dve.wait_ge(*FD_POOL.at(t - 2, "sent"))
                dve.wait_ge(*FT_DVE.at(t, "meta"))
                dve.wait_ge(*FD_PE.at(t, "out"))
                dve.tensor_tensor(yo[:, p:p + 1], ps[:, 6 + p:7 + p, 0:D],
                                  meta[:, bass.ds(t, 1), 1:2].broadcast_to([P, 1, D]), ALU.mult)\
                   .then_inc(*FD_DVE.step("y"))
                dve.tensor_scalar(dst2_u[:, p:p + 1, :], meta[:, bass.ds(t, 1), 0:1], float(K * N), None,
                                  ALU.add).then_inc(*FD_DVE.step("dst"))

            skewed(dve, [(turn, 0), (up, 1), (down, 2)], TILES2)

        @block.sync
        def _(sp):
            sp.wait_ge(table, N_TABLE + 1)
            for q in range(2):
                sp.wait_ge(scattered2[q], N_SENT2)

            def load(t, p, u):
                sp.wait_ge(*FT_DVE.at(t - 2, "meta"))
                row = sp.value_load(tab_row[0:1, bass.ds(t, 1)], min_val=0, max_val=E * REG + SPARE - P)
                sp.dma_start(xt[:, p], xe2[bass.ds(row, P), :]).then_inc(ld_xt[p], 16)

            skewed(sp, [(load, 0)], TILES2)

        @block.scalar
        def _(act):
            def up(t, p, u):
                act.wait_ge(*FU_DVE.at(t - 2, "gu"))
                act.wait_ge(*FU_PE.at(t, "gu"))
                act.activation(silu[:, p], ps[:, 2 + p, 0:HE], ACT.Silu).then_inc(*FU_ACT.step("silu"))

            def turn(t, p, u):
                act.wait_ge(*FD_PE.at(t - 2, "out"))
                act.wait_ge(*FH_PE.at(t, "guT"))
                act.activation(guT[:, p].rearrange("p c t -> p (c t)"), ps[:, 4 + p, 0:HE], ACT.Identity)\
                   .then_inc(*FH_ACT.step("guT"))

            skewed(act, [(turn, 2), (up, 1)], TILES2)

        @block.tensor
        def _(pe):
            pe.wait_ge(table, N_TABLE + 1)
            pe.wait_ge(*QF_DVE.at(B - 1, "gate"))

            def turn(t, p, u):
                pe.wait_ge(ld_xt[p], 16 * (u + 1))
                pe.wait_ge(*FT_DVE.at(t - 2, "xT"))
                pe.transpose(ps[:, p, 0:P], xt[:, p, 0:D], ident[:]).then_inc(*FT_PE.step("xT"))

            def up(t, p, u):
                e = pe.value_load(tab_e[0:1, bass.ds(t, 1)], min_val=0, max_val=E - 1)
                pe.wait_ge(*FT_DVE.at(t, "xT"))
                pe.wait_ge(*FU_DVE.at(t - 2, "gu"))
                pe.matmul(ps[:, 2 + p], xtT[:, p], wgu[:, bass.ds(e, 1)].rearrange("p e f -> p (e f)"),
                          start=True, stop=True).then_inc(*FU_PE.step("gu"))

            def turn_gu(t, p, u):
                pe.wait_ge(*FU_DVE.at(t, "gu"))
                pe.wait_ge(*FH_ACT.at(t - 2, "guT"))
                for c in range(HT):
                    mm = pe.transpose(ps[:, 4 + p, c * P:(c + 1) * P], gu[:, p, c * P:(c + 1) * P], ident[:])
                mm.then_inc(*FH_PE.step("guT"))

            def down(t, p, u):
                e = pe.value_load(tab_e[0:1, bass.ds(t, 1)], min_val=0, max_val=E - 1)
                pe.wait_ge(*FH_ACT.at(t, "guT"))
                pe.wait_ge(*FD_DVE.at(t - 2, "y"))
                for c in range(HT):
                    mm = pe.matmul(ps[:, 6 + p, 0:D], guT[:, p, c],
                                   wd[:, bass.ds(e, 1), c].rearrange("p e d -> p (e d)"), start=(c == 0),
                                   stop=(c == HT - 1))
                mm.then_inc(*FD_PE.step("out"))

            skewed(pe, [(turn, 0), (turn_gu, 2), (up, 1), (down, 2)], TILES2)

        @block.sync
        def _(sp):
            for q in range(2):
                sp.wait_ge(scattered_y2[q], 16 * TILES2 // 2)
            for c in range(NT // CH):
                if c >= 2:
                    sp.wait_ge(summed, 2 * (c - 1))
                for k in range(K):
                    sp.dma_start(y_in[:, c % 2, k], y2.rearrange("(k c t p) d -> k c p t d", k=K, t=CH, p=P)[k, c])\
                      .then_inc(ld_y2[c % 2], 16)
            for c in range(NT // CH):
                sp.wait_ge(summed, 2 * (c + 1))
                sp.dma_start(out.rearrange("(c t p) d -> c p t d", t=CH, p=P)[c], h[:, c * CH:(c + 1) * CH])\
                  .then_inc(stored, 16)
            sp.wait_ge(stored, 16 * (NT // CH))

        @block.vector
        def _(dve):
            for c in range(NT // CH):
                dve.wait_ge(ld_y2[c % 2], 32 * (c // 2 + 1))
                for k in range(K):
                    rows = h[:, c * CH:(c + 1) * CH]
                    dve.tensor_tensor(rows, y_in[:, c % 2, k], rows, ALU.add).then_inc(summed, 1)
                    dve.wait_ge(summed, 2 * c + k + 1)

def kernel(**inputs):
    import concourse.bacc as bacc
    from concourse.bass_utils import run_bass_kernel_spmd

    arrays = layouts({k: np.asarray(v) for k, v in inputs.items()})
    nc = bacc.Bacc("TRN2", target_bir_lowering=False, num_devices=1)
    aps = {n: nc.dram_tensor(f"in_{n}", v.shape, mybir.dt.from_np(v.dtype), kind="ExternalInput").ap()
           for n, v in arrays.items()}
    out = nc.dram_tensor("out", [N, D], F32, kind="ExternalOutput").ap()
    lm_tower(nc, aps, out)
    r = run_bass_kernel_spmd(nc, [{f"in_{n}": v for n, v in arrays.items()}], core_ids=[0])
    return r.results[0]["out"].reshape(B, L, D)
```

```python
from contextlib import ExitStack

import numpy as np

import concourse.bass as bass
from concourse import mybir

F32 = mybir.dt.float32
F32R = mybir.dt.float32r
BF16 = mybir.dt.bfloat16
I32 = mybir.dt.int32
U32 = mybir.dt.uint32
ALU = mybir.AluOpType
ACT = mybir.ActivationFunctionType
AX = mybir.AxisListType.X

P = 128
B, L, D = 8, 256, 128
N = B * L
ST = L // P
NT = N // P
VOCAB = 50257
H0, C0 = 8, 16
G0 = 4
E, K = 8, 2
F0 = 512
CAP = 640
FT = F0 // P
CT = CAP // P
HEAD = 2
H1, A1 = 8, 32
G1 = 2
F1 = 512
HE = 256
HT = HE // P
REG = N
TILES2 = N * K // P + E
SPARE = TILES2 * P - 2 * REG
XW = D + 2
EPS = 1e-5
ZW = 2048
NPAIR = TILES2 // 2
CH = 4
BIG = 1.0e6


class Steps:

    def __init__(self, sem, names, ahead=4):
        self.sem, self.names, self.ahead, self.next = sem, list(names), ahead, 0

    def step(self, name):
        assert self.names[self.next] == name, (self.names[self.next], name)
        self.next = (self.next + 1) % len(self.names)
        return self.sem, 1

    def at(self, rnd, name):
        return self.sem, len(self.names) * (rnd + self.ahead) + self.names.index(name) + 1

    def start(self, eng):
        eng.sem_inc(self.sem, len(self.names) * self.ahead)


def held(eng, sem, rnd):
    if not isinstance(rnd, int):
        eng.sem_inc(sem, 1)


def skewed(eng, stages, rounds, turn=2, unroll=1, peeled=0, opening=None):
    assert opening is None or len(opening) == sum(lag < 2 for _, lag in stages)
    most = max(lag for _, lag in stages)
    first = -(-most // turn) * turn + peeled
    body = turn * unroll
    turns = (rounds - first) // body

    def time(t, j=None):
        for stage, lag in (opening if opening and t < 2 else stages):
            p = (t - lag) % turn
            if j is None:
                if 0 <= t - lag < rounds:
                    stage(t - lag, p, (t - lag) // turn)
            else:
                stage(j * body + (t - lag), p, j * unroll + (t - lag) // turn)

    for t in range(first):
        time(t)
    with eng.Fori(0, turns) as j:
        for t in range(first, first + body):
            time(t, j)
    for t in range(first + body * turns, rounds + most):
        time(t)


def layouts(i):
    def c(x):
        return np.ascontiguousarray(x)

    return {
        "ids": c(i["x"].reshape(NT, P).T),
        "embed": c(i["L0_tok_embed_matrix"]),
        "wqkv": c(i["L0_attn_qkv_w"].reshape(H0, 3, C0, D).transpose(3, 1, 0, 2).reshape(D, 3 * D)),
        "bqkv": c(i["L0_attn_qkv_b"].reshape(H0, 3, C0).transpose(1, 0, 2).reshape(1, 3 * D)),
        "bv": c(i["L0_attn_qkv_b"].reshape(H0, 3, C0)[:, 2].reshape(D)),
        "wo": c(i["L0_attn_out_w"].T),
        "bo": c(i["L0_attn_out_b"]),
        "wr1": c(i["L0_ffn_Wr"]),
        "br": c(i["L0_ffn_br"]),
        "w1e": c(i["L0_ffn_W1"].transpose(1, 0, 2)),
        "b1e": c(i["L0_ffn_b1"].reshape(E, FT, P).transpose(2, 0, 1)),
        "w2e": c(i["L0_ffn_W2"].reshape(E, FT, P, D).transpose(2, 0, 1, 3)),
        "b2e": c(i["L0_ffn_b2"]),
        "ln0_w": c(i["L1_attn_ln0_w"].reshape(D, 1)),
        "ln0_b": c(i["L1_attn_ln0_b"].reshape(D, 1)),
        "ln1_w": c(i["L1_attn_ln1_w"]),
        "ln1_b": c(i["L1_attn_ln1_b"]),
        "qw": c(i["L1_attn_qw"].reshape(D, A1, H1).transpose(0, 2, 1).reshape(D, A1 * H1)),
        "kw": c(i["L1_attn_kw"].reshape(D, A1, H1).transpose(0, 2, 1).reshape(D, A1 * H1)),
        "qb": c(i["L1_attn_qb"].reshape(A1, H1).T.reshape(G1, P).T),
        "kb": c(i["L1_attn_kb"].reshape(A1, H1).T.reshape(G1, P).T),
        "vw": c(i["L1_attn_vw"].reshape(D, D, H1).transpose(0, 2, 1).reshape(D, H1 * D)),
        "vb": c(i["L1_attn_vb"].reshape(D, H1).T.reshape(H1 * D)),
        "w1": c(i["L1_attn_w1"].reshape(D, H1, F1)),
        "b1": c(i["L1_attn_b1"].reshape(F1 // P, P).T),
        "w2": c(i["L1_attn_w2"].reshape(F1 // P, P, D).transpose(1, 0, 2)),
        "b2": c(i["L1_attn_b2"]),
        "wr2": c(i["L1_ffn_router_w"].T),
        "wgu": c(np.concatenate([i["L1_ffn_w_gate"], i["L1_ffn_w_up"]], axis=2).transpose(1, 0, 2)),
        "wd": c(i["L1_ffn_w_down"].reshape(E, HT, P, D).transpose(2, 0, 1, 3)),
    }


def lm_tower(nc, a, out):
    with ExitStack() as ctx:
        def sb(name, shape, dt=F32):
            return ctx.enter_context(nc.sbuf_tensor(name, shape, dt))

        def sem(name):
            return ctx.enter_context(nc.semaphore(name))

        def dram(name, shape):
            return nc.dram_tensor(name, shape, F32, kind="Internal").ap()

        def steps(name, names):
            return Steps(sem(name), names)

        xe1 = dram("xe1", [E * CAP, XW])
        y1 = dram("y1", [K * N, D])
        xe2 = dram("xe2", [E * REG + SPARE, XW])
        y2 = dram("y2", [K * N, D])

        ps = ctx.enter_context(nc.psum_tensor("ps", [P, 8, 512], F32))

        ident = sb("ident", [P, P])
        before = sb("before", [P, P], BF16)
        ones_bf = sb("ones_bf", [P, P], BF16)
        causal = sb("causal", [P, P])
        zeros = sb("zeros", [P, ZW])
        half_neg = sb("half_neg", [P, 2])
        eps = sb("eps", [P, 2])
        iota_i = sb("iota_i", [P, 64], I32)
        expert_no = sb("expert_no", [P, E])
        slot_base1 = sb("slot_base1", [P, 1, E])
        slot_base2 = sb("slot_base2", [P, 1, E])
        row_id = sb("row_id", [P, NT, K])
        lo_rows = sb("lo_rows", [P, 2])
        row_no = sb("row_no", [P, 8], I32)

        h = sb("h", [P, NT, D])

        ids = sb("ids", [P, NT], I32)
        wqkv = sb("wqkv", [P, 3, H0, C0])
        bqkv = sb("bqkv", [1, 3, H0, C0])
        w_rep = sb("w_rep", [P, 2, G0, P])
        b_rep = sb("b_rep", [1, 2, G0, P])
        one = sb("one", [1, 1])
        first_use = sb("first_use", [1, 1])
        bias_qk = sb("bias_qk", [P, 2, G0])
        bias_lo = sb("bias_lo", [P, 2, G0])
        wo = sb("wo", [P, D])
        bv_bc = sb("bv_bc", [P, D])
        bo_bc = sb("bo_bc", [P, D])
        stats_b = sb("stats_b", [P, ST, 6])
        mv_b = sb("mv_b", [P, ST, 2])
        rstd_b = sb("rstd_b", [P, ST])

        wr1 = sb("wr1", [P, E])
        br_bc = sb("br_bc", [P, E])
        xs = sb("xs", [P, 2, ST, K, XW])
        xsT = sb("xsT", [P, L])
        lg = sb("lg", [P, ST, E])
        top8 = sb("top8", [P, ST, 8])
        idx8 = sb("idx8", [P, ST, 8], U32)
        idx_f = sb("idx_f", [P, ST, K])
        neg_top = sb("neg_top", [P, ST])
        e_all = sb("e_all", [P, ST, E])
        z_all = sb("z_all", [P, ST])
        e_top = sb("e_top", [P, ST, K])
        kept = sb("kept", [P, ST, K])
        pair_sum = sb("pair_sum", [P, ST])
        kept_sum = sb("kept_sum", [P, ST])
        rk = sb("rk", [P, ST])
        onehot = sb("onehot", [P, ST, K, E])
        chosen = sb("chosen", [P, ST, E], BF16)
        counts = sb("counts", [P, 2, E])
        pos = sb("pos", [P, ST, E])
        over = sb("over", [P, ST, E])
        picked = sb("picked", [P, ST, K, E])
        slot = sb("slot", [P, ST, K])
        keep = sb("keep", [P, ST, K])
        slot_u = sb("slot_u", [P, 2, ST, K], U32)

        ln0 = sb("ln0", [P, 2])
        ln1 = sb("ln1", [P, 2, H1])
        qkw = sb("qkw", [P, 2, G1, P])
        qkb = sb("qkb", [P, 2, G1])
        vw = sb("vw", [P, H1, D])
        vb_bc = sb("vb_bc", [P, H1, D])
        with ExitStack() as whole:
            w1 = whole.enter_context(nc.sbuf_tensor("w1", [P, H1, F1], F32))
        w1_lo = sb("w1_lo", [P, H1, F1], F32R)
        b1 = sb("b1", [P, F1 // P])
        b1_all = sb("b1_all", [P, F1 // P])
        w2 = sb("w2", [P, F1 // P, D])
        b2_bc = sb("b2_bc", [P, D])
        wr2 = sb("wr2", [P, E])
        mask = sb("mask", [P, L])

        q_bd1 = sb("q_bd1", [P, 2, G1, 4, L])
        s_T0 = sb("s_T0", [P, H1, L])
        wgu = q_bd1[:].rearrange("p x g (a b) l -> p (x g a) (b l)", a=E // 4)
        wd = s_T0[:].rearrange("p e (c d) -> p e c d", c=HT)
        n_i = sb("n_i", [1, E], I32)
        n_tiles = sb("n_tiles", [1, 1, E])
        ends = sb("ends", [1, 1, E])
        t_no = sb("t_no", [1, TILES2, 1])
        t_no_i = sb("t_no_i", [1, TILES2], I32)
        t_past = sb("t_past", [1, TILES2, E - 1])
        t_e = sb("t_e", [1, TILES2])
        t_start = sb("t_start", [1, TILES2])
        t_row = sb("t_row", [1, TILES2])
        tab_e = sb("tab_e", [1, 2 + NPAIR + 1, 2], I32)
        tab_row = sb("tab_row", [1, TILES2], I32)

        layer0 = ExitStack()

        def sb_layer0(name, shape, dt=F32):
            return layer0.enter_context(nc.sbuf_tensor(name, shape, dt))

        w1e = sb_layer0("w1e", [P, E, F0])
        w2e = sb_layer0("w2e", [P, E, FT, D])
        b1e = sb_layer0("b1e", [P, E, FT])
        b2e = sb_layer0("b2e", [P, E, D])
        xe = sb_layer0("xe", [P, 2, CT, XW])

        attention0 = ExitStack()

        def sb0(name, shape, dt=F32):
            return attention0.enter_context(nc.sbuf_tensor(name, shape, dt))

        ids_s = sb0("ids_s", [P, 2, ST], I32)
        emb = sb0("emb", [P, 2, ST, D])
        stats = sb0("stats", [P, ST, 6])
        mv = sb0("mv", [P, ST, 2])
        rstd = sb0("rstd", [P, ST])
        xn = sb0("xn", [P, 2, ST, D])
        xT = sb0("xT", [P, 2, L])
        hi_t = sb0("hi_t", [P, 2 * G0, L], F32R)
        q_bd = sb0("q_bd", [P, 2, G0, 2, L], F32R)
        k_op = sb0("k_op", [P, 2, G0, L], F32R)
        v_ext = sb0("v_ext", [P, 2, ST, H0, 32])
        mx = sb0("mx", [P, 2, ST, G0, 2])
        m16 = sb0("m16", [P, ST, 2 * H0])
        mT = sb0("mT", [2 * H0, L], F32R)
        head_rows = sb0("head_rows", [2 * H0, H0, P], F32R)
        head_eq = sb0("head_eq", [P, H0])
        head_of = sb0("head_of", [P, 1])
        pT = sb0("pT", [P, G0, ST, 2, L])
        pv_sb = sb0("pv_sb", [P, 2, L])
        rden = sb0("rden", [P, ST, H0, 1])
        cn = sb0("cn", [P, ST, H0, C0])
        cT = sb0("cT", [P, L])
        attention0.close()

        w1_p = sb_layer0("w1_p", [P, 2, F0])
        b1_p = sb_layer0("b1_p", [P, 2, FT])
        xeT = sb_layer0("xeT", [P, 2, CAP])
        hT = sb_layer0("hT", [P, 2, FT, CAP])
        yb = sb_layer0("yb", [P, CT, D])
        ye = sb_layer0("ye", [P, 2, CT, D])
        dst_u = sb_layer0("dst_u", [P, 2, CT], U32)
        layer0.close()

        attention1 = ExitStack()

        def sb1(name, shape, dt=F32):
            return attention1.enter_context(nc.sbuf_tensor(name, shape, dt))

        w1_hi = sb1("w1_hi", [P, H1, F1], F32R)
        yy = sb1("yy", [P, 2, K, ST, D])
        stats_a = sb1("stats_a", [P, ST, 6])
        mv_a = sb1("mv_a", [P, ST, 2])
        rstd_a = sb1("rstd_a", [P, ST])
        x1 = sb1("x1", [P, 2, ST, D])
        n0 = sb1("n0", [P, ST, D])
        x1T = sb1("x1T", [P, 2, L])
        x0T = sb1("x0T", [P, L])
        exp_q = sb1("exp_q", [P, G1, L])
        exp_k = sb1("exp_k", [P, G1, L])
        k_T1 = sb1("k_T1", [P, 2, G1, L])
        v1 = sb1("v1", [P, 2, ST, H1, D + 2])
        s_T1 = sb1("s_T1", [P, H1, P])
        r_den = sb1("r_den", [P, 6, 3])
        o = sb1("o", [P, ST, H1 * D])
        stats_o = sb1("stats_o", [P, ST, 2, 6])
        mv_o = sb1("mv_o", [P, ST, 2])
        rstd_o = sb1("rstd_o", [P, ST])
        on = sb1("on", [P, ST, H1, D])
        with ExitStack() as whole:
            yT = whole.enter_context(nc.sbuf_tensor("yT", [P, H1, L], F32))
        y_lo = sb1("y_lo", [P, H1, L], F32R)
        y_hi = sb1("y_hi", [P, H1, L], F32R)
        h1T = sb1("h1T", [P, F1 // P, L])
        att = sb1("att", [P, ST, D])
        attention1.close()

        xt = sb("xt", [P, 2, 2, XW])
        xtT = sb("xtT", [P, 2, P])
        meta = sb("meta", [P, TILES2, 2])
        silu = sb("silu", [P, 2, HE])
        gu = sb("gu", [P, 2, HE])
        guT = sb("guT", [P, 2, HT, P])
        yo = sb("yo", [P, 2, 2, D])
        dst2_u = sb("dst2_u", [P, 2, 2, 1], U32)
        y_in = sb("y_in", [P, NT // CH, K, CH, D])

        ld_ids = sem("ld_ids")
        ld_w0 = sem("ld_w0")
        pool_const = sem("pool_const")
        dve_const = sem("dve_const")
        bias_ready = sem("bias_ready")
        zeroed1 = sem("zeroed1")
        zeroed2 = sem("zeroed2")
        held_pool = sem("held_pool")
        held_dve = sem("held_dve")

        embedded = [sem("embedded0"), sem("embedded1")]
        scattered1 = [sem("scattered1_0"), sem("scattered1_1")]
        PG_POOL = steps("pg_pool", ["ids"])
        PA_POOL = steps("pa_pool", ["rstd eps", "rstd", "residual"])
        PN_DVE = steps("pn_dve", ["stats0", "stats1", "mean0", "mean1", "xn0", "xn1"])
        PA_DVE = steps("pa_dve", ["xT"]
                       + [f"k{g}" for g in range(G0)] + [f"q{g}{x}" for g in range(G0) for x in "ab"]
                       + ["v"] + [f"max{g}" for g in range(G0)] + ["max hi", "max lo"])
        PA_ACT = steps("pa_act", [f"hi k{g}" for g in range(G0)] + [f"hi q{g}" for g in range(G0)])
        PA_PE = steps("pa_pe", ["xT"] + [f"k{g}" for g in range(G0)] + [f"q{g}" for g in range(G0)]
                      + ["v"] + [f"scores{g}" for g in range(G0)])
        PB_DVE = steps("pb_dve", ["rden", "cn"])
        PB_ACT = steps("pb_act", ["mT"] + [f"exp{g}" for g in range(G0)] + ["pv", "cT"])
        PB_PE = steps("pb_pe", ["maxT"] + [f"scores{g}" for g in range(G0)] + ["pv", "ct", "cT", "out"])
        PR_DVE = steps("pr_dve", ["residual", "stats0", "stats1", "mean0", "mean1", "xs0", "xs1", "xsT", "logits",
                                  "top0", "top1", "idx0", "idx1", "idx f", "neg top", "pos", "counts"])
        PR_ACT = steps("pr_act", ["z0", "z1", "top0", "top1"])
        PR_PE = steps("pr_pe", ["xsT", "logits", "pos"])
        PR_POOL = steps("pr_pool", ["rstd eps", "rstd"] + [f"onehot{i}" for i in range(4)]
                        + ["chosen", "over", "pos base", "pos over", "picked0", "picked1", "row ids"])
        PF_DVE = steps("pf_dve", ["pair", "slot", "pair eps", "keep", "slot u", "kept", "kept sum", "kept eps",
                                  "rkept", "gate"])
        PF_POOL = steps("pf_pool", ["sent"])

        ld_xe = [sem("ld_xe0"), sem("ld_xe1")]
        scattered_y1 = [sem("scattered_y1_0"), sem("scattered_y1_1")]
        EX_W = steps("ex_w", ["w1", "b1"])
        EX_T = steps("ex_t", ["xT", "xT tail"])
        EX_U = steps("ex_u", [f"up{u}" for u in range(2 * FT)])
        EX_D = steps("ex_d", ["down a", "down b"])
        EX_TD = steps("ex_td", ["xT", "xT tail"])
        EX_UA = steps("ex_ua", [f"gelu{u}" for u in range(2 * FT)])
        EX_DD = steps("ex_dd", ["b2 a", "weighted a", "dst", "b2 b", "weighted b"])
        EX_POOL = steps("ex_pool", ["sent"])

        ld_w1 = sem("ld_w1")
        ld_yy = [sem("ld_yy0"), sem("ld_yy1")]
        scattered2 = [sem("scattered2_0"), sem("scattered2_1")]
        l1_const = sem("l1_const")
        w1_split = sem("w1_split")
        ld_wf = sem("ld_wf")
        b1_ready = sem("b1_ready")
        ld_we = sem("ld_we")
        QA_DVE = steps("qa_dve", ["add", "h2", "stats0", "stats1", "mean0", "mean1", "x1_0", "x1_1", "n stats0",
                                  "n stats1", "n mean0", "n mean1", "n0_0", "n0_1", "x1T", "x0T", "k0", "k1"]
                       + [f"q{g}{q}" for g in range(G1) for q in range(4)])
        QA_POOL = steps("qa_pool", ["rstd eps", "rstd", "h x1", "n rstd eps", "n rstd"])
        QA_PE = steps("qa_pe", ["xT", "k", "q"] + [f"v{n}" for n in range(4)])
        QA_ACT = steps("qa_act", ["k0", "k1", "q0", "q1"] + [f"v{n}" for n in range(4)])
        OUTS = [(s, heads) for s in range(ST) for heads in ((0, 1, 2), (3, 4, 5), (6, 7))]
        QB_PE = steps("qb_pe", [f"s{n}" for n in range(6)] + [f"o{n}" for n in range(6)])
        QB_DVE = steps("qb_dve", [f"s{n}" for n in (1, 2, 4, 5)]
                       + [x for n, (_, hs) in enumerate(OUTS) for x in [f"r{n}"] + [f"o{n}{i}" for i in range(len(hs))]]
                       + [f"stats{s}{c}" for s in range(ST) for c in range(2)] + ["mean0", "mean1", "n0", "n1"])
        QB_POOL = steps("qb_pool", ["mask0", "mask3", "rstd eps", "rstd"])
        QB_ACT = steps("qb_act", ["s0", "s3"])
        QC_PE = steps("qc_pe", [f"y{n}" for n in range(4)] + ["f"])
        QO_PE = steps("qo_pe", ["out"])
        QC_DVE = steps("qc_dve", [f"y{n}" for n in range(H1)])
        QC_POOL = steps("qc_pool", [f"lo{n}" for n in range(4)])
        QC_ACT = steps("qc_act", [f"hi{n}" for n in range(4)] + [f"f{n}" for n in range(4)])
        QR_PE = steps("qr_pe", ["xsT", "logits"])
        QF_PE = steps("qf_pe", ["pos"])
        QR_DVE = steps("qr_dve", ["b2", "h3", "stats0", "stats1", "mean0", "mean1", "xs0", "xs1", "xsT", "logits",
                                  "top0", "top1", "idx0", "idx1", "idx f", "neg top"])
        QR_ACT = steps("qr_act", ["top0", "top1"])
        QR_POOL = steps("qr_pool", ["rstd eps", "rstd"] + [f"onehot{i}" for i in range(4)] + ["chosen"])
        QF_DVE = steps("qf_dve", ["pos", "counts", "pair", "rk", "slot", "slot u", "gate"])
        QF_POOL = steps("qf_pool", ["pos base", "picked0", "picked1", "row ids", "sent"])

        table = sem("table")
        ld_xt = [sem(f"ld_xt{p}") for p in range(2)]
        scattered_y2 = [sem(f"scattered_y2_{p}") for p in range(2)]
        FT_PE = steps("ft_pe", ["xT"])
        FT_DVE = steps("ft_dve", ["xT", "meta"])
        FU_PE = steps("fu_pe", ["gu0", "gu1"])
        FU_ACT = steps("fu_act", ["silu0", "silu1"])
        FU_DVE = steps("fu_dve", ["gu0", "gu1"])
        FH_PE = steps("fh_pe", ["guT0", "guT1"])
        FH_ACT = steps("fh_act", ["guT0", "guT1"])
        FD_PE = steps("fd_pe", ["out"])
        FD_DVE = steps("fd_dve", ["y", "dst"])

        ld_y2 = [sem(f"ld_y2_{c}") for c in range(NT // CH)]
        summed = sem("summed")
        stored = sem("stored")

        block = ctx.enter_context(nc.Block())

        WE = [(dst[:, e:e + E // 2], a[src][:, e:e + E // 2]) for dst, src in ((w1e, "w1e"), (w2e, "w2e"))
              for e in (0, E // 2)] + [(b1e[:], a["b1e"]), (b2e[:], a["b2e"].partition_broadcast(P))]
        W1 = [(ln0[:, 0:1], a["ln0_w"]), (ln0[:, 1:2], a["ln0_b"]), (ln1[:, 0], a["ln1_w"]), (ln1[:, 1], a["ln1_b"]),
              (qkw[:, 0].rearrange("p g c -> p (g c)"), a["qw"]), (qkw[:, 1].rearrange("p g c -> p (g c)"), a["kw"]),
              (qkb[:, 0], a["qb"]), (qkb[:, 1], a["kb"]), (vw[:].rearrange("p h c -> p (h c)"), a["vw"]),
              (w1[:, 0:H1 // 2], a["w1"][:, 0:H1 // 2]), (w1[:, H1 // 2:], a["w1"][:, H1 // 2:]), (b1[:], a["b1"]),
              (w2[:], a["w2"]), (wr2[:], a["wr2"]),
              (vb_bc[:].rearrange("p h c -> p (h c)"), a["vb"].partition_broadcast(P)),
              (b2_bc[:], a["b2"].partition_broadcast(P))]
        N_WE, N_W1 = 16 * len(WE), 16 * len(W1)

        def zeros_in(buffers):
            return sum(-(-buf.shape[0] * buf.shape[1] // P // ZW) for buf in buffers)

        def zero(sp, buffers, done):
            sent = 0
            for buf in buffers:
                flat = buf.rearrange("(p r) x -> p (r x)", p=P)
                for c in range(0, flat.shape[1], ZW):
                    n = min(ZW, flat.shape[1] - c)
                    sp.dma_start(flat[:, c:c + n], zeros[:, 0:n]).then_inc(done, 16)
                    sent += 16
                    sp.wait_ge(done, sent)

        @block.sync
        def _(sp):
            sp.dma_start(ids[:], a["ids"]).then_inc(ld_ids, 16)
            sp.dma_start(wqkv[:].rearrange("p a h c -> p (a h c)"), a["wqkv"]).then_inc(ld_w0, 16)
            sp.dma_start(bqkv[:].rearrange("p a h c -> p (a h c)"), a["bqkv"]).then_inc(ld_w0, 16)
            sp.dma_start(wo[:], a["wo"]).then_inc(ld_w0, 16)
            sp.dma_start(bv_bc[:], a["bv"].partition_broadcast(P)).then_inc(ld_w0, 16)
            sp.dma_start(bo_bc[:], a["bo"].partition_broadcast(P)).then_inc(ld_w0, 16)
            sp.dma_start(wr1[:], a["wr1"]).then_inc(ld_w0, 16)
            sp.dma_start(br_bc[:], a["br"].partition_broadcast(P)).then_inc(ld_w0, 16)
            sp.wait_ge(pool_const, 2)
            for q in range(2):
                sp.wait_ge(embedded[q], 16 * ST)
            zero(sp, (xe1, y1), zeroed1)
            for n, (dst, src) in enumerate(WE):
                sp.dma_start(dst, src).then_inc(ld_we, 16)
                sp.wait_ge(ld_we, 16 * (n + 1))
            for n, (dst, src) in enumerate(W1):
                sp.dma_start(dst, src).then_inc(ld_w1, 16)
                sp.wait_ge(ld_w1, 16 * (n + 1))
            zero(sp, (xe2,), zeroed2)
        N_ZERO1, N_ZERO2 = 16 * zeros_in((xe1, y1)), 16 * zeros_in((xe2,))
        N_W0 = 7 * 16

        @block.gpsimd
        def _(pool):
            for s in (PG_POOL, PA_POOL, PR_POOL, PF_POOL, EX_POOL, QA_POOL, QB_POOL, QC_POOL, QR_POOL, QF_POOL):
                s.start(pool)
            pool.memset(ident[:], 0.0).then_inc(pool_const, 1)
            pool.memset(zeros[:], 0.0).then_inc(pool_const, 1)
            pool.wait_ge(pool_const, 2)
            pool.affine_select(out=ident[:], in_=ident[:], compare_op=ALU.not_equal, fill=1.0, base=0,
                               pattern=[[-1, P]], channel_multiplier=1).then_inc(pool_const, 1)
            pool.memset(half_neg[:], -0.5).then_inc(pool_const, 1)
            pool.memset(eps[:], EPS).then_inc(pool_const, 1)
            pool.iota(iota_i[:, 0:E], [[1, E]], base=0, channel_multiplier=0).then_inc(pool_const, 1)
            pool.iota(iota_i[:, 8:16], [[CAP, E]], base=0, channel_multiplier=0).then_inc(pool_const, 1)
            pool.iota(iota_i[:, 16:24], [[REG, E]], base=0, channel_multiplier=0).then_inc(pool_const, 1)
            pool.iota(iota_i[:, 32:64], [[P, NT], [N, K]], base=-K * N,
                      channel_multiplier=1).then_inc(pool_const, 1)
            pool.iota(row_no[:, 0:1], [[0, 1]], base=0, channel_multiplier=1).then_inc(pool_const, 1)
            pool.memset(before[:], 1.0).then_inc(pool_const, 1)
            pool.memset(causal[:], 1.0).then_inc(pool_const, 1)
            pool.wait_ge(pool_const, 12)
            pool.affine_select(out=before[:], in_=before[:], compare_op=ALU.is_gt, fill=0.0, base=0,
                               pattern=[[1, P]], channel_multiplier=-1).then_inc(pool_const, 1)
            pool.affine_select(out=causal[:], in_=causal[:], compare_op=ALU.is_ge, fill=0.0, base=0,
                               pattern=[[1, P]], channel_multiplier=-1).then_inc(pool_const, 1)
            pool.memset(mask[:, P:], 1.0).then_inc(pool_const, 1)
            pool.wait_ge(pool_const, 14)
            pool.tensor_copy(mask[:, 0:P], causal[:]).then_inc(pool_const, 1)
            pool.iota(t_no_i[:], [[1, TILES2]], base=0, channel_multiplier=0).then_inc(table, 1)
            pool.wait_ge(ld_ids, 16)

        POOL_CONSTS = 16

        @block.vector
        def _(dve):
            for s in (PN_DVE, PA_DVE, PB_DVE, PR_DVE, PF_DVE, EX_W, EX_TD, EX_DD,
                      QA_DVE, QB_DVE, QC_DVE, QR_DVE, QF_DVE, FT_DVE, FU_DVE, FD_DVE):
                s.start(dve)
            dve.memset(w_rep[:], 0.0).then_inc(dve_const, 1)
            dve.memset(b_rep[:], 0.0).then_inc(dve_const, 1)
            dve.memset(one[:], 1.0).then_inc(dve_const, 1)
            dve.memset(ones_bf[:], 1.0).then_inc(dve_const, 1)
            dve.memset(v_ext[:], 1.0).then_inc(dve_const, 1)
            dve.memset(counts[:], 0.0).then_inc(dve_const, 1)
            dve.memset(q_bd[:].bitcast(F32), 0.0).then_inc(dve_const, 1)
            dve.wait_ge(pool_const, 10)
            dve.tensor_copy(expert_no[:], iota_i[:, 0:E]).then_inc(dve_const, 1)
            dve.tensor_copy(slot_base1[:, 0], iota_i[:, 8:16]).then_inc(dve_const, 1)
            dve.tensor_copy(slot_base2[:, 0], iota_i[:, 16:24]).then_inc(dve_const, 1)
            dve.tensor_copy(row_id[:].rearrange("p t k -> p (t k)"), iota_i[:, 32:64]).then_inc(dve_const, 1)
            dve.tensor_scalar(row_no[:, 1:2], row_no[:, 0:1], 48, None, ALU.bitwise_and).then_inc(dve_const, 1)
            dve.tensor_scalar(row_no[:, 2:3], row_no[:, 0:1], H0 - 1, None, ALU.bitwise_and).then_inc(dve_const, 1)
            dve.wait_ge(dve_const, 13)
            dve.tensor_scalar(lo_rows[:, 0:1], row_no[:, 1:2], 32.0, None, ALU.is_equal).then_inc(dve_const, 1)
            dve.tensor_scalar(lo_rows[:, 1:2], row_no[:, 1:2], 16.0, None, ALU.is_equal).then_inc(dve_const, 1)
            dve.tensor_copy(head_of[:], row_no[:, 2:3]).then_inc(dve_const, 1)
            dve.wait_ge(dve_const, 16)
            dve.tensor_scalar(head_eq[:], expert_no[:], head_of[:], None, ALU.is_equal).then_inc(dve_const, 1)
            dve.wait_ge(dve_const, 17)
            dve.tensor_copy(head_rows[:], head_eq[0:2 * H0].unsqueeze(2).broadcast_to([2 * H0, H0, P]))\
               .then_inc(dve_const, 1)
            dve.wait_ge(ld_w0, N_W0)
            for x in range(2):
                for dst, src in ((w_rep, wqkv), (b_rep, bqkv)):
                    rows = dst[:, x].rearrange("p g (q r) -> p (g q) r", q=2)
                    for r in range(3):
                        dve.tensor_copy(rows[:, :, 16 * r:16 * r + 16], src[:, x]).then_inc(dve_const, 1)
            dve.wait_ge(bias_ready, 1)
            dve.tensor_copy(bias_qk[:].rearrange("p x g -> p (x g)"), ps[:, 0, 0:8]).then_inc(dve_const, 1)
            dve.wait_ge(dve_const, 31)
            for x in range(2):
                dve.tensor_scalar(bias_lo[:, x], bias_qk[:, x], lo_rows[:, x:x + 1], None, ALU.mult)\
                   .then_inc(dve_const, 1)

        DVE_CONSTS = 33

        @block.tensor
        def _(pe):
            for s in (PA_PE, PB_PE, PR_PE, EX_T, EX_U, EX_D, QA_PE, QB_PE, QC_PE, QO_PE, QR_PE, QF_PE,
                      FT_PE, FU_PE, FH_PE, FD_PE):
                s.start(pe)
            pe.wait_ge(dve_const, 30)
            for x in range(2):
                for g in range(G0):
                    mm = pe.matmul(ps[:, 0, x * G0 + g:x * G0 + g + 1], b_rep[:, x, g, :], one[:],
                                   start=True, stop=True)
            mm.then_inc(bias_ready, 1)
            pe.wait_ge(pool_const, POOL_CONSTS)

        @block.scalar
        def _(act):
            for s in (PA_ACT, PB_ACT, PR_ACT, EX_UA, QA_ACT, QB_ACT, QC_ACT, QR_ACT, FU_ACT, FH_ACT):
                s.start(act)
            act.wait_ge(dve_const, DVE_CONSTS)

        def choices(pool, own, dve_steps, b):
            pool.wait_ge(*dve_steps.at(b, "idx f"))
            held(pool, held_pool, b)
            for s in range(ST):
                for k in range(K):
                    pool.tensor_scalar(onehot[:, s, k], expert_no[:], idx_f[:, s, k:k + 1], None,
                                       ALU.is_equal).then_inc(*own.step(f"onehot{s * K + k}"))
            pool.wait_ge(*own.at(b, "onehot3"))
            pool.tensor_tensor(chosen[:], onehot[:, :, 0], onehot[:, :, 1], ALU.add)\
                .then_inc(*own.step("chosen"))

        def picks(pool, own, dve_steps, b, p, cap, base):
            pool.wait_ge(*dve_steps.at(b, "pos"))
            if cap is not None:
                held(pool, held_pool, b)
                pool.tensor_scalar(over[:], pos[:], cap, BIG, ALU.is_ge, ALU.mult)\
                    .then_inc(*own.step("over"))
                pool.wait_ge(*own.at(b, "over"))
            pool.tensor_tensor(pos[:], pos[:], base[:].broadcast_to([P, ST, E]), ALU.add)\
                .then_inc(*own.step("pos base"))
            pool.wait_ge(*own.at(b, "pos base"))
            if cap is not None:
                pool.tensor_tensor(pos[:], pos[:], over[:], ALU.add).then_inc(*own.step("pos over"))
                pool.wait_ge(*own.at(b, "pos over"))
            for s in range(ST):
                pool.tensor_tensor(picked[:, s], onehot[:, s],
                                   pos[:, s:s + 1, :].broadcast_to([P, K, E]), ALU.mult)\
                    .then_inc(*own.step(f"picked{s}"))
            pool.tensor_copy(xs[:, p, :, :, D], row_id[:, bass.ds(b * ST, ST), :])\
                .then_inc(*own.step("row ids"))

        def scatter(pool, b, p, dve_steps, rows, n_rows, done):
            pool.wait_ge(*dve_steps.at(b, "gate"))
            held(pool, held_pool, b)
            for s in range(ST):
                for k in range(K):
                    pool.indirect_dma_start(
                        out=rows, out_offset=bass.IndirectOffsetOnAxis(ap=slot_u[:, p, s, k:k + 1], axis=0),
                        in_=xs[:, p, s, k], in_offset=None, bounds_check=n_rows - 1, oob_is_err=False,
                    ).then_inc(done[p], 16)

        def scattered(pool, p, u, own, done):
            pool.wait_ge(done[p], 16 * ST * K * (u + 1))
            pool.sem_inc(*own.step("sent"))

        def row_stats(dve, own, b, rows):
            for s in range(ST):
                dve.bn_stats(stats_b[:, s], rows[s].rearrange("p a d -> p (a d)"))\
                   .then_inc(*own.step(f"stats{s}"))
            dve.wait_ge(*own.at(b, "stats1"))
            held(dve, held_dve, b)
            for s in range(ST):
                dve.bn_aggr(mv_b[:, s], stats_b[:, s]).then_inc(*own.step(f"mean{s}"))

        def norm_rows(dve, own, pool_steps, send_steps, b, p, rows):
            dve.wait_ge(*pool_steps.at(b, "rstd"))
            dve.wait_ge(*send_steps.at(b - 2, "sent"))
            for s in range(ST):
                dve.tensor_scalar(xs[:, p, s, :, 0:D], rows[s].broadcast_to([P, K, D]), mv_b[:, s, 0:1],
                                  rstd_b[:, s:s + 1], ALU.subtract, ALU.mult)\
                   .then_inc(*own.step(f"xs{s}"))

        def choose(dve, own, b):
            dve.wait_ge(*own.at(b, "logits"))
            held(dve, held_dve, b)
            for s in range(ST):
                dve.max(top8[:, s], lg[:, s]).then_inc(*own.step(f"top{s}"))
            dve.wait_ge(*own.at(b, "top1"))
            held(dve, held_dve, b)
            for s in range(ST):
                dve.max_index(idx8[:, s], top8[:, s], lg[:, s]).then_inc(*own.step(f"idx{s}"))
            dve.wait_ge(*own.at(b, "idx1"))
            dve.tensor_copy(idx_f[:], idx8[:, :, 0:K]).then_inc(*own.step("idx f"))
            dve.tensor_scalar(neg_top[:], top8[:, :, 0], -1.0, None, ALU.mult)\
               .then_inc(*own.step("neg top"))

        def place(dve, own, pe_steps, b, layer, bank):
            dve.wait_ge(*pe_steps.at(b, "pos"))
            o = L + 32
            dve.tensor_tensor(pos[:], ps[:, bank, o:o + ST * E].rearrange("p (s e) -> p s e", s=ST),
                              counts[:, layer:layer + 1].broadcast_to([P, ST, E]), ALU.add)\
               .then_inc(*own.step("pos"))
            dve.wait_ge(*own.at(b, "pos"))
            dve.tensor_tensor(counts[:, layer], ps[:, bank, o + ST * E:o + (ST + 1) * E], counts[:, layer],
                              ALU.add).then_inc(*own.step("counts"))

        def route_turn(pe, own, dve_steps, b, p):
            pe.wait_ge(*dve_steps.at(b, "xs1"))
            for s in range(ST):
                mm = pe.transpose(ps[:, 7, s * P:(s + 1) * P], xs[:, p, s, 0, 0:D], ident[:])
            mm.then_inc(*own.step("xsT"))

        def route_logits(pe, own, dve_steps, b, wr):
            pe.wait_ge(*dve_steps.at(b, "xsT"))
            for s in range(ST):
                mm = pe.matmul(ps[:, 7, L + s * E:L + (s + 1) * E], xsT[:, s * P:(s + 1) * P], wr[:],
                               start=True, stop=True)
            mm.then_inc(*own.step("logits"))

        def route_places(pe, own, pool_steps, b, bank):
            pe.wait_ge(*pool_steps.at(b, "chosen"))
            o = L + 32
            pe.matmul(ps[:, bank, o:o + E], before[:], chosen[:, 0], start=True, stop=True)
            pe.matmul(ps[:, bank, o + E:o + 2 * E], before[:], chosen[:, 1], start=True, stop=False)
            pe.matmul(ps[:, bank, o + E:o + 2 * E], ones_bf[:], chosen[:, 0], start=False, stop=True)
            pe.matmul(ps[:, bank, o + 2 * E:o + 3 * E], ones_bf[:], chosen[:, 0], start=True, stop=False)
            pe.matmul(ps[:, bank, o + 2 * E:o + 3 * E], ones_bf[:], chosen[:, 1], start=False, stop=True)\
              .then_inc(*own.step("pos"))

        @block.gpsimd
        def _(pool):
            def gather(b, p, u):
                pool.wait_ge(*PN_DVE.at(b - 2, "xn1"))
                pool.wait_ge(*PA_POOL.at(b - 2, "residual"))
                pool.tensor_copy(ids_s[:, p], ids[:, bass.ds(b * ST, ST)]).then_inc(*PG_POOL.step("ids"))
                pool.wait_ge(*PG_POOL.at(b, "ids"))
                held(pool, held_pool, b)
                for s in range(ST):
                    pool.indirect_dma_start(
                        out=emb[:, p, s], out_offset=None, in_=a["embed"],
                        in_offset=bass.IndirectOffsetOnAxis(ap=ids_s[:, p, s:s + 1].bitcast(U32), axis=0),
                    ).then_inc(embedded[p], 16)

            def norm_keys(b, p, u):
                pool.wait_ge(*PN_DVE.at(b, "mean1"))
                pool.tensor_tensor(rstd[:], mv[:, :, 1], eps[:], ALU.add).then_inc(*PA_POOL.step("rstd eps"))
                pool.wait_ge(*PA_POOL.at(b, "rstd eps"))
                pool.tensor_tensor(rstd[:], rstd[:], half_neg[:], ALU.pow).then_inc(*PA_POOL.step("rstd"))

            def residual(b, p, u):
                pool.wait_ge(embedded[p], 16 * ST * (u + 1))
                pool.tensor_tensor(h[:, bass.ds(b * ST, ST), :], emb[:, p],
                                   bo_bc[:].unsqueeze(1).broadcast_to([P, ST, D]), ALU.add)\
                    .then_inc(*PA_POOL.step("residual"))

            def norm_route(b, p, u):
                pool.wait_ge(*PR_DVE.at(b, "mean1"))
                pool.tensor_tensor(rstd_b[:], mv_b[:, :, 1], eps[:], ALU.add)\
                    .then_inc(*PR_POOL.step("rstd eps"))
                pool.wait_ge(*PR_POOL.at(b, "rstd eps"))
                pool.tensor_tensor(rstd_b[:], rstd_b[:], half_neg[:], ALU.pow)\
                    .then_inc(*PR_POOL.step("rstd"))

            def rows_of(b, p, u):
                choices(pool, PR_POOL, PR_DVE, b)
                picks(pool, PR_POOL, PR_DVE, b, p, float(CAP), slot_base1)

            def send(b, p, u):
                pool.wait_ge(zeroed1, N_ZERO1)
                scatter(pool, b, p, PF_DVE, xe1, E * CAP, scattered1)

            def sent(b, p, u):
                scattered(pool, p, u, PF_POOL, scattered1)

            pool.wait_ge(ld_w0, N_W0)
            skewed(pool, [(norm_route, 3), (residual, 1), (gather, 0), (send, 4), (norm_keys, 0), (rows_of, 3),
                          (sent, 4)], B)

        @block.vector
        def _(dve):
            def stats_keys(b, p, u):
                dve.wait_ge(embedded[p], 16 * ST * (u + 1))
                for s in range(ST):
                    dve.bn_stats(stats[:, s], emb[:, p, s]).then_inc(*PN_DVE.step(f"stats{s}"))
                dve.wait_ge(*PN_DVE.at(b, "stats1"))
                held(dve, held_dve, b)
                for s in range(ST):
                    dve.bn_aggr(mv[:, s], stats[:, s]).then_inc(*PN_DVE.step(f"mean{s}"))

            def norm_keys(b, p, u):
                dve.wait_ge(*PA_POOL.at(b, "rstd"))
                for s in range(ST):
                    dve.tensor_scalar(xn[:, p, s], emb[:, p, s], mv[:, s, 0:1], rstd[:, s:s + 1],
                                      ALU.subtract, ALU.mult).then_inc(*PN_DVE.step(f"xn{s}"))

            def turned(b, p, u):
                dve.wait_ge(*PA_PE.at(b, "xT"))
                dve.tensor_copy(xT[:, p], ps[:, 0, 0:L]).then_inc(*PA_DVE.step("xT"))

            def keys(b, p, u):
                for g in range(G0):
                    dve.wait_ge(*PA_ACT.at(b, f"hi k{g | 1}"))
                    dve.scalar_tensor_tensor(k_op[:, p, g], ps[:, 1 + g // 2, (g % 2) * L:(g % 2 + 1) * L],
                                             bias_qk[:, 1, g:g + 1], hi_t[:, g].bitcast(F32), ALU.add,
                                             ALU.subtract).then_inc(*PA_DVE.step(f"k{g}"))

            def queries(b, p, u):
                for g in range(G0):
                    dve.wait_ge(*PA_ACT.at(b, f"hi q{g | 1}"))
                    for q in range(2):
                        r = slice(64 * q, 64 * q + 64)
                        dve.scalar_tensor_tensor(
                            q_bd[r, p, g, q], ps[r, 1 + g // 2, (g % 2) * L:(g % 2 + 1) * L],
                            bias_qk[r, 0, g:g + 1], hi_t[r, G0 + g].bitcast(F32), ALU.add, ALU.subtract,
                        ).then_inc(*PA_DVE.step(f"q{g}{'ab'[q]}"))

            def values(b, p, u):
                dve.wait_ge(*PA_PE.at(b, "v"))
                dve.tensor_tensor(v_ext[:, p, :, :, 0:C0],
                                  ps[:, 0, L:2 * L].rearrange("p (s h c) -> p s h c", s=ST, h=H0),
                                  bv_bc[:].rearrange("p (s h c) -> p s h c", s=1, h=H0)
                                  .broadcast_to([P, ST, H0, C0]), ALU.add).then_inc(*PA_DVE.step("v"))

            def maxima(groups):
                def part(b, p, u):
                    for g in groups:
                        dve.wait_ge(*PA_PE.at(b, f"scores{g}"))
                        bank = 3 + 2 * (g % 2)
                        dve.tensor_reduce(mx[:, p, :, g, :],
                                          ps[:, bank:bank + 2].rearrange("p s (q t) -> p s q t", q=2), AX,
                                          ALU.max).then_inc(*PA_DVE.step(f"max{g}"))
                return part

            def less_parts(b, p, u):
                dve.wait_ge(*PB_PE.at(b - 1, "maxT"))
                dve.wait_ge(*PA_DVE.at(b, f"max{G0 - 1}"))
                rows = mx[:, p].rearrange("p s g q -> p s (g q)")
                dve.tensor_scalar(m16[:, :, 0:H0].bitcast(F32R), rows, -1.0, None, ALU.mult)\
                   .then_inc(*PA_DVE.step("max hi"))
                dve.wait_ge(*PA_DVE.at(b, "max hi"))
                dve.scalar_tensor_tensor(m16[:, :, H0:].bitcast(F32R), rows, -1.0, m16[:, :, 0:H0],
                                         ALU.mult, ALU.subtract).then_inc(*PA_DVE.step("max lo"))

            def contexts(b, p, u):
                dve.wait_ge(*PB_PE.at(b, "ct"))
                heads = ps[:, 7].rearrange("p (s h c) -> p (s h) c", s=ST, h=H0)
                dve.reciprocal(rden[:].rearrange("p s h c -> p (s h) c"), heads[:, :, C0:C0 + 1])\
                   .then_inc(*PB_DVE.step("rden"))
                dve.wait_ge(*PB_DVE.at(b, "rden"))
                dve.tensor_tensor(cn[:].rearrange("p s h c -> p (s h) c"), heads[:, :, 0:C0],
                                  rden[:].rearrange("p s h c -> p (s h) c").broadcast_to([P, ST * H0, C0]),
                                  ALU.mult).then_inc(*PB_DVE.step("cn"))

            def residual(b, p, u):
                rows = h[:, bass.ds(b * ST, ST), :]
                dve.wait_ge(*PB_PE.at(b, "out"))
                dve.wait_ge(*PA_POOL.at(b, "residual"))
                dve.tensor_tensor(rows, ps[:, 7, L:2 * L].rearrange("p (s d) -> p s d", s=ST), rows, ALU.add)\
                   .then_inc(*PR_DVE.step("residual"))
                dve.wait_ge(*PR_DVE.at(b, "residual"))
                held(dve, held_dve, b)
                row_stats(dve, PR_DVE, b, [h[:, bass.ds(b * ST + s, 1), :] for s in range(ST)])

            def rows_norm(b, p, u):
                norm_rows(dve, PR_DVE, PR_POOL, PF_POOL, b, p, [h[:, bass.ds(b * ST + s, 1), :] for s in range(ST)])

            def rows_turned(b, p, u):
                dve.wait_ge(*PR_PE.at(b, "xsT"))
                dve.tensor_copy(xsT[:], ps[:, 7, 0:L]).then_inc(*PR_DVE.step("xsT"))

            def pick(b, p, u):
                dve.wait_ge(*PR_PE.at(b, "logits"))
                dve.tensor_tensor(lg[:], ps[:, 7, L:L + ST * E].rearrange("p (s e) -> p s e", s=ST),
                                  br_bc[:].unsqueeze(1).broadcast_to([P, ST, E]), ALU.add)\
                   .then_inc(*PR_DVE.step("logits"))
                choose(dve, PR_DVE, b)

            def placed(b, p, u):
                place(dve, PR_DVE, PR_PE, b, 0, 0)

            def finish(b, p, u):
                own = PF_DVE
                dve.wait_ge(*PR_ACT.at(b, "top1"))
                dve.tensor_reduce(pair_sum[:], e_top[:], AX, ALU.add).then_inc(*own.step("pair"))
                dve.wait_ge(*PR_POOL.at(b, "row ids"))
                dve.tensor_reduce(slot[:], picked[:], AX, ALU.add).then_inc(*own.step("slot"))
                dve.wait_ge(*own.at(b, "slot"))
                dve.scalar_tensor_tensor(pair_sum[:], z_all[:], 1e-9, pair_sum[:], ALU.mult, ALU.add)\
                   .then_inc(*own.step("pair eps"))
                dve.tensor_scalar(keep[:], slot[:], BIG / 2, None, ALU.is_lt).then_inc(*own.step("keep"))
                dve.tensor_copy(slot_u[:, p], slot[:]).then_inc(*own.step("slot u"))
                dve.wait_ge(*own.at(b, "keep"))
                dve.tensor_tensor(kept[:], e_top[:], keep[:], ALU.mult).then_inc(*own.step("kept"))
                dve.wait_ge(*own.at(b, "kept"))
                dve.tensor_reduce(kept_sum[:], kept[:], AX, ALU.add).then_inc(*own.step("kept sum"))
                dve.wait_ge(*own.at(b, "kept sum"))
                dve.scalar_tensor_tensor(kept_sum[:], pair_sum[:], 1e-9, kept_sum[:], ALU.mult, ALU.add)\
                   .then_inc(*own.step("kept eps"))
                dve.wait_ge(*own.at(b, "kept eps"))
                dve.reciprocal(rk[:], kept_sum[:]).then_inc(*own.step("rkept"))
                dve.wait_ge(*own.at(b, "rkept"))
                dve.tensor_tensor(xs[:, p, :, :, D + 1], kept[:], rk[:].unsqueeze(2).broadcast_to([P, ST, K]),
                                  ALU.mult).then_inc(*own.step("gate"))

            skewed(dve, [(turned, 1), (finish, 4), (residual, 3), (rows_norm, 3), (keys, 1), (rows_turned, 3),
                         (stats_keys, 0), (pick, 3), (queries, 1), (values, 1), (norm_keys, 0),
                         (maxima((0,)), 1), (contexts, 2), (maxima((1,)), 1), (placed, 3), (maxima((2, 3)), 1),
                         (less_parts, 1)], B)

        @block.scalar
        def _(act):
            def high(name, x, groups):
                def part(b, p, u):
                    for g in groups:
                        act.wait_ge(*PA_PE.at(b, f"{name}{g | 1}"))
                        act.activation(hi_t[:, (1 - x) * G0 + g],
                                       ps[:, 1 + g // 2, (g % 2) * L:(g % 2 + 1) * L], ACT.Identity,
                                       bias=bias_lo[:, x, g:g + 1], scale=lo_rows[:, x:x + 1])\
                           .then_inc(*PA_ACT.step(f"hi {name}{g}"))
                return part

            def maxima(b, p, u):
                act.wait_ge(*PB_PE.at(b, "maxT"))
                act.activation(mT[:], ps[0:2 * H0, 1, 0:L], ACT.Identity).then_inc(*PB_ACT.step("mT"))

            def exps(groups):
                def part(b, p, u):
                    for g in groups:
                        act.wait_ge(*PB_PE.at(b, f"scores{g}"))
                        bank = 3 + 2 * (g % 2)
                        act.activation(pT[:, g].rearrange("p s q t -> p (s q t)"),
                                       ps[:, bank:bank + 2].rearrange("p s t -> p (s t)"), ACT.Exp,
                                       scale=float(C0) ** -0.5).then_inc(*PB_ACT.step(f"exp{g}"))
                return part

            def sums(b, p, u):
                act.wait_ge(*PB_PE.at(b, "pv"))
                act.activation(pv_sb[:].rearrange("p g t -> p (g t)"), ps[:, 7], ACT.Identity)\
                   .then_inc(*PB_ACT.step("pv"))

            def contexts(b, p, u):
                act.wait_ge(*PB_PE.at(b, "cT"))
                act.activation(cT[:], ps[:, 7, 0:L], ACT.Identity).then_inc(*PB_ACT.step("cT"))

            def weights(b, p, u):
                act.wait_ge(*PR_DVE.at(b, "neg top"))
                for s in range(ST):
                    act.activation(e_all[:, s], lg[:, s], ACT.Exp, bias=neg_top[:, s:s + 1],
                                   accum_out=z_all[:, s:s + 1]).then_inc(*PR_ACT.step(f"z{s}"))
                for s in range(ST):
                    act.activation(e_top[:, s], top8[:, s, 0:K], ACT.Exp, bias=neg_top[:, s:s + 1])\
                       .then_inc(*PR_ACT.step(f"top{s}"))

            skewed(act, [(maxima, 2), (exps((0, 1)), 2), (high("k", 1, range(G0)), 1), (exps((2, 3)), 2),
                         (high("q", 0, range(G0)), 1), (sums, 2), (weights, 3), (contexts, 2)], B)

        @block.tensor
        def _(pe):
            def turn(b, p, u):
                pe.wait_ge(*PN_DVE.at(b, "xn1"))
                for s in range(ST):
                    mm = pe.transpose(ps[:, 0, s * P:(s + 1) * P], xn[:, p, s], ident[:])
                mm.then_inc(*PA_PE.step("xT"))

            def project(name, x, groups):
                def part(b, p, u):
                    if name == "k" and groups[0] == 0:
                        pe.wait_ge(*PA_DVE.at(b, "xT"))
                        pe.wait_ge(*PB_ACT.at(b - 1, "mT"))
                    for g in groups:
                        if name == "q":
                            pe.wait_ge(*PA_DVE.at(b, f"k{g | 1}"))
                        pe.matmul(ps[:, 1 + g // 2, (g % 2) * L:(g % 2 + 1) * L], w_rep[:, x, g], xT[:, p],
                                  start=True, stop=True).then_inc(*PA_PE.step(f"{name}{g}"))
                return part

            def values(b, p, u):
                for s in range(ST):
                    mm = pe.matmul(ps[:, 0, L + s * P:L + (s + 1) * P], xT[:, p, s * P:(s + 1) * P],
                                   wqkv[:, 2].rearrange("p h c -> p (h c)"), start=True, stop=True)
                mm.then_inc(*PA_PE.step("v"))

            def row_scores(groups):
                def part(b, p, u):
                    for g in groups:
                        if g < 2:
                            pe.wait_ge(*PA_DVE.at(b, f"q{g}b"))
                            pe.wait_ge(*PB_ACT.at(b - 1, f"exp{g + 2}"))
                        else:
                            pe.wait_ge(*PA_DVE.at(b, f"max{g - 2}"))
                        for s in range(ST):
                            for q in range(2):
                                mm = pe.matmul(ps[:, 3 + 2 * (g % 2) + s, q * L:(q + 1) * L],
                                               q_bd[:, p, g, q, s * P:(s + 1) * P], k_op[:, p, g],
                                               start=True, stop=True)
                        mm.then_inc(*PA_PE.step(f"scores{g}"))
                return part

            def turn_max(b, p, u):
                pe.wait_ge(*PA_DVE.at(b, "max lo"))
                for s in range(ST):
                    mm = pe.transpose(ps[0:2 * H0, 1, s * P:(s + 1) * P], m16[:, s], ident[:])
                mm.then_inc(*PB_PE.step("maxT"))

            def scores(groups):
                def part(b, p, u):
                    for g in groups:
                        if g < 2:
                            pe.wait_ge(*PB_ACT.at(b, "mT"))
                        else:
                            pe.wait_ge(*PB_ACT.at(b, f"exp{g - 2}"))
                        for s in range(ST):
                            bank = ps[:, 3 + 2 * (g % 2) + s]
                            pe.matmul(bank, k_op[:, p, g, s * P:(s + 1) * P],
                                      q_bd[:, p, g].rearrange("p q t -> p (q t)"), start=True, stop=False)
                            for q in range(2):
                                mm = pe.matmul(bank[:, q * L:(q + 1) * L], head_rows[:, 2 * g + q], mT[:],
                                               start=False, stop=(q == 1))
                        mm.then_inc(*PB_PE.step(f"scores{g}"))
                return part

            def weigh(b, p, u):
                pe.wait_ge(*PB_ACT.at(b, "exp3"))
                pe.wait_ge(*PR_DVE.at(b - 1, "logits"))
                for hd in range(H0):
                    j = hd % 4
                    for s in range(ST):
                        mm = pe.matmul(ps[32 * j:32 * j + 32, 7, (hd // 4) * L:(hd // 4 + 1) * L],
                                       v_ext[:, p, s, hd], pT[:, hd // 2, s, hd % 2], start=(s == 0),
                                       stop=(s == ST - 1))
                mm.then_inc(*PB_PE.step("pv"))

            def turn_sums(b, p, u):
                pe.wait_ge(*PB_ACT.at(b, "pv"))
                for s in range(ST):
                    for g in range(2):
                        mm = pe.transpose(ps[:, 7, s * L + g * P:s * L + (g + 1) * P],
                                          pv_sb[:, g, s * P:(s + 1) * P], ident[:])
                mm.then_inc(*PB_PE.step("ct"))

            def turn_contexts(b, p, u):
                pe.wait_ge(*PB_DVE.at(b, "cn"))
                for s in range(ST):
                    mm = pe.transpose(ps[:, 7, s * P:(s + 1) * P], cn[:, s].rearrange("p h c -> p (h c)"),
                                      ident[:])
                mm.then_inc(*PB_PE.step("cT"))

            def outputs(b, p, u):
                pe.wait_ge(*PB_ACT.at(b, "cT"))
                for s in range(ST):
                    mm = pe.matmul(ps[:, 7, L + s * P:L + (s + 1) * P], cT[:, s * P:(s + 1) * P], wo[:],
                                   start=True, stop=True)
                mm.then_inc(*PB_PE.step("out"))

            def rows_turn(b, p, u):
                route_turn(pe, PR_PE, PR_DVE, b, p)

            def logits(b, p, u):
                route_logits(pe, PR_PE, PR_DVE, b, wr1)

            def places(b, p, u):
                if not isinstance(b, int) or b + 2 < B:
                    pe.wait_ge(*PA_DVE.at(b + 2, "v"))
                route_places(pe, PR_PE, PR_POOL, b, 0)

            skewed(pe, [(turn_max, 2), (turn, 1), (scores((0, 1)), 2), (project("k", 1, range(G0)), 1),
                        (scores((2,)), 2), (rows_turn, 3), (scores((3,)), 2), (logits, 3),
                        (project("q", 0, range(G0)), 1), (values, 1), (weigh, 2), (row_scores((0, 1)), 1),
                        (turn_sums, 2), (row_scores((2,)), 1), (places, 3), (turn_contexts, 2),
                        (row_scores((3,)), 1), (outputs, 2)], B)

        N_SENT1 = 16 * ST * K * B // 2
        HALF = CAP // 2

        @block.sync
        def _(sp):
            def load(e, p, u):
                sp.wait_ge(*EX_DD.at(e - 2, "weighted b"))
                sp.dma_start(xe[:, p], xe1.rearrange("(e j p) x -> e p j x", e=E, j=CT)[bass.ds(e, 1)]
                             .rearrange("e p j x -> (e p) j x")).then_inc(ld_xe[p], 16)

            for q in range(2):
                sp.wait_ge(scattered1[q], N_SENT1)
            skewed(sp, [(load, 0)], E)

        @block.tensor
        def _(pe):
            pe.wait_ge(ld_w1, N_W1)
            pe.wait_ge(*PR_DVE.at(B - 1, "logits"))
            for f in range(F1 // P):
                for hd in range(H1):
                    mm = pe.matmul(ps[:, 7, f:f + 1], w1[:, hd, f * P:(f + 1) * P], ln1[:, 1, hd:hd + 1],
                                   start=(hd == 0), stop=(hd == H1 - 1))
            mm.then_inc(b1_ready, 1)
            pe.wait_ge(*PR_DVE.at(B - 1, "counts"))

            def turn(e, p, u):
                pe.wait_ge(ld_xe[p], 16 * (u + 1))
                pe.wait_ge(*EX_TD.at(e - 1, "xT tail"))
                for j in range(4):
                    mm = pe.transpose(ps[:, 0, j * P:(j + 1) * P], xe[:, p, j, 0:D], ident[:])
                mm.then_inc(*EX_T.step("xT"))
                pe.transpose(ps[:, 1, 0:P], xe[:, p, 4, 0:D], ident[:]).then_inc(*EX_T.step("xT tail"))

            def up(e, p, u):
                pe.wait_ge(*EX_TD.at(e, "xT tail"))
                pe.wait_ge(*EX_W.at(e, "b1"))
                for n in range(2 * FT):
                    f, half = n // 2, n % 2
                    pe.wait_ge(*(EX_UA.at(e - 1, f"gelu{n + 4}") if n < 4 else EX_UA.at(e, f"gelu{n - 4}")))
                    pe.matmul(ps[:, 2 + n % 4, 0:HALF], w1_p[:, p, f * P:(f + 1) * P],
                              xeT[:, p, half * HALF:(half + 1) * HALF], start=True, stop=True)\
                      .then_inc(*EX_U.step(f"up{n}"))

            def down(e, p, u):
                pe.wait_ge(*EX_UA.at(e, f"gelu{2 * FT - 1}"))
                for j in range(CT):
                    half = int(j >= HEAD)
                    pe.wait_ge(*EX_DD.at(e - 1, "b2 " + "ab"[half]))
                    for f in range(FT):
                        mm = pe.matmul(ps[:, 6 + half, (j - half * HEAD) * P:(j - half * HEAD + 1) * P],
                                       hT[:, p, f, j * P:(j + 1) * P],
                                       w2e[:, bass.ds(e, 1), f].rearrange("p e d -> p (e d)"), start=(f == 0),
                                       stop=(f == FT - 1))
                    if j == HEAD - 1:
                        mm.then_inc(*EX_D.step("down a"))
                mm.then_inc(*EX_D.step("down b"))

            skewed(pe, [(up, 1), (turn, 0), (down, 1)], E)

        @block.scalar
        def _(act):
            act.activation(first_use[:], one[:], ACT.Gelu)

            def up(e, p, u):
                act.wait_ge(*EX_D.at(e - 2, "down b"))
                act.wait_ge(*EX_W.at(e, "b1"))
                for n in range(2 * FT):
                    f, half = n // 2, n % 2
                    act.wait_ge(*EX_U.at(e, f"up{n}"))
                    act.activation(hT[:, p, f, half * HALF:(half + 1) * HALF], ps[:, 2 + n % 4, 0:HALF],
                                   ACT.Gelu, bias=b1_p[:, p, f:f + 1]).then_inc(*EX_UA.step(f"gelu{n}"))

            skewed(act, [(up, 1)], E)
            act.wait_ge(*EX_W.at(E - 1, "w1"))
            act.activation(w1_hi[:], w1[:], ACT.Identity).then_inc(w1_split, 1)

        @block.vector
        def _(dve):
            dve.wait_ge(ld_w1, N_W1)
            dve.wait_ge(b1_ready, 1)
            dve.tensor_tensor(b1_all[:], ps[:, 7, 0:4], b1[:], ALU.add).then_inc(l1_const, 1)
            dve.wait_ge(ld_we, N_WE)

            def turn(e, p, u):
                dve.wait_ge(*EX_UA.at(e - 2, f"gelu{2 * FT - 1}"))
                dve.tensor_copy(w1_p[:, p:p + 1], w1e[:, bass.ds(e, 1)]).then_inc(*EX_W.step("w1"))
                dve.tensor_copy(b1_p[:, p:p + 1], b1e[:, bass.ds(e, 1)]).then_inc(*EX_W.step("b1"))
                dve.wait_ge(*EX_T.at(e, "xT"))
                dve.tensor_copy(xeT[:, p, 0:4 * P], ps[:, 0]).then_inc(*EX_TD.step("xT"))
                dve.wait_ge(*EX_T.at(e, "xT tail"))
                dve.tensor_copy(xeT[:, p, 4 * P:], ps[:, 1, 0:P]).then_inc(*EX_TD.step("xT tail"))

            def down(e, p, u):
                b2 = b2e[:, bass.ds(e, 1)]
                dve.wait_ge(*EX_DD.at(e - 1, "weighted b"))
                for half, tiles in enumerate((slice(0, HEAD), slice(HEAD, CT))):
                    n, part = tiles.stop - tiles.start, "ab"[half]
                    dve.wait_ge(*EX_D.at(e, "down " + part))
                    dve.tensor_tensor(yb[:, tiles], ps[:, 6 + half, 0:n * P].rearrange("p (j d) -> p j d", j=n),
                                      b2.broadcast_to([P, n, D]), ALU.add).then_inc(*EX_DD.step("b2 " + part))
                    dve.wait_ge(*EX_DD.at(e, "b2 " + part))
                    dve.wait_ge(*EX_POOL.at(e - 2, "sent"))
                    dve.tensor_tensor(ye[:, p, tiles], yb[:, tiles],
                                      xe[:, p, tiles, D + 1:D + 2].broadcast_to([P, n, D]), ALU.mult)\
                       .then_inc(*EX_DD.step("weighted " + part))
                    if half == 0:
                        dve.tensor_scalar(dst_u[:, p], xe[:, p, :, D], float(K * N), None, ALU.add)\
                           .then_inc(*EX_DD.step("dst"))

            skewed(dve, [(turn, 0), (down, 1)], E)
            dve.wait_ge(w1_split, 1)
            dve.tensor_tensor(w1_lo[:], w1[:], w1_hi[:].bitcast(F32), ALU.subtract)\
               .then_inc(w1_split, 1)

        @block.gpsimd
        def _(pool):
            def send(e, p, u):
                for j in range(CT):
                    if j in (0, HEAD):
                        pool.wait_ge(*EX_DD.at(e, "dst" if j == 0 else "weighted b"))
                        held(pool, held_pool, e)
                    pool.indirect_dma_start(
                        out=y1, out_offset=bass.IndirectOffsetOnAxis(ap=dst_u[:, p, j:j + 1], axis=0),
                        in_=ye[:, p, j], in_offset=None, bounds_check=K * N - 1, oob_is_err=False,
                    ).then_inc(scattered_y1[p], 16)
                pool.wait_ge(scattered_y1[p], 16 * CT * (u + 1))
                pool.sem_inc(*EX_POOL.step("sent"))

            skewed(pool, [(send, 1)], E)

        N_SENT_Y1 = 16 * CT * E // 2
        L1_CONSTS = 4

        @block.sync
        def _(sp):
            for q in range(2):
                sp.wait_ge(scattered_y1[q], N_SENT_Y1)

            def load(b, p, u):
                sp.wait_ge(*QA_DVE.at(b - 2, "h2"))
                for k in range(K):
                    sp.dma_start(yy[:, p, k], y1.rearrange("(k t p) d -> k p t d", k=K, t=NT)
                                 [k][:, bass.ds(b * ST, ST), :]).then_inc(ld_yy[p], 16)

            skewed(sp, [(load, 0)], B)
            sp.wait_ge(*QB_PE.at(B - 1, "s5"))
            sp.dma_start(wgu[:, 0:E // 2], a["wgu"][:, 0:E // 2]).then_inc(ld_wf, 16)
            sp.dma_start(wgu[:, E // 2:], a["wgu"][:, E // 2:]).then_inc(ld_wf, 16)
            sp.wait_ge(*QB_PE.at(B - 1, "o5"))
            sp.dma_start(wd, a["wd"]).then_inc(ld_wf, 16)
        N_WF = 3 * 16


        @block.gpsimd
        def _(pool):
            def low(parts):
                def part(b, p, u):
                    for m in parts:
                        pool.wait_ge(*QC_ACT.at(b, f"hi{m}"))
                        pool.tensor_tensor(y_lo[:, 2 * m:2 * m + 2], yT[:, 2 * m:2 * m + 2],
                                           y_hi[:, 2 * m:2 * m + 2].bitcast(F32), ALU.subtract)\
                            .then_inc(*QC_POOL.step(f"lo{m}"))
                return part

            def norm_outputs(b, p, u):
                pool.wait_ge(*QB_DVE.at(b, "mean1"))
                pool.tensor_tensor(rstd_o[:], mv_o[:, :, 1], eps[:], ALU.add)\
                    .then_inc(*QB_POOL.step("rstd eps"))
                pool.wait_ge(*QB_POOL.at(b, "rstd eps"))
                pool.tensor_tensor(rstd_o[:], rstd_o[:], half_neg[:], ALU.pow).then_inc(*QB_POOL.step("rstd"))

            def norm_keys(name):
                def norm(b, p, u):
                    pool.wait_ge(*QA_DVE.at(b, name + "mean1"))
                    pool.tensor_tensor(rstd_a[:], mv_a[:, :, 1], eps[:], ALU.add)\
                        .then_inc(*QA_POOL.step(name + "rstd eps"))
                    pool.wait_ge(*QA_POOL.at(b, name + "rstd eps"))
                    pool.tensor_tensor(rstd_a[:], rstd_a[:], half_neg[:], ALU.pow)\
                        .then_inc(*QA_POOL.step(name + "rstd"))
                return norm

            def residual(b, p, u):
                rows = h[:, bass.ds(b * ST, ST), :]
                pool.wait_ge(*QA_DVE.at(b, "x1_1"))
                pool.tensor_tensor(rows, rows, x1[:, p], ALU.add).then_inc(*QA_POOL.step("h x1"))

            def norm_route(b, p, u):
                pool.wait_ge(*QR_DVE.at(b, "mean1"))
                pool.tensor_tensor(rstd_b[:], mv_b[:, :, 1], eps[:], ALU.add)\
                    .then_inc(*QR_POOL.step("rstd eps"))
                pool.wait_ge(*QR_POOL.at(b, "rstd eps"))
                pool.tensor_tensor(rstd_b[:], rstd_b[:], half_neg[:], ALU.pow)\
                    .then_inc(*QR_POOL.step("rstd"))

            def chosen_of(b, p, u):
                choices(pool, QR_POOL, QR_DVE, b)

            def rows_of(b, p, u):
                picks(pool, QF_POOL, QF_DVE, b, p, None, slot_base2)

            def send(b, p, u):
                scatter(pool, b, p, QF_DVE, xe2, E * REG, scattered2)

            def sent(b, p, u):
                scattered(pool, p, u, QF_POOL, scattered2)

            pool.memset(v1[:, :, :, :, D:], 1.0).then_inc(l1_const, 1)
            pool.wait_ge(zeroed2, N_ZERO2)

            def masks(b, p, u):
                for n, hs in ((0, slice(0, 2)), (3, slice(4, 6))):
                    pool.wait_ge(*QB_ACT.at(b, f"s{n}"))
                    pool.tensor_tensor(s_T0[:, hs, 0:P], s_T0[:, hs, 0:P],
                                       causal[:].unsqueeze(1).broadcast_to([P, 2, P]), ALU.mult)\
                        .then_inc(*QB_POOL.step(f"mask{n}"))

            first_norm, second_norm = norm_keys(""), norm_keys("n ")
            skewed(pool, [(masks, 1), (rows_of, 4), (first_norm, 0), (low((0, 1)), 2), (norm_outputs, 1),
                          (residual, 0), (second_norm, 0), (low((2,)), 2), (low((3,)), 2), (norm_route, 3),
                          (send, 4), (chosen_of, 3), (sent, 4)], B,
                    opening=[(first_norm, 0), (residual, 0), (second_norm, 0), (masks, 1), (norm_outputs, 1)])

        @block.vector
        def _(dve):

            def stream(b, p, u):
                rows = h[:, bass.ds(b * ST, ST), :]
                dve.wait_ge(ld_yy[p], 16 * K * (u + 1))
                dve.tensor_tensor(yy[:, p, 0], yy[:, p, 0], yy[:, p, 1], ALU.add).then_inc(*QA_DVE.step("add"))
                dve.wait_ge(*QA_DVE.at(b, "add"))
                dve.tensor_tensor(rows, yy[:, p, 0], rows, ALU.add).then_inc(*QA_DVE.step("h2"))
                dve.wait_ge(*QA_DVE.at(b, "h2"))
                held(dve, held_dve, b)
                for s in range(ST):
                    dve.bn_stats(stats_a[:, s], h[:, bass.ds(b * ST + s, 1), :].rearrange("p a d -> p (a d)"))\
                       .then_inc(*QA_DVE.step(f"stats{s}"))
                dve.wait_ge(*QA_DVE.at(b, "stats1"))
                held(dve, held_dve, b)
                for s in range(ST):
                    dve.bn_aggr(mv_a[:, s], stats_a[:, s]).then_inc(*QA_DVE.step(f"mean{s}"))

            def norm1(b, p, u):
                dve.wait_ge(*QA_POOL.at(b, "rstd"))
                for s in range(ST):
                    dve.tensor_scalar(x1[:, p, s:s + 1], h[:, bass.ds(b * ST + s, 1), :], mv_a[:, s, 0:1],
                                      rstd_a[:, s:s + 1], ALU.subtract, ALU.mult)\
                       .then_inc(*QA_DVE.step(f"x1_{s}"))
                dve.wait_ge(*QA_DVE.at(b, "x1_1"))
                for s in range(ST):
                    dve.bn_stats(stats_a[:, s], x1[:, p, s]).then_inc(*QA_DVE.step(f"n stats{s}"))
                dve.wait_ge(*QA_DVE.at(b, "n stats1"))
                held(dve, held_dve, b)
                for s in range(ST):
                    dve.bn_aggr(mv_a[:, s], stats_a[:, s]).then_inc(*QA_DVE.step(f"n mean{s}"))

            def norm2(b, p, u):
                dve.wait_ge(*QA_POOL.at(b, "n rstd"))
                for s in range(ST):
                    dve.tensor_scalar(n0[:, s], x1[:, p, s], mv_a[:, s, 0:1], rstd_a[:, s:s + 1],
                                      ALU.subtract, ALU.mult).then_inc(*QA_DVE.step(f"n0_{s}"))

            def turned(b, p, u):
                dve.wait_ge(*QA_PE.at(b, "xT"))
                dve.tensor_copy(x1T[:, p], ps[:, 0, 0:L]).then_inc(*QA_DVE.step("x1T"))
                dve.tensor_scalar(x0T[:], ps[:, 0, L:], ln0[:, 0:1], ln0[:, 1:2], ALU.mult, ALU.add)\
                   .then_inc(*QA_DVE.step("x0T"))

            def clip(b, p, u):
                if isinstance(b, int) and b == 0:
                    dve.wait_ge(l1_const, L1_CONSTS)
                lo, hi = float(np.exp(np.float32(-10))), float(np.exp(np.float32(10)))
                for g in range(G1):
                    dve.wait_ge(*QA_ACT.at(b, f"k{g}"))
                    dve.tensor_scalar(k_T1[:, p, g], exp_k[:, g], hi, lo, ALU.min, ALU.max)\
                       .then_inc(*QA_DVE.step(f"k{g}"))
                for g in range(G1):
                    dve.wait_ge(*QA_ACT.at(b, f"q{g}"))
                    for q in range(4):
                        r = slice(32 * q, 32 * q + 32)
                        dve.tensor_scalar(q_bd1[r, p, g, q], exp_q[r, g], hi, lo, ALU.min, ALU.max)\
                           .then_inc(*QA_DVE.step(f"q{g}{q}"))

            def scores(b, p, u):
                dve.wait_ge(*QB_DVE.at(b - 1, "n1"))
                for n in (1, 2, 4, 5):
                    g, m = n // 3, n % 3
                    dve.wait_ge(*QB_PE.at(b, f"s{n}"))
                    bank = ps[:, 3 + n % 4]
                    if m < 2:
                        hs = slice(4 * g + 2 * m, 4 * g + 2 * m + 2)
                        dve.tensor_tensor(s_T0[:, hs], bank.rearrange("p (h l) -> p h l", h=2),
                                          mask[:].unsqueeze(1).broadcast_to([P, 2, L]), ALU.mult)\
                           .then_inc(*QB_DVE.step(f"s{n}"))
                    else:
                        dve.tensor_tensor(s_T1[:, 4 * g:4 * g + 4], bank.rearrange("p (h l) -> p h l", h=4),
                                          causal[:].unsqueeze(1).broadcast_to([P, 4, P]), ALU.mult)\
                           .then_inc(*QB_DVE.step(f"s{n}"))

            def outputs(b, p, u):
                for n, (s, hs) in enumerate(OUTS):
                    dve.wait_ge(*QB_PE.at(b, f"o{n}"))
                    bank = ps[:, 3 + (n + 2) % 4, 0:(D + 1) * len(hs)].rearrange("p (h d) -> p h d", d=D + 1)
                    dve.reciprocal(r_den[:, n, 0:len(hs)].unsqueeze(2), bank[:, :, D:D + 1])\
                       .then_inc(*QB_DVE.step(f"r{n}"))
                    dve.wait_ge(*QB_DVE.at(b, f"r{n}"))
                    for i, hd in enumerate(hs):
                        dve.scalar_tensor_tensor(o[:, s, hd * D:(hd + 1) * D], bank[:, i, 0:D],
                                                 r_den[:, n, i:i + 1], vb_bc[:, hd], ALU.mult, ALU.add)\
                           .then_inc(*QB_DVE.step(f"o{n}{i}"))

            def output_stats(b, p, u):
                dve.wait_ge(*QB_DVE.at(b, "o51"))
                for s in range(ST):
                    for c in range(2):
                        dve.bn_stats(stats_o[:, s, c], o[:, s, 512 * c:512 * c + 512])\
                           .then_inc(*QB_DVE.step(f"stats{s}{c}"))
                dve.wait_ge(*QB_DVE.at(b, "stats11"))
                held(dve, held_dve, b)
                for s in range(ST):
                    dve.bn_aggr(mv_o[:, s], stats_o[:, s].rearrange("p c x -> p (c x)"))\
                       .then_inc(*QB_DVE.step(f"mean{s}"))

            def norm_outputs(b, p, u):
                dve.wait_ge(*QB_POOL.at(b, "rstd"))
                dve.wait_ge(*QC_PE.at(b - 1, "y3"))
                for s in range(ST):
                    dve.tensor_scalar(on[:, s].rearrange("p h d -> p (h d)"), o[:, s], mv_o[:, s, 0:1],
                                      rstd_o[:, s:s + 1], ALU.subtract, ALU.mult)\
                       .then_inc(*QB_DVE.step(f"n{s}"))

            def features(heads):
                def part(b, p, u):
                    for n in heads:
                        dve.wait_ge(*QC_PE.at(b, f"y{n // 2}"))
                        dve.scalar_tensor_tensor(yT[:, n], ps[:, 1 + n // 2 % 2, (n % 2) * L:(n % 2 + 1) * L],
                                                 ln1[:, 0, n:n + 1], x1T[:, p], ALU.mult, ALU.add)\
                           .then_inc(*QC_DVE.step(f"y{n}"))
                return part

            def residual(b, p, u):
                rows = h[:, bass.ds(b * ST, ST), :]
                dve.wait_ge(*QO_PE.at(b, "out"))
                dve.tensor_tensor(att[:], ps[:, 0, 0:L].rearrange("p (s d) -> p s d", s=ST),
                                  b2_bc[:].unsqueeze(1).broadcast_to([P, ST, D]), ALU.add)\
                   .then_inc(*QR_DVE.step("b2"))
                dve.wait_ge(*QA_POOL.at(b, "h x1"))
                dve.wait_ge(*QR_DVE.at(b, "b2"))
                dve.scalar_tensor_tensor(rows, att[:], 0.0, rows, ALU.max, ALU.add)\
                   .then_inc(*QR_DVE.step("h3"))
                dve.wait_ge(*QR_DVE.at(b, "h3"))
                held(dve, held_dve, b)
                row_stats(dve, QR_DVE, b, [h[:, bass.ds(b * ST + s, 1), :] for s in range(ST)])

            def rows_norm(b, p, u):
                norm_rows(dve, QR_DVE, QR_POOL, QF_POOL, b, p, [h[:, bass.ds(b * ST + s, 1), :] for s in range(ST)])

            def rows_turned(b, p, u):
                dve.wait_ge(*QR_PE.at(b, "xsT"))
                dve.tensor_copy(xsT[:], ps[:, 7, 0:L]).then_inc(*QR_DVE.step("xsT"))

            def pick(b, p, u):
                dve.wait_ge(*QR_PE.at(b, "logits"))
                dve.tensor_copy(lg[:].rearrange("p s e -> p (s e)"), ps[:, 7, L:L + ST * E])\
                   .then_inc(*QR_DVE.step("logits"))
                choose(dve, QR_DVE, b)

            def placed(b, p, u):
                place(dve, QF_DVE, QF_PE, b, 1, 7)

            def finish(b, p, u):
                own = QF_DVE
                dve.wait_ge(*QR_ACT.at(b, "top1"))
                dve.tensor_reduce(pair_sum[:], e_top[:], AX, ALU.add).then_inc(*own.step("pair"))
                dve.wait_ge(*own.at(b, "pair"))
                dve.reciprocal(rk[:], pair_sum[:]).then_inc(*own.step("rk"))
                dve.wait_ge(*QF_POOL.at(b, "row ids"))
                dve.tensor_reduce(slot[:], picked[:], AX, ALU.add).then_inc(*own.step("slot"))
                dve.wait_ge(*own.at(b, "slot"))
                dve.tensor_copy(slot_u[:, p], slot[:]).then_inc(*own.step("slot u"))
                dve.tensor_tensor(xs[:, p, :, :, D + 1], e_top[:], rk[:].unsqueeze(2).broadcast_to([P, ST, K]),
                                  ALU.mult).then_inc(*own.step("gate"))

            features03, features45, features67 = features(range(4)), features((4, 5)), features((6, 7))
            skewed(dve, [(stream, 0), (scores, 1), (placed, 4), (outputs, 1), (features03, 2), (finish, 4),
                         (output_stats, 1), (norm1, 0), (features45, 2), (norm2, 0), (features67, 2),
                         (residual, 3), (norm_outputs, 1), (rows_norm, 3), (turned, 0), (rows_turned, 3),
                         (clip, 0), (pick, 3)], B,
                   opening=[(stream, 0), (norm1, 0), (norm2, 0), (scores, 1), (outputs, 1), (turned, 0), (clip, 0),
                            (output_stats, 1), (norm_outputs, 1)])

        @block.scalar
        def _(act):
            act.activation(first_use[:], one[:], ACT.Exp)
            for p in range(2):
                act.activation(q_bd1[:, p].rearrange("p g q l -> p (g q l)"), zeros[:], ACT.Identity)\
                   .then_inc(l1_const, 1)

            def exps(b, p, u):
                act.wait_ge(*QA_DVE.at(b - 1, "q13"))
                for x, dst, name, bank in ((1, exp_k, "k", 2), (0, exp_q, "q", 1)):
                    act.wait_ge(*QA_PE.at(b, name))
                    for g in range(G1):
                        act.activation(dst[:, g], ps[:, bank, g * L:(g + 1) * L], ACT.Exp,
                                       bias=qkb[:, x, g:g + 1]).then_inc(*QA_ACT.step(f"{name}{g}"))

            def values(b, p, u):
                for n in range(4):
                    s, half = n // 2, n % 2
                    act.wait_ge(*QA_PE.at(b, f"v{n}"))
                    act.activation(v1[:, p, s, 4 * half:4 * half + 4, 0:D],
                                   ps[:, 2 - n % 2].rearrange("p (h d) -> p h d", h=4), ACT.Identity)\
                       .then_inc(*QA_ACT.step(f"v{n}"))

            def scores(b, p, u):
                for n, hs in ((0, slice(0, 2)), (3, slice(4, 6))):
                    act.wait_ge(*QB_PE.at(b, f"s{n}"))
                    act.activation(s_T0[:, hs].rearrange("p h l -> p (h l)"), ps[:, 3 + n], ACT.Identity)\
                       .then_inc(*QB_ACT.step(f"s{n}"))

            def high(parts):
                def part(b, p, u):
                    for m in parts:
                        act.wait_ge(*QC_DVE.at(b, f"y{2 * m + 1}"))
                        act.activation(y_hi[:, 2 * m:2 * m + 2], yT[:, 2 * m:2 * m + 2], ACT.Identity)\
                           .then_inc(*QC_ACT.step(f"hi{m}"))
                return part

            def features(b, p, u):
                act.wait_ge(*QC_PE.at(b, "f"))
                for n in range(4):
                    act.activation(h1T[:, n], ps[:, 3 + n, 0:L], ACT.Relu, bias=b1_all[:, n:n + 1])\
                       .then_inc(*QC_ACT.step(f"f{n}"))

            def weights(b, p, u):
                act.wait_ge(*QR_DVE.at(b, "neg top"))
                for s in range(ST):
                    act.activation(e_top[:, s], top8[:, s, 0:K], ACT.Exp, bias=neg_top[:, s:s + 1])\
                       .then_inc(*QR_ACT.step(f"top{s}"))

            skewed(act, [(scores, 1), (high((0, 1)), 2), (high((2,)), 2), (high((3,)), 2), (exps, 0),
                         (features, 2), (values, 0), (weights, 3)], B)

        @block.tensor
        def _(pe):
            pe.wait_ge(l1_const, L1_CONSTS)
            pe.wait_ge(*EX_DD.at(E - 1, "b2 b"))

            def turn(b, p, u):
                pe.wait_ge(*QA_DVE.at(b, "n0_1"))
                pe.wait_ge(*QR_DVE.at(b - 3, "b2"))
                for s in range(ST):
                    pe.transpose(ps[:, 0, s * P:(s + 1) * P], x1[:, p, s], ident[:])
                for s in range(ST):
                    mm = pe.transpose(ps[:, 0, L + s * P:L + (s + 1) * P], n0[:, s], ident[:])
                mm.then_inc(*QA_PE.step("xT"))

            def keys(b, p, u):
                pe.wait_ge(*QA_DVE.at(b, "x0T"))
                pe.wait_ge(*QA_ACT.at(b - 1, "v3"))
                for x, name, bank in ((1, "k", 2), (0, "q", 1)):
                    for g in range(G1):
                        mm = pe.matmul(ps[:, bank, g * L:(g + 1) * L], qkw[:, x, g], x0T[:], start=True,
                                       stop=True)
                    mm.then_inc(*QA_PE.step(name))

            def values(b, p, u):
                for n in range(4):
                    s, half = n // 2, n % 2
                    pe.wait_ge(*QA_ACT.at(b, ("k1", "q1", "v0", "v1")[n]))
                    pe.matmul(ps[:, 2 - n % 2], x1T[:, p, s * P:(s + 1) * P],
                              vw[:, 4 * half:4 * half + 4].rearrange("p h d -> p (h d)"), start=True,
                              stop=True).then_inc(*QA_PE.step(f"v{n}"))

            def scores(b, p, u):
                pe.wait_ge(*QA_DVE.at(b, "q13"))
                pe.wait_ge(*QC_ACT.at(b - 2, "f3"))
                for n in range(6):
                    g, m = n // 3, n % 3
                    if n >= 4:
                        pe.wait_ge(*(QB_ACT.at(b, "s0") if n == 4 else QB_DVE.at(b, "s1")))
                    if m < 2:
                        rhs, key = q_bd1[:, p, g, 2 * m:2 * m + 2], k_T1[:, p, g, 0:P]
                    else:
                        rhs, key = q_bd1[:, p, g, :, P:L], k_T1[:, p, g, P:L]
                    pe.matmul(ps[:, 3 + n % 4].rearrange("p (h l) -> p h l", h=rhs.shape[1]), key, rhs,
                              start=True, stop=True).then_inc(*QB_PE.step(f"s{n}"))

            OUT_WAITS = ((QB_POOL, "mask0"), (QB_POOL, "mask3"), (QB_DVE, "s4"), (QB_DVE, "s5"),
                         (QB_DVE, "o02"), (QB_DVE, "o12"))

            def outputs(b, p, u):
                pe.wait_ge(*QA_ACT.at(b, "v3"))
                for n, (s, hs) in enumerate(OUTS):
                    steps_of, name = OUT_WAITS[n]
                    if n == 0:
                        pe.wait_ge(*QB_DVE.at(b, "s2"))
                    pe.wait_ge(*steps_of.at(b, name))
                    for i, hd in enumerate(hs):
                        dst = ps[:, 3 + (n + 2) % 4, (D + 1) * i:(D + 1) * (i + 1)]
                        mm = pe.matmul(dst, s_T0[:, hd, s * P:(s + 1) * P], v1[:, p, 0, hd, 0:D + 1],
                                       start=True, stop=(s == 0))
                        if s:
                            mm = pe.matmul(dst, s_T1[:, hd], v1[:, p, 1, hd, 0:D + 1], start=False, stop=True)
                    mm.then_inc(*QB_PE.step(f"o{n}"))

            def turn_outputs(parts):
                def part(b, p, u):
                    for n in parts:
                        if n == 0:
                            pe.wait_ge(*QB_DVE.at(b, "n1"))
                        for i in range(2):
                            for s in range(ST):
                                mm = pe.transpose(ps[:, 1 + n % 2, i * L + s * P:i * L + (s + 1) * P],
                                                  on[:, s, 2 * n + i], ident[:])
                        mm.then_inc(*QC_PE.step(f"y{n}"))
                return part

            def features(heads):
                def part(b, p, u):
                    pe.wait_ge(w1_split, 2)
                    pe.wait_ge(*QC_ACT.at(b, f"hi{heads[0] // 2}"))
                    for hd in heads:
                        for n in range(4):
                            for w in (w1_hi, w1_lo):
                                pe.matmul(ps[:, 3 + n, 0:L], w[:, hd, n * P:(n + 1) * P], y_hi[:, hd],
                                          start=(hd == 0 and w is not w1_lo), stop=False)
                    pe.wait_ge(*QC_POOL.at(b, f"lo{heads[0] // 2}"))
                    for hd in heads:
                        for n in range(4):
                            mm = pe.matmul(ps[:, 3 + n, 0:L], w1_hi[:, hd, n * P:(n + 1) * P], y_lo[:, hd],
                                           start=False, stop=(hd == H1 - 1))
                    if heads[-1] == H1 - 1:
                        mm.then_inc(*QC_PE.step("f"))
                return part

            def project(b, p, u):
                pe.wait_ge(*QR_DVE.at(b - 1, "b2"))
                pe.wait_ge(*QC_ACT.at(b, "f3"))
                for s in range(ST):
                    for f in range(F1 // P):
                        mm = pe.matmul(ps[:, 0, s * P:(s + 1) * P], h1T[:, f, s * P:(s + 1) * P], w2[:, f],
                                       start=(f == 0), stop=(f == F1 // P - 1))
                mm.then_inc(*QO_PE.step("out"))

            def rows_turn(b, p, u):
                route_turn(pe, QR_PE, QR_DVE, b, p)

            def logits(b, p, u):
                route_logits(pe, QR_PE, QR_DVE, b, wr2)

            def places(b, p, u):
                route_places(pe, QF_PE, QR_POOL, b, 7)

            skewed(pe, [(scores, 1), (places, 4), (outputs, 1), (turn_outputs((0, 1)), 2), (project, 3),
                        (features((0, 1)), 2), (turn_outputs((2,)), 2), (features((2, 3)), 2),
                        (turn_outputs((3,)), 2), (features((4, 5)), 2), (features((6,)), 2), (turn, 0),
                        (features((7,)), 2), (rows_turn, 3), (keys, 0), (logits, 3), (values, 0)], B)

        N_SENT2 = 16 * ST * K * B // 2
        N_TABLE = 16

        @block.gpsimd
        def _(pool):
            def send(t, p, u):
                pool.wait_ge(*FD_DVE.at(t, "dst"))
                held(pool, held_pool, t)
                for i in range(2):
                    pool.indirect_dma_start(
                        out=y2, out_offset=bass.IndirectOffsetOnAxis(ap=dst2_u[:, p, i, 0:1], axis=0),
                        in_=yo[:, p, i], in_offset=None, bounds_check=K * N - 1, oob_is_err=False,
                    ).then_inc(scattered_y2[p], 16)

            skewed(pool, [(send, 2)], NPAIR)

        @block.vector
        def _(dve):
            n = [1]

            def then(ins):
                n[0] += 1
                ins.then_inc(table, 1)
                dve.wait_ge(table, n[0])

            dve.wait_ge(*QF_DVE.at(B - 1, "gate"))
            dve.wait_ge(table, 1)
            then(dve.tensor_copy(t_no[:, :, 0], t_no_i[:]))
            then(dve.tensor_scalar(n_tiles[:, 0], counts[0:1, 1], float(P - 1), None, ALU.add))
            then(dve.tensor_copy(n_i[:], n_tiles[:, 0]))
            then(dve.tensor_scalar(n_i[:], n_i[:], 7, None, ALU.arith_shift_right))
            then(dve.tensor_copy(n_tiles[:, 0], n_i[:]))
            then(dve.memset(t_start[:], 0.0))
            then(dve.tensor_tensor_scan(ends[:, 0], n_tiles[:, 0], t_start[:, 0:E], 0.0, ALU.add, ALU.add))
            then(dve.tensor_tensor(t_past[:], t_no[:].broadcast_to([1, TILES2, E - 1]),
                                   ends[:, :, 0:E - 1].broadcast_to([1, TILES2, E - 1]), ALU.is_ge))
            then(dve.tensor_reduce(t_e[:], t_past[:], AX, ALU.add))
            then(dve.tensor_tensor(t_past[:], t_past[:], n_tiles[:, :, 0:E - 1].broadcast_to([1, TILES2, E - 1]),
                                   ALU.mult))
            then(dve.tensor_reduce(t_start[:], t_past[:], AX, ALU.add))
            then(dve.memset(tab_e[:], 0))
            pairs = t_e[:].rearrange("p (t i) -> p t i", i=2)
            then(dve.tensor_copy(tab_e[:, 2:2 + NPAIR], pairs))
            then(dve.scalar_tensor_tensor(t_row[:], t_e[:], float(REG // P), t_start[:], ALU.mult, ALU.subtract))
            then(dve.tensor_tensor(t_row[:], t_row[:], t_no[:, :, 0], ALU.add))
            then(dve.tensor_scalar(tab_row[:], t_row[:], float(P), None, ALU.mult))

            def hidden(i):
                def part(t, p, u):
                    dve.wait_ge(*FU_ACT.at(t, f"silu{i}"))
                    dve.tensor_tensor(gu[:, i], ps[:, 1 + i, HE:], silu[:, i], ALU.mult)\
                       .then_inc(*FU_DVE.step(f"gu{i}"))
                return part

            def turn(t, p, u):
                dve.wait_ge(*FT_PE.at(t, "xT"))
                dve.tensor_copy(xtT[:].rearrange("p i t -> p (i t)"), ps[:, 0, 0:2 * P])\
                   .then_inc(*FT_DVE.step("xT"))
                dve.tensor_copy(meta[:, bass.ds(t * 2, 2), :], xt[:, p, :, D:]).then_inc(*FT_DVE.step("meta"))

            def down(t, p, u):
                if not isinstance(u, int) or u > 0:
                    dve.wait_ge(scattered_y2[p], 32 * u)
                dve.wait_ge(*FT_DVE.at(t, "meta"))
                dve.wait_ge(*FD_PE.at(t, "out"))
                dve.tensor_tensor(yo[:, p], ps[:, 7, 0:2 * D].rearrange("p (i d) -> p i d", i=2),
                                  meta[:, bass.ds(t * 2, 2), 1:2].broadcast_to([P, 2, D]), ALU.mult)\
                   .then_inc(*FD_DVE.step("y"))
                dve.tensor_scalar(dst2_u[:, p], meta[:, bass.ds(t * 2, 2), 0:1], float(K * N), None,
                                  ALU.add).then_inc(*FD_DVE.step("dst"))

            skewed(dve, [(hidden(0), 1), (turn, 0), (hidden(1), 1), (down, 2)], NPAIR, peeled=2)

        @block.sync
        def _(sp):
            sp.wait_ge(table, N_TABLE + 1)
            for q in range(2):
                sp.wait_ge(scattered2[q], N_SENT2)

            def load(t, p, u):
                sp.wait_ge(*FT_DVE.at(t - 2, "meta"))
                for i in range(2):
                    row = sp.value_load(tab_row[0:1, bass.ds(t * 2 + i, 1)], min_val=0,
                                        max_val=E * REG + SPARE - P)
                    sp.dma_start(xt[:, p, i], xe2[bass.ds(row, P), :]).then_inc(ld_xt[p], 16)

            skewed(sp, [(load, 0)], NPAIR)

        @block.scalar
        def _(act):
            act.activation(first_use[:], one[:], ACT.Silu)

            def hidden(t, p, u):
                for i in range(2):
                    act.wait_ge(*FU_PE.at(t, f"gu{i}"))
                    act.activation(silu[:, i], ps[:, 1 + i, 0:HE], ACT.Silu).then_inc(*FU_ACT.step(f"silu{i}"))

            def turn(t, p, u):
                for i in range(2):
                    act.wait_ge(*FH_PE.at(t, f"guT{i}"))
                    act.activation(guT[:, i].rearrange("p c t -> p (c t)"), ps[:, 5 + i, 0:HE], ACT.Identity)\
                       .then_inc(*FH_ACT.step(f"guT{i}"))

            skewed(act, [(hidden, 1), (turn, 1)], NPAIR)

        @block.tensor
        def _(pe):
            pe.wait_ge(table, N_TABLE + 1)
            pe.wait_ge(ld_wf, N_WF)
            pe.wait_ge(*QF_DVE.at(B - 1, "gate"))
            experts, looks = {}, [0]

            def look(t, p, u):
                if p == 0 and not (isinstance(t, int) and t == 0):
                    return
                first = 0 if p == 0 else t + 1
                looks[0] += 1
                regs = [pe.alloc_register(f"expert{looks[0]}_{i}") for i in range(6)]
                pe.load(regs, tab_e[0:1, bass.ds(first, 3), :].rearrange("p t i -> p (t i)"))
                found = [pe.snap(reg, min_val=0, max_val=E - 1) for reg in regs]
                experts["up"] = (found[4:6], found[2:4])
                experts["down"] = (found[0:2], found[2:4])

            def up(t, p, u):
                pe.wait_ge(*FT_DVE.at(t, "xT"))
                for i in range(2):
                    pe.matmul(ps[:, 1 + i], xtT[:, i],
                              wgu[:, bass.ds(experts["up"][p][i], 1)].rearrange("p e f -> p (e f)"),
                              start=True, stop=True).then_inc(*FU_PE.step(f"gu{i}"))

            def turn(t, p, u):
                pe.wait_ge(ld_xt[p], 32 * (u + 1))
                for i in range(2):
                    mm = pe.transpose(ps[:, 0, i * P:(i + 1) * P], xt[:, p, i, 0:D], ident[:])
                mm.then_inc(*FT_PE.step("xT"))

            def down(t, p, u):
                pe.wait_ge(*FH_ACT.at(t, "guT1"))
                pe.wait_ge(*FD_DVE.at(t - 1, "y"))
                for i in range(2):
                    for c in range(HT):
                        mm = pe.matmul(ps[:, 7, i * D:(i + 1) * D], guT[:, i, c],
                                       wd[:, bass.ds(experts["down"][p][i], 1), c].rearrange("p e d -> p (e d)"),
                                       start=(c == 0), stop=(c == HT - 1))
                mm.then_inc(*FD_PE.step("out"))

            def turn_hidden(t, p, u):
                for i in range(2):
                    pe.wait_ge(*FU_DVE.at(t, f"gu{i}"))
                    for c in range(HT):
                        mm = pe.transpose(ps[:, 5 + i, c * P:(c + 1) * P], gu[:, i, c * P:(c + 1) * P], ident[:])
                    mm.then_inc(*FH_PE.step(f"guT{i}"))

            skewed(pe, [(look, 1), (up, 1), (turn, 0), (down, 2), (turn_hidden, 1)], NPAIR, unroll=2)

        @block.sync
        def _(sp):
            for q in range(2):
                sp.wait_ge(scattered_y2[q], 16 * TILES2 // 2)
            for c in range(NT // CH):
                for k in range(K):
                    sp.dma_start(y_in[:, c, k], y2.rearrange("(k c t p) d -> k c p t d", k=K, t=CH, p=P)[k, c])\
                      .then_inc(ld_y2[c], 16)
            for c in range(NT // CH):
                sp.wait_ge(summed, 2 * (c + 1))
                sp.dma_start(out.rearrange("(c t p) d -> c p t d", t=CH, p=P)[c], h[:, c * CH:(c + 1) * CH])\
                  .then_inc(stored, 16)
            sp.wait_ge(stored, 16 * (NT // CH))

        @block.vector
        def _(dve):
            for c in range(NT // CH):
                dve.wait_ge(ld_y2[c], 32)
                for k in range(K):
                    rows = h[:, c * CH:(c + 1) * CH]
                    dve.tensor_tensor(rows, y_in[:, c, k], rows, ALU.add).then_inc(summed, 1)
                    dve.wait_ge(summed, 2 * c + k + 1)

def kernel(**inputs):
    import concourse.bacc as bacc
    from concourse.bass_utils import run_bass_kernel_spmd

    arrays = layouts({k: np.asarray(v) for k, v in inputs.items()})
    nc = bacc.Bacc("TRN2", target_bir_lowering=False, num_devices=1)
    aps = {n: nc.dram_tensor(f"in_{n}", v.shape, mybir.dt.from_np(v.dtype), kind="ExternalInput").ap()
           for n, v in arrays.items()}
    out = nc.dram_tensor("out", [N, D], F32, kind="ExternalOutput").ap()
    lm_tower(nc, aps, out)
    r = run_bass_kernel_spmd(nc, [{f"in_{n}": v for n, v in arrays.items()}], core_ids=[0])
    return r.results[0]["out"].reshape(B, L, D)
```
